# Optimizing a Trainium2 kernel written in Bass

```python
import numpy as np
import jax
import jax.numpy as jnp

def _softmax(x, axis=-1):
    return jax.nn.softmax(x, axis=axis)

def _gelu(x):
    return jax.nn.gelu(x, approximate=True)

def _silu(x):
    return jax.nn.silu(x)

def _sigmoid(x):
    return jax.nn.sigmoid(x)

def _layernorm(x, axis=-1, eps=1e-05):
    m = jnp.mean(x, axis=axis, keepdims=True)
    v = jnp.var(x, axis=axis, keepdims=True)
    return (x - m) / jnp.sqrt(v + eps)

def _scatter_add(tgt, idx, src, axis=0):
    return tgt.at[idx].add(src)

def _segment_sum(src, seg, n):
    return jax.ops.segment_sum(src, seg, n)
kernel_name = 'mk_adaln_d2_jaxref_r4_126649'

def setup_inputs(seed: int=0):
    np.random.seed(seed)
    _w = jnp.asarray

    def _L0_attn_setup():
        import jax, jax.numpy as jnp
        import numpy as np
        D_MODEL, D_STATE, EXPAND = (256, 16, 2)
        D_INNER = D_MODEL * EXPAND
        LN_EPS = 1e-05
        key = jax.random.key(seed)
        ks = jax.random.split(key, 10)
        B, T = (2, 1024)
        s_in = 1.0 / np.sqrt(D_MODEL)
        s_inner = 1.0 / np.sqrt(D_INNER)
        return {'x': jax.random.normal(ks[0], (B, T, D_MODEL), jnp.float32), 'norm_w': jnp.ones((D_MODEL,), jnp.float32), 'norm_b': jnp.zeros((D_MODEL,), jnp.float32), 'W_in': jax.random.normal(ks[1], (D_MODEL, D_INNER), jnp.float32) * s_in, 'W_gate': jax.random.normal(ks[2], (D_MODEL, D_INNER), jnp.float32) * s_in, 'W_dt': jax.random.normal(ks[3], (D_INNER, D_INNER), jnp.float32) * s_inner, 'b_dt': jax.random.normal(ks[4], (D_INNER,), jnp.float32) * 0.01, 'W_B': jax.random.normal(ks[5], (D_INNER, D_STATE), jnp.float32) * s_inner, 'W_C': jax.random.normal(ks[6], (D_INNER, D_STATE), jnp.float32) * s_inner, 'A_log': -jax.random.uniform(ks[7], (D_INNER, D_STATE), jnp.float32) * 0.5, 'W_out': jax.random.normal(ks[8], (D_INNER, D_MODEL), jnp.float32) * s_inner}
    _L0_attn_in = _L0_attn_setup()

    def _L0_ffn_setup():
        import jax, jax.numpy as jnp
        import numpy as np
        E = 8
        key = jax.random.key(seed)
        k0, k1, k2, k3 = jax.random.split(key, 4)
        B, S, H, F = (4, 1024, 256, 1024)
        x = jax.random.normal(k0, (B, S, H), jnp.float32)
        Wr = jax.random.normal(k1, (E, H), jnp.float32) * 0.02
        W1 = jax.random.normal(k2, (E, H, F), jnp.float32) * 0.02
        b1 = jnp.zeros((E, F), jnp.float32)
        W2 = jax.random.normal(k3, (E, F, H), jnp.float32) * 0.02
        b2 = jnp.zeros((E, H), jnp.float32)
        return {'x': x, 'Wr': Wr, 'W1': W1, 'b1': b1, 'W2': W2, 'b2': b2}
    _L0_ffn_in = _L0_ffn_setup()
    _L0_c = _w((lambda *s: np.random.randn(*s).astype(np.float32) * 0.05)(4, 256))
    _L0_wmod = _w((lambda *s: np.random.randn(*s).astype(np.float32) * 0.05)(256, 6 * 256) * 256 ** (-0.5))

    def _L1_attn_setup():
        import jax, jax.numpy as jnp
        import numpy as np
        B, S, HID, NH = (4, 1024, 256, 16)
        D = HID // NH
        EPS = 1e-05

        def _delta_scan(q, k, v, beta):
            vsum = v.sum(-1)
            qs = jnp.moveaxis(q, 1, 0)
            ks_ = jnp.moveaxis(k, 1, 0)
            vs = jnp.moveaxis(vsum, 1, 0)
            bs = jnp.moveaxis(beta, 1, 0)

            def step(h, inp):
                q_t, k_t, vsum_t, beta_t = inp
                h = h * beta_t[..., None, None]
                h = h + (k_t * vsum_t[..., None])[:, :, None, :]
                o_t = jnp.einsum('bhj,bhjk->bhk', q_t, h)
                return (h, o_t)
            h0 = jnp.zeros((q.shape[0], q.shape[2], D, D), dtype=q.dtype)
            _, o = jax.lax.scan(step, h0, (qs, ks_, vs, bs))
            return jnp.moveaxis(o, 0, 1)
        key = jax.random.key(seed)
        ks = jax.random.split(key, 8)
        x = jax.random.normal(ks[0], (B, S, HID), dtype=jnp.float32)
        sc = 0.03
        Wq = jax.random.normal(ks[1], (HID, HID), dtype=jnp.float32) * sc
        Wk = jax.random.normal(ks[2], (HID, HID), dtype=jnp.float32) * sc
        Wv = jax.random.normal(ks[3], (HID, HID), dtype=jnp.float32) * sc
        Wbeta = jax.random.normal(ks[4], (HID, NH), dtype=jnp.float32) * sc
        b_beta = jnp.full((NH,), 0.9, dtype=jnp.float32)
        Wo = jax.random.normal(ks[5], (HID, HID), dtype=jnp.float32) * sc
        b_o = jnp.zeros((HID,), dtype=jnp.float32)
        ln_g = jnp.ones((HID,), dtype=jnp.float32)
        ln_b = jnp.zeros((HID,), dtype=jnp.float32)
        return {'x': x, 'Wq': Wq, 'Wk': Wk, 'Wv': Wv, 'Wbeta': Wbeta, 'b_beta': b_beta, 'Wo': Wo, 'b_o': b_o, 'ln_g': ln_g, 'ln_b': ln_b}
    _L1_attn_in = _L1_attn_setup()

    def _L1_ffn_setup():
        import jax, jax.numpy as jnp
        import numpy as np

        def _ln(x, w, b):
            m = jnp.mean(x, axis=-1, keepdims=True)
            v = jnp.var(x, axis=-1, keepdims=True)
            return (x - m) / jnp.sqrt(v + 1e-05) * w + b
        B, T, C = (4, 512, 256)
        E_RWKV, E = (2, 3)
        H = 4 * C
        S = 0.02
        key = jax.random.key(seed)
        ks = jax.random.split(key, 20)
        d = {}
        d['x'] = jax.random.normal(ks[0], (B, T, C), jnp.float32)
        d['v_first'] = jax.random.normal(ks[1], (B, T, C), jnp.float32)
        d['capital_shares'] = jax.random.uniform(ks[2], (E,), jnp.float32)
        d['ln1_w'] = jnp.ones((C,), jnp.float32)
        d['ln1_b'] = jnp.zeros((C,), jnp.float32)
        d['ln2_w'] = jnp.ones((C,), jnp.float32)
        d['ln2_b'] = jnp.zeros((C,), jnp.float32)
        d['Wr'] = S * jax.random.normal(ks[3], (C, C), jnp.float32)
        d['Wv'] = S * jax.random.normal(ks[4], (C, C), jnp.float32)
        d['Wo'] = S * jax.random.normal(ks[5], (C, C), jnp.float32)
        d['Ws'] = S * jax.random.normal(ks[6], (C, C), jnp.float32)
        d['K_rwkv'] = S * jax.random.normal(ks[7], (E_RWKV, C, H), jnp.float32)
        d['V_rwkv'] = S * jax.random.normal(ks[8], (E_RWKV, H, C), jnp.float32)
        d['conf_rwkv'] = S * jax.random.normal(ks[9], (E_RWKV, C), jnp.float32)
        d['W1'] = S * jax.random.normal(ks[10], (C, C), jnp.float32)
        d['W2'] = S * jax.random.normal(ks[11], (C, C), jnp.float32)
        d['W3'] = S * jax.random.normal(ks[12], (C, C), jnp.float32)
        d['conf_trans'] = S * jax.random.normal(ks[13], (C,), jnp.float32)
        d['w_diff'] = S * jax.random.normal(ks[14], (C,), jnp.float32)
        d['W_aff'] = S * jax.random.normal(ks[15], (C, E), jnp.float32)
        d['W_bridge'] = S * jax.random.normal(ks[16], (C, C), jnp.float32)
        return d
    _L1_ffn_in = _L1_ffn_setup()
    _L1_c = _w((lambda *s: np.random.randn(*s).astype(np.float32) * 0.05)(4, 256))
    _L1_wmod = _w((lambda *s: np.random.randn(*s).astype(np.float32) * 0.05)(256, 6 * 256) * 256 ** (-0.5))
    _d = {'L0_attn_x': _L0_attn_in['x'], 'L0_attn_norm_w': _L0_attn_in['norm_w'], 'L0_attn_norm_b': _L0_attn_in['norm_b'], 'L0_attn_W_in': _L0_attn_in['W_in'], 'L0_attn_W_gate': _L0_attn_in['W_gate'], 'L0_attn_W_dt': _L0_attn_in['W_dt'], 'L0_attn_b_dt': _L0_attn_in['b_dt'], 'L0_attn_W_B': _L0_attn_in['W_B'], 'L0_attn_W_C': _L0_attn_in['W_C'], 'L0_attn_A_log': _L0_attn_in['A_log'], 'L0_attn_W_out': _L0_attn_in['W_out'], 'L0_ffn_Wr': _L0_ffn_in['Wr'], 'L0_ffn_W1': _L0_ffn_in['W1'], 'L0_ffn_b1': _L0_ffn_in['b1'], 'L0_ffn_W2': _L0_ffn_in['W2'], 'L0_ffn_b2': _L0_ffn_in['b2'], 'L0_c': _L0_c, 'L0_wmod': _L0_wmod, 'L1_attn_Wq': _L1_attn_in['Wq'], 'L1_attn_Wk': _L1_attn_in['Wk'], 'L1_attn_Wv': _L1_attn_in['Wv'], 'L1_attn_Wbeta': _L1_attn_in['Wbeta'], 'L1_attn_b_beta': _L1_attn_in['b_beta'], 'L1_attn_Wo': _L1_attn_in['Wo'], 'L1_attn_b_o': _L1_attn_in['b_o'], 'L1_attn_ln_g': _L1_attn_in['ln_g'], 'L1_attn_ln_b': _L1_attn_in['ln_b'], 'L1_ffn_v_first': _L1_ffn_in['v_first'], 'L1_ffn_capital_shares': _L1_ffn_in['capital_shares'], 'L1_ffn_ln1_w': _L1_ffn_in['ln1_w'], 'L1_ffn_ln1_b': _L1_ffn_in['ln1_b'], 'L1_ffn_ln2_w': _L1_ffn_in['ln2_w'], 'L1_ffn_ln2_b': _L1_ffn_in['ln2_b'], 'L1_ffn_Wr': _L1_ffn_in['Wr'], 'L1_ffn_Wv': _L1_ffn_in['Wv'], 'L1_ffn_Wo': _L1_ffn_in['Wo'], 'L1_ffn_Ws': _L1_ffn_in['Ws'], 'L1_ffn_K_rwkv': _L1_ffn_in['K_rwkv'], 'L1_ffn_V_rwkv': _L1_ffn_in['V_rwkv'], 'L1_ffn_conf_rwkv': _L1_ffn_in['conf_rwkv'], 'L1_ffn_W1': _L1_ffn_in['W1'], 'L1_ffn_W2': _L1_ffn_in['W2'], 'L1_ffn_W3': _L1_ffn_in['W3'], 'L1_ffn_conf_trans': _L1_ffn_in['conf_trans'], 'L1_ffn_w_diff': _L1_ffn_in['w_diff'], 'L1_ffn_W_aff': _L1_ffn_in['W_aff'], 'L1_ffn_W_bridge': _L1_ffn_in['W_bridge'], 'L1_c': _L1_c, 'L1_wmod': _L1_wmod}
    _x0 = _d['L0_attn_x']
    _d['L0_attn_x'] = jax.random.normal(jax.random.fold_in(jax.random.key(seed), 1), (4, 2048, 256), dtype=_x0.dtype)
    del _x0
    return _d

def reference(L0_attn_x, L0_attn_norm_w, L0_attn_norm_b, L0_attn_W_in, L0_attn_W_gate, L0_attn_W_dt, L0_attn_b_dt, L0_attn_W_B, L0_attn_W_C, L0_attn_A_log, L0_attn_W_out, L0_ffn_Wr, L0_ffn_W1, L0_ffn_b1, L0_ffn_W2, L0_ffn_b2, L0_c, L0_wmod, L1_attn_Wq, L1_attn_Wk, L1_attn_Wv, L1_attn_Wbeta, L1_attn_b_beta, L1_attn_Wo, L1_attn_b_o, L1_attn_ln_g, L1_attn_ln_b, L1_ffn_v_first, L1_ffn_capital_shares, L1_ffn_ln1_w, L1_ffn_ln1_b, L1_ffn_ln2_w, L1_ffn_ln2_b, L1_ffn_Wr, L1_ffn_Wv, L1_ffn_Wo, L1_ffn_Ws, L1_ffn_K_rwkv, L1_ffn_V_rwkv, L1_ffn_conf_rwkv, L1_ffn_W1, L1_ffn_W2, L1_ffn_W3, L1_ffn_conf_trans, L1_ffn_w_diff, L1_ffn_W_aff, L1_ffn_W_bridge, L1_c, L1_wmod):

    def _L0_attn_ref(x, norm_w, norm_b, W_in, W_gate, W_dt, b_dt, W_B, W_C, A_log, W_out):
        import jax, jax.numpy as jnp
        import numpy as np
        D_MODEL, D_STATE, EXPAND = (256, 16, 2)
        D_INNER = D_MODEL * EXPAND
        LN_EPS = 1e-05
        residual = x
        mu = jnp.mean(x, axis=-1, keepdims=True)
        var = jnp.mean((x - mu) ** 2, axis=-1, keepdims=True)
        xn = (x - mu) / jnp.sqrt(var + LN_EPS) * norm_w + norm_b
        z = xn @ W_in
        gate = jax.nn.silu(xn @ W_gate)
        dt = jnp.clip(jax.nn.softplus(z @ W_dt + b_dt), 0.001, 1.0)
        Bp = z @ W_B
        Cp = z @ W_C
        A = -jnp.clip(jnp.exp(A_log), 1e-06, 1.0)
        Bsz, T, d_inner = z.shape
        d_state = Bp.shape[-1]

        def step(h, inp):
            dt_t, B_t, C_t, z_t = inp
            dA = jnp.exp(jnp.clip(dt_t[:, :, None] * A, -20.0, 0.0))
            dB = dt_t[:, :, None] * B_t[:, None, :]
            h = dA * h + dB * z_t[:, :, None]
            y_t = jnp.einsum('bds,bs->bd', h, C_t)
            return (h, y_t)
        h0 = jnp.zeros((Bsz, d_inner, d_state), jnp.float32)
        seq = (jnp.swapaxes(dt, 0, 1), jnp.swapaxes(Bp, 0, 1), jnp.swapaxes(Cp, 0, 1), jnp.swapaxes(z, 0, 1))
        _, ys = jax.lax.scan(step, h0, seq)
        y = jnp.swapaxes(ys, 0, 1) * gate
        return residual + y @ W_out

    def _L0_ffn_ref(x, Wr, W1, b1, W2, b2):
        import jax, jax.numpy as jnp
        import numpy as np
        E = 8
        B, S, H = x.shape
        xf = x.reshape(-1, H)
        probs = jax.nn.softmax(xf @ Wr.T, axis=-1)
        eid = E - 1
        h = jax.nn.gelu(xf @ W1[eid] + b1[eid], approximate=False)
        y = (h @ W2[eid] + b2[eid]) * probs[:, eid:eid + 1]
        return y.reshape(B, S, H)

    def _L1_attn_ref(x, Wq, Wk, Wv, Wbeta, b_beta, Wo, b_o, ln_g, ln_b):
        import jax, jax.numpy as jnp
        import numpy as np
        B, S, HID, NH = (4, 1024, 256, 16)
        D = HID // NH
        EPS = 1e-05

        def _delta_scan(q, k, v, beta):
            vsum = v.sum(-1)
            qs = jnp.moveaxis(q, 1, 0)
            ks_ = jnp.moveaxis(k, 1, 0)
            vs = jnp.moveaxis(vsum, 1, 0)
            bs = jnp.moveaxis(beta, 1, 0)

            def step(h, inp):
                q_t, k_t, vsum_t, beta_t = inp
                h = h * beta_t[..., None, None]
                h = h + (k_t * vsum_t[..., None])[:, :, None, :]
                o_t = jnp.einsum('bhj,bhjk->bhk', q_t, h)
                return (h, o_t)
            h0 = jnp.zeros((q.shape[0], q.shape[2], D, D), dtype=q.dtype)
            _, o = jax.lax.scan(step, h0, (qs, ks_, vs, bs))
            return jnp.moveaxis(o, 0, 1)
        b, s, hid = x.shape
        residual = x
        q = (x @ Wq).reshape(b, s, NH, D)
        k = (x @ Wk).reshape(b, s, NH, D)
        v = (x @ Wv).reshape(b, s, NH, D)
        beta = jax.nn.sigmoid(x @ Wbeta + b_beta)
        o = _delta_scan(q, k, v, beta).reshape(b, s, hid)
        out = o @ Wo + b_o
        y = residual + out
        mu = y.mean(-1, keepdims=True)
        var = ((y - mu) ** 2).mean(-1, keepdims=True)
        return ln_g * (y - mu) * jax.lax.rsqrt(var + EPS) + ln_b

    def _L1_ffn_ref(x, v_first, capital_shares, ln1_w, ln1_b, ln2_w, ln2_b, Wr, Wv, Wo, Ws, K_rwkv, V_rwkv, conf_rwkv, W1, W2, W3, conf_trans, w_diff, W_aff, W_bridge):
        import jax, jax.numpy as jnp
        import numpy as np

        def _ln(x, w, b):
            m = jnp.mean(x, axis=-1, keepdims=True)
            v = jnp.var(x, axis=-1, keepdims=True)
            return (x - m) / jnp.sqrt(v + 1e-05) * w + b
        B, T, C = x.shape
        xln = _ln(x, ln1_w, ln1_b)
        att_out = jax.nn.sigmoid(xln @ Wr) * (xln @ Wv) @ Wo
        rwkv_state = xln @ Ws
        x = x + att_out
        h = _ln(x, ln2_w, ln2_b)
        conf_r = jax.nn.sigmoid(jnp.einsum('btc,ec->bte', h, conf_rwkv))
        conf_t = jax.nn.sigmoid(h @ conf_trans)[..., None]
        confidences = jnp.concatenate([conf_r, conf_t], axis=-1)
        E = confidences.shape[-1]
        difficulty = jax.nn.sigmoid(h @ w_diff)[..., None]
        affinity = h @ W_aff
        bids = confidences * capital_shares * difficulty + affinity
        winners = jnp.argmax(bids, axis=-1)
        flat_h = h.reshape(-1, C)
        flat_state = rwkv_state.reshape(-1, C)
        flat_w = winners.reshape(-1)
        flat_conf = confidences.reshape(-1, E)
        win_conf = jnp.take_along_axis(flat_conf, flat_w[:, None], axis=1)
        scale = win_conf / (jax.lax.stop_gradient(win_conf) + 1e-06)
        hr = jnp.square(jax.nn.relu(jnp.einsum('nc,ech->enh', flat_h, K_rwkv)))
        out_rwkv = jnp.einsum('enh,ehc->enc', hr, V_rwkv)
        out_trans = flat_h @ W1 * jax.nn.sigmoid(flat_state @ W2) @ W3
        all_out = jnp.concatenate([out_rwkv, out_trans[None]], axis=0)
        onehot = jax.nn.one_hot(flat_w, E, dtype=flat_h.dtype)
        final = jnp.einsum('ne,enc->nc', onehot, all_out) * scale
        return x + final.reshape(B, T, C)
    x = L0_attn_x
    mod = (_silu(L0_c) @ L0_wmod).reshape(L0_c.shape[0], 6, 1, -1)
    sa, ca, ga, sb, cb, gb = (mod[:, 0], mod[:, 1], mod[:, 2], mod[:, 3], mod[:, 4], mod[:, 5])
    ga = (2 * (ga >= 0) - 1) * jnp.maximum(jnp.abs(ga), 0.25)
    gb = (2 * (gb >= 0) - 1) * jnp.maximum(jnp.abs(gb), 0.25)
    h = _layernorm(x, axis=-1) * (1 + ca) + sa
    x = x + ga * _L0_attn_ref(h, L0_attn_norm_w, L0_attn_norm_b, L0_attn_W_in, L0_attn_W_gate, L0_attn_W_dt, L0_attn_b_dt, L0_attn_W_B, L0_attn_W_C, L0_attn_A_log, L0_attn_W_out)
    h = _layernorm(x, axis=-1) * (1 + cb) + sb
    x = x + gb * _L0_ffn_ref(h, L0_ffn_Wr, L0_ffn_W1, L0_ffn_b1, L0_ffn_W2, L0_ffn_b2)
    mod = (_silu(L1_c) @ L1_wmod).reshape(L1_c.shape[0], 6, 1, -1)
    sa, ca, ga, sb, cb, gb = (mod[:, 0], mod[:, 1], mod[:, 2], mod[:, 3], mod[:, 4], mod[:, 5])
    ga = (2 * (ga >= 0) - 1) * jnp.maximum(jnp.abs(ga), 0.25)
    gb = (2 * (gb >= 0) - 1) * jnp.maximum(jnp.abs(gb), 0.25)
    h = _layernorm(x, axis=-1) * (1 + ca) + sa
    x = x + ga * _L1_attn_ref(h, L1_attn_Wq, L1_attn_Wk, L1_attn_Wv, L1_attn_Wbeta, L1_attn_b_beta, L1_attn_Wo, L1_attn_b_o, L1_attn_ln_g, L1_attn_ln_b)
    h = _layernorm(x, axis=-1) * (1 + cb) + sb
    x = x + gb * _L1_ffn_ref(h, L1_ffn_v_first, L1_ffn_capital_shares, L1_ffn_ln1_w, L1_ffn_ln1_b, L1_ffn_ln2_w, L1_ffn_ln2_b, L1_ffn_Wr, L1_ffn_Wv, L1_ffn_Wo, L1_ffn_Ws, L1_ffn_K_rwkv, L1_ffn_V_rwkv, L1_ffn_conf_rwkv, L1_ffn_W1, L1_ffn_W2, L1_ffn_W3, L1_ffn_conf_trans, L1_ffn_w_diff, L1_ffn_W_aff, L1_ffn_W_bridge)
    return x

_drawn_inputs = setup_inputs


def setup_inputs(seed=0):
    import zlib

    import numpy as np

    out = dict(_drawn_inputs(seed))
    spreads = {'L0_attn_norm_w': (1.0, 0.2),
     'L0_attn_norm_b': (0.0, 0.1),
     'L0_ffn_b1': (0.0, 0.8),
     'L0_ffn_b2': (0.0, 0.8),
     'L1_attn_b_beta': (0.8999999761581421, 0.6),
     'L1_attn_b_o': (0.0, 0.563),
     'L1_attn_ln_g': (1.0, 0.2),
     'L1_attn_ln_b': (0.0, 0.399),
     'L1_ffn_ln1_w': (1.0, 0.6),
     'L1_ffn_ln1_b': (0.0, 0.8),
     'L1_ffn_ln2_w': (1.0, 0.6),
     'L1_ffn_ln2_b': (0.0, 0.8)}
    factors = {'L0_attn_b_dt': 8.0,
     'L0_ffn_Wr': 8.0,
     'L0_ffn_W1': 8.0,
     'L0_ffn_W2': 8.0,
     'L1_ffn_capital_shares': 7.802,
     'L1_ffn_Wr': 8.0,
     'L1_ffn_Wv': 5.056,
     'L1_ffn_Wo': 5.099,
     'L1_ffn_Ws': 8.0,
     'L1_ffn_K_rwkv': 4.227,
     'L1_ffn_V_rwkv': 3.886,
     'L1_ffn_conf_rwkv': 8.0,
     'L1_ffn_W1': 8.0,
     'L1_ffn_W2': 8.0,
     'L1_ffn_W3': 8.0,
     'L1_ffn_conf_trans': 8.0,
     'L1_ffn_w_diff': 8.0,
     'L1_ffn_W_aff': 4.554}
    for name, (base, spread) in spreads.items():
        noise = np.random.default_rng([zlib.crc32(name.encode()), seed]).standard_normal(out[name].shape)
        drawn = base * np.exp(spread * noise) if base else spread * noise
        out[name] = jnp.asarray(drawn.astype(out[name].dtype))
    for name, factor in factors.items():
        out[name] = (out[name] * factor).astype(out[name].dtype)
    return out
```

```python
from contextlib import ExitStack

import concourse.bass as bass
from concourse import mybir

F32 = mybir.dt.float32
F32R = mybir.dt.float32r
I32 = mybir.dt.int32
ALU = mybir.AluOpType
ACT = mybir.ActivationFunctionType
AX = mybir.AxisListType.X

P = 128
B, T, C = 4, 2048, 256
CT = 512
NT = CT // P
NCH = B * T // CT
CPB = T // CT
KC = C // P
DI, DS = 512, 16
DB = DI // P
F = 1024
NH, HD = 16, 16
E_MOE = 8
EPS = 1e-5
DT_MIN, DT_MAX = 0.001, 1.0
DT_CLAMP = 20.0
GATE_MIN = 0.25
NQ = C + 3 * NH

ROWS = ["cA0", "sA0", "gA0", "cB0", "sB0", "gB0", "cA1", "sA1", "gA1w", "gA1b", "cB1", "sB1", "gB1"]
ROW = {name: k for k, name in enumerate(ROWS)}
NROW_S = 3
NROW_D = len(ROWS) - NROW_S

SLOTS = ["ffn_0", "ffn_1", "rv", "sw", "e0_0", "e0_1", "e1_0", "e1_1"]
NSLOT = len(SLOTS)
CREDIT = 1
HB = F // 2 // P
NHB = F // P

SSM_UNITS = DS * DB + DB

PACE = {name: k for name, k in [
    ("a_stats", 1), ("a_norm", 3), ("b_turn", 5), ("b_router", 6),
    ("c0", 7), ("c1", 8), ("c2", 9), ("c3", 10), ("c4", 11), ("c5", 12), ("c6", 13), ("c7", 14),
    ("d_x2", 15), ("e_stats", 16), ("e_norm", 18), ("f_turn", 19), ("f_kv", 20), ("g_turn", 21),
    ("g_scan", 22), ("h_out", 23), ("h_stats", 24), ("h_norm", 26), ("i_stats", 27), ("i_norm", 29),
    ("i_stats2", 30), ("i_norm2", 31), ("j_turn", 32), ("k_proj", 34), ("l_out", 36),
    ("m_stats", 37), ("m_norm", 38), ("m_turn", 40), ("n_bids", 42), ("n_trans", 44),
    ("o0", 45), ("o1", 46), ("o2", 47), ("o3", 48), ("o4", 49), ("o5", 50), ("o6", 51), ("o7", 52),
    ("o_out", 53),
    ("p0", 54), ("p1", 56), ("p2", 57), ("p3", 59), ("p4", 60), ("p5", 62), ("p6", 64), ("p7", 66),
    ("q_out", 68),
]}

FRONT = ["xn0", "xn1", "z0", "z1", "z2", "z3", "gt0", "gt1", "gt2", "gt3", "bc", "ct", "dt0", "dt1", "dt2", "dt3"]
TAIL = ["y0", "y1", "y2", "y3", "wo0", "wo1"]
SCAN_BANKS = ["A0", "A1", "H0", "H1"]
BANK_USES = {
    "A0": FRONT[0::4] + [f"dA{u}" for u in range(0, DS * DB, 2)] + TAIL[0::4],
    "A1": FRONT[1::4] + [f"dA{u}" for u in range(1, DS * DB, 2)] + TAIL[1::4],
    "H0": FRONT[2::4] + [f"hT{u}" for u in range(0, DS * NT, 2)] + TAIL[2::4],
    "H1": FRONT[3::4] + [f"hT{u}" for u in range(1, DS * NT, 2)] + TAIL[3::4],
    "B0": ["h1T0"] + [f"c{k}" for k in (0, 2, 4, 6)] + ["h2T0", "kvT0", "qsT0", "xlT0", "r0", "s0", "sW0", "hhT0", "tw0"]
          + [f"o{k}" for k in (0, 2, 4, 6)] + [f"p{k}" for k in (0, 2, 4, 6)],
    "B1": ["h1T1"] + [f"c{k}" for k in (1, 3, 5, 7)] + ["h2T1", "kvT1", "qsT1", "xlT1", "r1", "s1", "sW1", "hhT1", "tw1"]
          + [f"o{k}" for k in (1, 3, 5, 7)] + [f"p{k}" for k in (1, 3, 5, 7)],
    "B2": ["router", "ffn0", "kq0", "kq2", "btT0", "ao0", "v0", "att0", "bids", "tr0", "e0_0", "e1_0"],
    "B3": ["routerT", "ffn1", "kq1", "kq3", "btT1", "ao1", "v1", "att1", "bidsT", "tr1", "e0_1", "e1_1"],
}


class Bank:

    def __init__(self, tensor, full, free, uses):
        self.t, self.full, self.free, self.uses = tensor, full, free, uses

    def fills_before(self, chunk, use):
        return chunk * len(self.uses) + self.uses.index(use) + CREDIT

    def fills_with(self, chunk, use):
        return self.fills_before(chunk, use) + 1


class Signal:

    def __init__(self, sem, n, credit=0):
        self.sem, self.n, self.credit = sem, n, credit

    def at(self, chunk, k):
        return chunk * self.n + k + self.credit


class Own:

    def __init__(self, eng, sig, chunk):
        self.eng, self.sig, self.chunk, self.k = eng, sig, chunk, 0

    def mark(self, instruction):
        self.k += 1
        instruction.then_inc(self.sig.sem, 1)
        return self.k

    def wait(self, k=None):
        self.eng.wait_ge(self.sig.sem, self.sig.at(self.chunk, self.k if k is None else k))

    def step(self, instruction):
        self.mark(instruction)
        self.wait()

    def end(self):
        assert self.k == self.sig.n, f"{self.k} own steps, {self.sig.n} stated"


class Pace:

    def __init__(self, unit, chunk):
        self.unit, self.chunk, self.at = unit, chunk, 0

    def __call__(self, name):
        self.upto(PACE[name])

    def upto(self, n):
        while self.unit is not None and self.at < n:
            self.unit(self.chunk, self.at)
            self.at += 1


def since(eng, sig, chunk, k=0):
    if not (isinstance(chunk, int) and chunk == 0 and k == 0):
        eng.wait_ge(sig.sem, sig.at(chunk, k))


def build(nc, w, out):
    ctx = ExitStack()
    with ctx:
        ctx.enter_context(nc.allow_non_contiguous_dma("small constants, column by column"))
        place = [(nc.sbuf_base + 63) // 64 * 64]

        def sb(name, shape, dt=F32):
            size = 4
            for n in shape[1:]:
                size *= n
            t = nc.alloc_sbuf_tensor_at(name, list(shape), dt, offset=place[0])
            where[name] = place[0]
            place[0] += (size + 31) // 32 * 32
            return t

        def over(name, shape, at, dt=F32):
            return nc.alloc_sbuf_tensor_at(name, list(shape), dt, offset=where[at])

        where = {}

        def sem(name):
            return ctx.enter_context(nc.semaphore(name))

        credited = []

        def signal(name, n, credit=0):
            sig = Signal(sem(name), n, credit)
            if credit:
                credited.append(sig.sem)
            return sig

        w_in = {h: sb(f"w_in_{h}", [P, KC, 2 * DI], F32R) for h in "hl"}
        w_dt = {h: sb(f"w_dt_{h}", [P, DB, DI], F32R) for h in "hl"}
        w_bc = sb("w_bc", [P, DB, 2 * DS])
        w_out = sb("w_out", [P, DB, C])
        w_kq = sb("w_kq", [P, KC, NQ])
        w_ao = sb("w_ao", [P, KC, C])
        w_fo = sb("w_fo", [P, KC, C])
        w_2 = sb("w_2", [P, KC, C])
        w_3 = sb("w_3", [P, KC, C])
        w_rt = {h: sb(f"w_rt_{h}", [P, KC, P], F32R) for h in "hl"}
        w_bd = {h: sb(f"w_bd_{h}", [P, KC, P], F32R) for h in "hl"}
        ws_in = [sb(f"ws_in{k}", [P, 2, KC, HB * P], F32R) for k in range(2)]
        ws_out = [sb(f"ws_out{k}", [P, HB, C]) for k in range(2)]
        xnh = sb("xnh", [P, KC, CT], F32R)
        xnl = sb("xnl", [P, KC, CT], F32R)
        xnf = over("xnf", [P, KC, CT], "xnl")
        bu = over("bu", [P, 4, CT], "xnh")
        zh = sb("zh", [P, DB, CT], F32R)
        zl = sb("zl", [P, DB, CT], F32R)
        hs = over("hs", [P, 2, DB, CT], "zh")
        stage = [over("stage0", [P, 2048], "zh"), over("stage1", [P, 2048], "zl")]
        z = sb("z", [P, DB, CT])
        dt = sb("dt", [P, DB, CT])
        modrow = over("modrow", [B, len(ROWS) * C], "z")
        gate = sb("gate", [P, NT, DI])
        acc = sb("acc", [P, NT, DI])
        wm = over("wm", [P, KC, 6 * C], "gate")
        h0 = over("h0", [P, NT, C], "acc")
        where["acc_hi"] = where["acc"] + 4 * NT * C
        n0 = over("n0", [P, NT, C], "acc_hi")
        bb = sb("bb", [P, 4, CT])
        modraw = over("modraw", [B, 6 * C], "bb")
        fh = sb("fh", [P, KC, CT], F32R)
        fl = sb("fl", [P, KC, CT], F32R)
        ff = over("ff", [P, KC, CT], "fl")
        bx = over("bx", [P, NT, C], "fh")
        ca = sb("ca", [P, KC, CT])
        cb = sb("cb", [P, KC, CT])
        hid = sb("hid", [P, HB, CT])
        qx = over("qx", [P, NT, C], "hid")
        xin = sb("xin", [P, NT, C])
        x1 = sb("x1", [P, NT, C])
        hA = sb("hA", [P, NT, C])
        nn = sb("nn", [P, NT, C])
        xd = sb("xd", [P, NT, C])
        mod_s = sb("mod_s", [P, NROW_S, C])
        mod_d = sb("mod_d", [P, NROW_D, C])
        b2_row = sb("b2_row", [P, C])
        bo_row = sb("bo_row", [P, C])
        ident = sb("ident", [P, P])
        rows8 = sb("rows8", [8, CT])
        bcs = sb("bcs", [2 * DS, CT])
        ctok = sb("ctok", [P, NT, 2 * DS])
        a_neg = sb("a_neg", [P, DB, DS])
        state = sb("state", [P, DS, DB])
        state_l = sb("state_l", [P, KC])
        keep = sb("keep", [P, NCH], I32)
        mhalf = sb("mhalf", [P, NT])
        cols = sb("cols", [P, 16])
        bdt_col = sb("bdt_col", [P, DB])
        b1_col = sb("b1_col", [P, F // P])
        bbeta_row = sb("bbeta_row", [P, NH])
        cs_row = sb("cs_row", [P, 3])
        c_in = over("c_in", [B, 2 * C], "xd")
        c_t = sb("c_t", [P, 2, KC, B])
        lnw_row = over("lnw_row", [B, 2 * C], "nn")
        st_s, mv_s, rs_s = sb("st_s", [P, NT, 6]), sb("mv_s", [P, NT, 2]), sb("rs_s", [P, NT])
        st_d, mv_d, rs_d = sb("st_d", [P, NT, 6]), sb("mv_d", [P, NT, 2]), sb("rs_d", [P, NT])
        carrier = sb("carrier", [P, 2])
        eps_t = sb("eps_t", [P, NT])
        lg = sb("lg", [P, NT, E_MOE])
        lg_m = sb("lg_m", [P, NT])
        prob = sb("prob", [P, NT])
        sm = sb("sm", [P, NT, 3 * NH])
        bl = sb("bl", [P, NT, 8])
        sg = sb("sg", [P, NT, 4])
        bid = sb("bid", [P, NT, 3])
        bmax = sb("bmax", [P, NT])
        win = sb("win", [P, NT, 3])
        wc = sb("wc", [P, NT, 3])
        wcs = sb("wcs", [P, NT])
        coef = sb("coef", [P, NT, 3])
        assert place[0] <= nc.sbuf_usable_end, place[0]

        w_split = nc.dram_tensor("w_split", (NSLOT, P, 2 * KC * HB * P), F32, kind="Internal").ap()
        mods = nc.dram_tensor("mods", (NCH, len(ROWS) * C), F32, kind="Internal").ap()
        b_rows = nc.dram_tensor("b_rows", (DS, CT), F32, kind="Internal").ap()

        psum = {name: ctx.enter_context(nc.psum_tensor(f"ps_{name}", [P, CT], F32)) for name in BANK_USES}
        bank = {name: Bank(psum[name], sem(f"full_{name}"), sem(f"free_{name}"), uses)
                for name, uses in BANK_USES.items()}
        bank_of = {use: bank[name] for name in BANK_USES for use in BANK_USES[name]}

        def fill(eng, chunk, use):
            b = bank_of[use]
            n = b.fills_before(chunk, use)
            if not (isinstance(n, int) and n == CREDIT):
                eng.wait_ge(b.free, n)
            return b

        def take(eng, chunk, use):
            b = bank_of[use]
            eng.wait_ge(b.full, b.fills_with(chunk, use))
            return b

        def used(eng, chunk, use):
            b = bank_of[use]
            eng.wait_ge(b.free, b.fills_with(chunk, use))

        def kp(ap):
            return ap.rearrange("(k p) m -> p k m", p=P)

        def col(ap):
            return ap.rearrange("(k p) -> p k", p=P)

        def row(ap):
            return ap.rearrange("(a n) -> a n", a=1)

        s_xin = signal("s_xin", 16)
        s_mods = signal("s_mods", 16)
        s_modd = [signal(f"s_modd{k}", 16) for k in range(3)]
        s_bw = signal("s_bw", 16)
        s_bb = [signal(f"s_bb{k}", 16 * DS // 4) for k in range(4)]
        s_w = [signal(f"s_w{k}", 0) for k in range(2)]
        s_out = signal("s_out", 16, CREDIT)
        s_mv = signal("s_mv", 2)
        s_rs = signal("s_rs", 2)
        s_n = signal("s_n", 2)
        s_h0 = signal("s_h0", 1)
        s_xg = signal("s_xg", 1)
        s_xnh = signal("s_xnh", KC)
        s_xnl = signal("s_xnl", KC)
        s_zh = signal("s_zh", DB)
        s_zl = signal("s_zl", DB)
        s_sp = signal("s_sp", DB)
        s_dt = signal("s_dt", DB)
        s_u = signal("s_u", DB)
        s_bu = signal("s_bu", DS * DB)
        s_yg = signal("s_yg", 1)
        s_x1 = signal("s_x1", 1, CREDIT)
        d_mv = signal("d_mv", 6)
        d_rs = signal("d_rs", 6)
        d_n = signal("d_n", 6)
        d_h = signal("d_h", 3)
        d_fh = signal("d_fh", 3 * KC)
        d_fl = signal("d_fl", 3 * KC)
        d_lsub = signal("d_lsub", 1)
        d_lexp = signal("d_lexp", 1)
        d_rl = signal("d_rl", 16)
        d_hfree = signal("d_hfree", 3 * (NHB - 1), CREDIT)
        d_x2 = signal("d_x2", 1, CREDIT)
        d_sm = signal("d_sm", 1)
        d_bx = signal("d_bx", 2)
        d_hb = signal("d_hb", 1)
        d_y2 = signal("d_y2", 1)
        d_xb = signal("d_xb", 1)
        d_x3 = signal("d_x3", 1, CREDIT)
        d_sg = signal("d_sg", 1)
        d_x5 = signal("d_x5", 1, CREDIT)
        o_dve_s = signal("o_dve_s", OWN["dve_s"])
        o_dve_d = signal("o_dve_d", OWN["dve_d"])
        o_pool_s = signal("o_pool_s", OWN["pool_s"])
        o_pool_d = signal("o_pool_d", OWN["pool_d"])
        o_act_s = signal("o_act_s", OWN["act_s"])

        u_load = sem("u_load")
        u_stage = [sem("u_stage0"), sem("u_stage1")]
        u_wm = sem("u_wm")
        u_split = sem("u_split")
        u_store = [sem("u_store0"), sem("u_store1")]
        u_dve = sem("u_dve")
        u_id = sem("u_id")
        u_silu = sem("u_silu")
        u_exp = sem("u_exp")
        u_ct = sem("u_ct")
        u_ctc = sem("u_ctc")
        u_mm = sem("u_mm")
        u_raw = sem("u_raw")
        u_rows = sem("u_rows")
        u_sum = sem("u_sum")
        u_zero = sem("u_zero")
        u_mods = sem("u_mods")
        u_wsm = sem("u_wsm")

        e_last = E_MOE - 1
        k_r, v_r = w["L1_ffn_K_rwkv"], w["L1_ffn_V_rwkv"]
        pieces = [
            [(0, DI, kp(w["L0_attn_W_in"])), (DI, DI, kp(w["L0_attn_W_gate"]))],
            [(0, DI, kp(w["L0_attn_W_dt"]))],
            [(0, HB * P, kp(w["L0_ffn_W1"][e_last])[:, :, 0:HB * P])],
            [(0, HB * P, kp(w["L0_ffn_W1"][e_last])[:, :, HB * P:F])],
            [(0, C, kp(w["L1_ffn_Wr"])), (C, C, kp(w["L1_ffn_Wv"]))],
            [(0, C, kp(w["L1_ffn_Ws"])), (C, C, kp(w["L1_ffn_W1"]))],
            [(0, HB * P, kp(k_r[0])[:, :, 0:HB * P])],
            [(0, HB * P, kp(k_r[0])[:, :, HB * P:F])],
            [(0, HB * P, kp(k_r[1])[:, :, 0:HB * P])],
            [(0, HB * P, kp(k_r[1])[:, :, HB * P:F])],
        ]
        shapes = [(KC, 2 * DI), (DB, DI)] + [(KC, HB * P)] * NSLOT
        w_down = {"ffn_0": w["L0_ffn_W2"][e_last][0:HB * P], "ffn_1": w["L0_ffn_W2"][e_last][HB * P:F],
                  "e0_0": v_r[0][0:HB * P], "e0_1": v_r[0][HB * P:F],
                  "e1_0": v_r[1][0:HB * P], "e1_1": v_r[1][HB * P:F]}

        def staged(n, shape):
            k, m = shape
            return stage[n % 2][:, 0:k * m].rearrange("p (k m) -> p k m", k=k)

        small = [
            (w_bc[:, :, 0:DS], kp(w["L0_attn_W_C"])), (w_bc[:, :, DS:2 * DS], kp(w["L0_attn_W_B"])),
            (w_out[:, :, :], kp(w["L0_attn_W_out"])), (w_kq[:, :, 0:C], kp(w["L1_attn_Wk"])),
            (w_kq[:, :, C + 2 * NH:NQ], kp(w["L1_attn_Wbeta"])), (w_ao[:, :, :], kp(w["L1_attn_Wo"])),
            (w_fo[:, :, :], kp(w["L1_ffn_Wo"])), (w_2[:, :, :], kp(w["L1_ffn_W2"])),
            (w_3[:, :, :], kp(w["L1_ffn_W3"])),
            (cols[:, 0:2], col(w["L0_attn_norm_w"])), (cols[:, 2:4], col(w["L0_attn_norm_b"])),
            (cols[:, 4:6], col(w["L1_ffn_ln1_w"])), (cols[:, 6:8], col(w["L1_ffn_ln1_b"])),
            (cols[:, 8:10], col(w["L1_ffn_ln2_w"])), (cols[:, 10:12], col(w["L1_ffn_ln2_b"])),
            (bdt_col[:, :], col(w["L0_attn_b_dt"])), (b1_col[:, :], col(w["L0_ffn_b1"][e_last])),
            (bbeta_row[:, :], row(w["L1_attn_b_beta"]).to_broadcast([P, NH])),
            (cs_row[:, :], row(w["L1_ffn_capital_shares"]).to_broadcast([P, 3])),
            (b2_row[:, :], row(w["L0_ffn_b2"][e_last]).to_broadcast([P, C])),
            (bo_row[:, :], row(w["L1_attn_b_o"]).to_broadcast([P, C])),
            (lnw_row[:, 0:C], row(w["L1_attn_ln_g"]).to_broadcast([B, C])),
            (lnw_row[:, C:2 * C], row(w["L1_attn_ln_b"]).to_broadcast([B, C])),
            (c_in[:, 0:C], w["L0_c"]), (c_in[:, C:2 * C], w["L1_c"]),
            (a_neg[:, :, :], w["L0_attn_A_log"].rearrange("(d p) s -> p d s", p=P)),
        ]
        pad = [ca[:, 0, 0:KC * P].rearrange("p (k m) -> p k m", k=KC),
               ca[:, 1, 0:KC * P].rearrange("p (k m) -> p k m", k=KC)]
        padded = []
        for k in range(KC):
            ch = slice(k * P, (k + 1) * P)
            padded += [(pad[0][:, k, 0:E_MOE], w["L0_ffn_Wr"][:, ch].rearrange("e p -> p e")),
                       (pad[1][:, k, 0:2], w["L1_ffn_conf_rwkv"][:, ch].rearrange("e p -> p e")),
                       (pad[1][:, k, 2:3], w["L1_ffn_conf_trans"][ch].rearrange("(p a) -> p a", a=1)),
                       (pad[1][:, k, 3:4], w["L1_ffn_w_diff"][ch].rearrange("(p a) -> p a", a=1)),
                       (pad[1][:, k, 4:7], w["L1_ffn_W_aff"][ch, :])]
        qv = [hid[:, 0:1, :], hid[:, 1:2, :]]
        wq_st = cb[:, :, 0:C]
        wv_st = cb[:, :, C:2 * C]

        with nc.Block() as block:

            def store_split(sp, n):
                if n < 2:
                    return
                sp.wait_ge(u_split, n + 1)
                sp.dma_start(w_split[n - 2], ws_in[n % 2][:, :, :, :].bitcast(F32).rearrange("p h k m -> p (h k m)"))\
                  .then_inc(u_store[n % 2], 16)

            @block.sync
            def _(sp):
                for semaphore in credited + [x for b in bank.values() for x in (b.full, b.free)]:
                    sp.sem_inc(semaphore, CREDIT)
                for dst, src in small:
                    sp.dma_start(dst, src).then_inc(u_load, 16)
                for k, name in enumerate(["L1_attn_Wq", "L1_attn_Wv"]):
                    sp.dma_start((wq_st, wv_st)[k], kp(w[name])).then_inc(u_load, 16)
                sp.wait_ge(u_zero, 1)
                for dst, src in padded:
                    sp.dma_start(dst, src).then_inc(u_load, 16)
                for n, (loads, shape) in enumerate(zip(pieces, shapes)):
                    if n >= 2:
                        sp.wait_ge(u_split, n - 1)
                    for at, m, src in loads:
                        sp.dma_start(staged(n, shape)[:, :, at:at + m], src).then_inc(u_stage[n % 2], 16)
                    if n >= 3:
                        store_split(sp, n - 1)
                store_split(sp, len(pieces) - 1)
                for k in range(2):
                    sp.wait_ge(u_store[k], 16 * NSLOT // 2)
                sp.wait_ge(u_rows, 2)
                for b in range(B):
                    for c in range(CPB):
                        sp.dma_start(mods[b * CPB + c:b * CPB + c + 1, :], modrow[b:b + 1, :]).then_inc(u_mods, 16)
                sp.wait_ge(u_mods, 16 * NCH)

            @block.gpsimd
            def _(pool):
                pool.memset(ca[:, :, :], 0.0).then_inc(u_zero, 1)
                pool.memset(ident[:, :], 0.0).then_inc(u_id, 1)
                pool.memset(keep[:, :], -1).then_inc(u_id, 1)
                pool.memset(mhalf[:, :], -0.5).then_inc(u_id, 1)
                pool.memset(eps_t[:, :], EPS)
                pool.wait_ge(u_id, 3)
                pool.affine_select(out=ident[:, :], in_=ident[:, :], compare_op=ALU.not_equal, fill=1.0,
                                   base=0, pattern=[[-1, P]], channel_multiplier=1).then_inc(u_id, 1)
                pool.memset(keep[:, 0:NCH:CPB], 0).then_inc(u_id, 1)
                pool.memset(state[:, :, :], 0.0).then_inc(u_id, 1)
                pool.memset(state_l[:, :], 0.0).then_inc(u_id, 1)

            n_small = 16 * (len(small) + 2 + len(padded))

            @block.scalar
            def _(act):
                act.wait_ge(u_load, n_small)
                act.activation(c_in[:, :], c_in[:, :], ACT.Silu).then_inc(u_silu, 1)
                act.activation(a_neg[:, :, :], a_neg[:, :, :], ACT.Exp).then_inc(u_exp, 1)
                for layer in range(2):
                    if layer:
                        act.wait_ge(u_mm, 3)
                    act.dma_start(wm[:, :, :], kp(w[f"L{layer}_wmod"])).then_inc(u_wm, 16)

            @block.tensor
            def _(pe):
                pe.wait_ge(u_silu, 1)
                pe.wait_ge(u_id, 7)
                for layer in range(2):
                    for k in range(KC):
                        at = layer * C + k * P
                        last = pe.transpose(psum["A0"][:, (layer * KC + k) * B:(layer * KC + k + 1) * B],
                                            c_in[:, at:at + P], ident[0:B, 0:B])
                last.then_inc(u_ct, 1)
                pe.wait_ge(u_ctc, 1)
                for layer in range(2):
                    pe.wait_ge(u_wm, 16 * (layer + 1))
                    for g in range(3):
                        name = ["B0", "B1", "B2"][g]
                        if layer:
                            pe.wait_ge(u_raw, g + 1)
                        for k in range(KC):
                            last = pe.matmul(psum[name][0:B, :], c_t[:, layer, k, :],
                                             wm[:, k, g * 2 * C:(g + 1) * 2 * C], start=k == 0, stop=k == KC - 1)
                        last.then_inc(u_mm, 1)

            @block.vector
            def _(dve):
                done = [0]

                def step(ins):
                    done[0] += 1
                    ins.then_inc(u_dve, 1)
                    dve.wait_ge(u_dve, done[0])

                for n, (loads, shape) in enumerate(zip(pieces, shapes)):
                    earlier = sum(len(l) for l, _ in list(zip(pieces, shapes))[n % 2:n:2])
                    dve.wait_ge(u_stage[n % 2], 16 * (earlier + len(loads)))
                    src = staged(n, shape)
                    if n == 0:
                        high, low = w_in["h"][:, :, :], w_in["l"][:, :, :]
                    elif n == 1:
                        high, low = w_dt["h"][:, :, :], w_dt["l"][:, :, :]
                    else:
                        high, low = ws_in[n % 2][:, 0], ws_in[n % 2][:, 1]
                        if n >= 4:
                            dve.wait_ge(u_store[n % 2], 16 * ((n - 2) // 2))
                    step(dve.tensor_copy(high, src))
                    dve.tensor_tensor(low, src, high.bitcast(F32), ALU.subtract).then_inc(u_split, 1)
                dve.wait_ge(u_load, n_small)
                for k, wt in enumerate((w_rt, w_bd)):
                    step(dve.tensor_copy(wt["h"][:, :, :], pad[k]))
                    step(dve.tensor_tensor(wt["l"][:, :, :], pad[k], wt["h"][:, :, :].bitcast(F32), ALU.subtract))
                for k, wt in enumerate((wq_st, wv_st)):
                    for c in range(KC):
                        step(dve.tensor_reduce(w_kq[:, c, C + k * NH:C + (k + 1) * NH],
                                               wt[:, c, :].rearrange("p (h d) -> p h d", h=NH), AX, ALU.add))
                dve.wait_ge(u_exp, 1)
                step(dve.tensor_scalar(a_neg[:, :, :], a_neg[:, :, :], 1e-6, 1.0, ALU.max, ALU.min))
                step(dve.tensor_scalar(a_neg[:, :, :], a_neg[:, :, :], -1.0, None, ALU.mult))
                dve.wait_ge(u_ct, 1)
                dve.tensor_copy(c_t[:, :, :, :], psum["A0"][:, 0:2 * KC * B]
                                .rearrange("p (l k b) -> p l k b", l=2, k=KC)).then_inc(u_ctc, 1)

                def mrow(name):
                    return modrow[:, ROW[name] * C:(ROW[name] + 1) * C]

                for layer in range(2):
                    for g in range(3):
                        dve.wait_ge(u_mm, 3 * layer + g + 1)
                        dve.tensor_copy(modraw[:, g * 2 * C:(g + 1) * 2 * C], psum[["B0", "B1", "B2"][g]][0:B, :])\
                           .then_inc(u_raw, 1)
                    dve.wait_ge(u_raw, 3 * layer + 3)
                    raw = [modraw[:, k * C:(k + 1) * C] for k in range(6)]
                    for part, (sa, ca_, ga) in enumerate((raw[0:3], raw[3:6])):
                        p_ = "AB"[part]
                        if part == 0:
                            dve.tensor_copy(mrow(f"sA{layer}"), sa)
                        step(dve.tensor_scalar(mrow(f"c{p_}{layer}"), ca_, 1.0, None, ALU.add))
                        goal = mrow("gA1w") if (layer, part) == (1, 0) else mrow(f"g{p_}{layer}")
                        step(dve.tensor_scalar(ca_, ga, 0.0, 2.0, ALU.is_ge, ALU.mult))
                        step(dve.tensor_scalar(ca_, ca_, -1.0, None, ALU.add))
                        step(dve.scalar_tensor_tensor(out=ga, in0=ga, scalar=-1.0, in1=ga, op0=ALU.mult, op1=ALU.max))
                        step(dve.tensor_scalar(ga, ga, GATE_MIN, None, ALU.max))
                        step(dve.tensor_tensor(ga, ga, ca_, ALU.mult))
                        if (layer, part) == (1, 0):
                            step(dve.tensor_tensor(mrow("gA1b"), ga, lnw_row[:, C:2 * C], ALU.mult))
                            step(dve.tensor_tensor(goal, ga, lnw_row[:, 0:C], ALU.mult))
                        else:
                            step(dve.tensor_copy(goal, ga))
                    dve.tensor_copy(mrow(f"sB{layer}"), raw[3]).then_inc(u_rows, 1)
                    dve.wait_ge(u_rows, layer + 1)

        x_v = w["L0_attn_x"].rearrange("b (c t p) m -> (b c) p t m", t=NT, p=P)
        out_v = out.rearrange("b (c t p) m -> (b c) p t m", t=NT, p=P)

        slot_dmas = [2 if name in w_down else 1 for name in SLOTS]
        for k in range(2):
            s_w[k].n = 16 * sum(slot_dmas[k::2])

        def slot_ready(eng, j, name):
            q = SLOTS.index(name)
            eng.wait_ge(s_w[q % 2].sem, s_w[q % 2].at(j, 16 * sum(slot_dmas[q % 2:q + 1:2])))

        def block_used(eng, j, n):
            k, e = n % NHB, n // NHB
            if k == NHB - 1:
                take(eng, j, ["ffn1", "e0_1", "e1_1"][e])
            else:
                eng.wait_ge(d_hfree.sem, d_hfree.at(j, (NHB - 1) * e + k + 1))

        def per_tile(m):
            return m.unsqueeze(1).to_broadcast([P, NT, C])

        def m_s(name):
            return mod_s[:, ROW[name], :]

        def m_d(name):
            return mod_d[:, ROW[name] - NROW_S, :]

        with nc.Block() as block:

            @block.sync
            def _(sp):
                def load_x(i):
                    since(sp, s_x1, i)
                    sp.dma_start(xin[:, :, :], x_v[bass.ds(i, 1)].rearrange("a p t m -> p (a t) m"))\
                      .then_inc(s_xin.sem, 16)
                    sp.dma_start(mod_s[:, :, :].rearrange("p r m -> p (r m)"),
                                 mods[bass.ds(i, 1), 0:NROW_S * C].to_broadcast([P, NROW_S * C]))\
                      .then_inc(s_mods.sem, 16)

                def front(i):
                    load_x(i)
                    used(sp, i, "bc")
                    sp.dma_start(b_rows[:, :], bcs[DS:2 * DS, :]).then_inc(s_bw.sem, 16)
                    sp.wait_ge(s_bw.sem, s_bw.at(i, 16))

                def unit(i, u):
                    if u % DB == 0 and u // DB < DS:
                        s = u // DB
                        if s >= 4:
                            sp.wait_ge(s_bu.sem, s_bu.at(i, DB * (s - 3)))
                        sp.dma_start(bb[:, s % 4, :], b_rows[s:s + 1, :].to_broadcast([P, CT]))\
                          .then_inc(s_bb[s % 4].sem, 16)

                def load_mod(j, k):
                    lo, hi = [(0, 3), (3, 7), (7, 10)][k]
                    since(sp, (d_x2, d_x3, d_x5)[k], j)
                    sp.dma_start(mod_d[:, lo:hi, :].rearrange("p r m -> p (r m)"),
                                 mods[bass.ds(j, 1), (NROW_S + lo) * C:(NROW_S + hi) * C]
                                 .to_broadcast([P, (hi - lo) * C])).then_inc(s_modd[k].sem, 16)

                def load_slot(j, name):
                    q = SLOTS.index(name)
                    before = {"ffn_1": ("start", "B3"), "rv": ("block", 3), "sw": ("full", "ffn1"),
                              "e0_0": ("full", "v1"), "e0_1": ("full", "tw1"), "e1_0": ("block", NHB + 3),
                              "e1_1": ("full", "e0_1")}
                    kind, what = before.get(name, ("start", None))
                    if kind == "full":
                        take(sp, j, what)
                    elif kind == "block":
                        block_used(sp, j, what)
                    elif what is None:
                        since(sp, d_hfree, j)
                    else:
                        last = bank[what]
                        sp.wait_ge(last.full, j * len(last.uses) + CREDIT)
                    sp.dma_start(ws_in[q % 2][:, :, :, :].bitcast(F32).rearrange("p h k m -> p (h k m)"), w_split[q])\
                      .then_inc(s_w[q % 2].sem, 16)
                    if name in w_down:
                        sp.dma_start(ws_out[q % 2][:, :, :], kp(w_down[name])).then_inc(s_w[q % 2].sem, 16)

                def dense(j, pace):
                    load_mod(j, 0)
                    load_mod(j, 1)
                    load_mod(j, 2)
                    load_slot(j, "ffn_0")
                    load_slot(j, "ffn_1")
                    pace("c3")
                    load_slot(j, "rv")
                    pace("c7")
                    load_slot(j, "sw")
                    pace("k_proj")
                    load_slot(j, "e0_0")
                    pace("n_trans")
                    load_slot(j, "e0_1")
                    pace("o3")
                    load_slot(j, "e1_0")
                    pace("o7")
                    load_slot(j, "e1_1")
                    pace("q_out")
                    sp.wait_ge(d_x5.sem, d_x5.at(j, 1))
                    sp.dma_start(out_v[bass.ds(j, 1)].rearrange("a p t m -> p (a t) m"), xd[:, :, :])\
                      .then_inc(s_out.sem, 16)

                front(0)
                Pace(unit, 0).upto(SSM_UNITS)
                with sp.Fori(1, NCH) as i:
                    front(i)
                    pace = Pace(unit, i)
                    pace.upto(1)
                    dense(i - 1, pace)
                dense(NCH - 1, Pace(None, 0))
                sp.wait_ge(s_out.sem, s_out.at(NCH, 0))

            @block.gpsimd
            def _(pool):
                def rstd(own, mv, rs, mv_at, sig):
                    own.step(pool.tensor_tensor(rs[:, :], mv[:, :, 1], eps_t[:, :], ALU.add))
                    pool.tensor_tensor(rs[:, :], rs[:, :], mhalf[:, :], ALU.pow).then_inc(sig.sem, 1)

                def front(i):
                    own = Own(pool, o_pool_s, i)
                    pool.wait_ge(s_mv.sem, s_mv.at(i, 1))
                    rstd(own, mv_s, rs_s, 1, s_rs)
                    pool.wait_ge(s_mods.sem, s_mods.at(i, 16))
                    pool.wait_ge(s_n.sem, s_n.at(i, 1))
                    own.step(pool.tensor_tensor(h0[:, :, :], h0[:, :, :], per_tile(m_s("cA0")), ALU.mult))
                    pool.tensor_tensor(h0[:, :, :], h0[:, :, :], per_tile(m_s("sA0")), ALU.add).then_inc(s_h0.sem, 1)
                    pool.wait_ge(s_mv.sem, s_mv.at(i, 2))
                    rstd(own, mv_s, rs_s, 2, s_rs)
                    pool.wait_ge(s_n.sem, s_n.at(i, 2))
                    own.step(pool.tensor_tensor(h0[:, :, :], h0[:, :, :], per_tile(m_s("gA0")), ALU.mult))
                    pool.tensor_tensor(xin[:, :, :], xin[:, :, :], h0[:, :, :], ALU.add).then_inc(s_xg.sem, 1)
                    for d in range(DB):
                        pool.wait_ge(s_dt.sem, s_dt.at(i, d + 1))
                        pool.tensor_tensor(z[:, d, :], z[:, d, :], dt[:, d, :], ALU.mult).then_inc(s_u.sem, 1)
                    own.end()

                def unit(i, u):
                    s, d = u // DB, u % DB
                    if s == DS:
                        return
                    if s == 0:
                        pool.wait_ge(s_u.sem, s_u.at(i, d + 1))
                    if d == 0:
                        pool.wait_ge(s_bb[s % 4].sem, s_bb[s % 4].at(i, 16 * (s // 4 + 1)))
                    if u >= 4:
                        used(pool, i, f"dA{u - 4}")
                    ins = pool.tensor_tensor(bu[:, u % 4, :], z[:, d, :], bb[:, s % 4, :], ALU.mult)
                    ins.then_inc(s_bu.sem, 1)

                def modulate(own, j, k, scale, shift):
                    own.step(pool.tensor_tensor(hA[:, :, :], hA[:, :, :], per_tile(m_d(scale)), ALU.mult))
                    pool.tensor_tensor(hA[:, :, :], hA[:, :, :], per_tile(m_d(shift)), ALU.add).then_inc(d_h.sem, 1)

                def norm(own, j, k):
                    pool.wait_ge(d_mv.sem, d_mv.at(j, k + 1))
                    rstd(own, mv_d, rs_d, k + 1, d_rs)

                def dense(j, pace):
                    own = Own(pool, o_pool_d, j)
                    pace("a_stats")
                    norm(own, j, 0)
                    pool.wait_ge(s_modd[0].sem, s_modd[0].at(j, 16))
                    pool.wait_ge(d_n.sem, d_n.at(j, 1))
                    modulate(own, j, 0, "cB0", "sB0")
                    pace("b_turn")
                    pace("e_stats")
                    norm(own, j, 1)
                    pool.wait_ge(s_modd[1].sem, s_modd[1].at(j, 16))
                    pool.wait_ge(d_n.sem, d_n.at(j, 2))
                    modulate(own, j, 1, "cA1", "sA1")
                    pool.tensor_tensor(xd[:, :, :], xd[:, :, :], per_tile(m_d("gA1b")), ALU.add).then_inc(d_xb.sem, 1)
                    pace("f_kv")
                    used(pool, j, "h2T1")
                    pool.tensor_tensor(hA[:, :, :], hA[:, :, :], per_tile(bo_row[:, :]), ALU.add).then_inc(d_hb.sem, 1)
                    pace("h_stats")
                    norm(own, j, 2)
                    pool.wait_ge(d_n.sem, d_n.at(j, 3))
                    own.step(pool.tensor_tensor(nn[:, :, :], nn[:, :, :], per_tile(m_d("gA1w")), ALU.mult))
                    pool.wait_ge(d_xb.sem, d_xb.at(j, 1))
                    pool.tensor_tensor(xd[:, :, :], xd[:, :, :], nn[:, :, :], ALU.add).then_inc(d_x3.sem, 1)
                    pace("i_stats")
                    norm(own, j, 3)
                    pool.wait_ge(s_modd[2].sem, s_modd[2].at(j, 16))
                    pool.wait_ge(d_n.sem, d_n.at(j, 4))
                    modulate(own, j, 2, "cB1", "sB1")
                    pace("i_stats2")
                    norm(own, j, 4)
                    pace("j_turn")
                    pace("m_stats")
                    norm(own, j, 5)
                    pace("m_turn")
                    pace("q_out")
                    own.end()

                front(0)
                Pace(unit, 0).upto(SSM_UNITS)
                with pool.Fori(1, NCH) as i:
                    front(i)
                    dense(i - 1, Pace(unit, i))
                dense(NCH - 1, Pace(None, 0))

            @block.scalar
            def _(act):
                def front(i):
                    own = Own(act, o_act_s, i)
                    for k in range(KC):
                        b = take(act, i, f"xn{k}")
                        act.activation(xnf[:, k, :], b.t[:, :], ACT.Identity, scale=cols[:, k:k + 1],
                                       bias=cols[:, 2 + k:3 + k]).then_inc(b.free, 1)
                    for k in range(KC):
                        used(act, i, f"xn{k}")
                        act.activation(xnh[:, k, :], xnf[:, k, :], ACT.Copy).then_inc(s_xnh.sem, 1)
                    for d in range(DB):
                        b = take(act, i, f"z{d}")
                        act.activation(zh[:, d, :], b.t[:, :], ACT.Copy).then_inc(s_zh.sem, 1)
                        act.activation(z[:, d, :], b.t[:, :], ACT.Copy).then_inc(b.free, 1)
                    for t in range(NT):
                        b = take(act, i, f"gt{t}")
                        act.activation(gate[:, t, :], b.t[:, :], ACT.Silu).then_inc(b.free, 1)
                    b = take(act, i, "bc")
                    act.activation(bcs[:, :], b.t[0:2 * DS, :], ACT.Copy).then_inc(b.free, 1)
                    b = take(act, i, "ct")
                    act.activation(ctok[:, :, :], b.t[:, 0:NT * 2 * DS].rearrange("p (t c) -> p t c", t=NT),
                                   ACT.Copy).then_inc(b.free, 1)
                    for d in range(DB):
                        used(act, i, f"dt{d}")
                        own.mark(act.activation(dt[:, d, :], dt[:, d, :], ACT.Exp))
                    for d in range(DB):
                        own.wait(d + 1)
                        act.activation(dt[:, d, :], dt[:, d, :], ACT.Ln, bias=1.0).then_inc(s_sp.sem, 1)
                    own.end()

                def unit(i, u):
                    s, d = u // DB, u % DB
                    if s == DS:
                        return
                    if s == 0:
                        act.wait_ge(s_dt.sem, s_dt.at(i, d + 1))
                    b = fill(act, i, f"dA{u}")
                    act.activation(b.t[:, :], dt[:, d, :], ACT.Exp, scale=a_neg[:, d, s:s + 1]).then_inc(b.full, 1)

                def tail(i):
                    for k in range(DB):
                        b = take(act, i, f"y{k}")
                        act.activation(z[:, k, :], b.t[:, :], ACT.Copy).then_inc(b.free, 1)

                def turned(j, use, scale=None, shift=None):
                    for k in range(KC):
                        b = take(act, j, f"{use}{k}")
                        if scale is None:
                            ins = act.activation(ff[:, k, :], b.t[:, :], ACT.Copy)
                        else:
                            ins = act.activation(ff[:, k, :], b.t[:, :], ACT.Identity,
                                                 scale=cols[:, scale + k:scale + k + 1],
                                                 bias=cols[:, shift + k:shift + k + 1])
                        ins.then_inc(b.free, 1)

                def high(j, use):
                    for k in range(KC):
                        used(act, j, f"{use}{k}")
                        act.activation(fh[:, k, :], ff[:, k, :], ACT.Copy).then_inc(d_fh.sem, 1)

                def to_rows(j, use):
                    b = take(act, j, use)
                    act.activation(rows8[:, :], b.t[0:8, :], ACT.Copy).then_inc(b.free, 1)

                def dense(j, pace):
                    pace("b_turn")
                    turned(j, "h1T")
                    high(j, "h1T")
                    to_rows(j, "router")
                    act.wait_ge(d_lsub.sem, d_lsub.at(j, 1))
                    act.activation(lg[:, :, :], lg[:, :, :], ACT.Exp).then_inc(d_lexp.sem, 1)
                    pace("b_router")
                    for k in range(F // P):
                        b = take(act, j, f"c{k}")
                        if k >= HB:
                            block_used(act, j, k - HB)
                        act.activation(hid[:, k % HB, :], b.t[:, :], ACT.Gelu, bias=b1_col[:, k:k + 1])\
                           .then_inc(b.free, 1)
                        pace(f"c{k}")
                    pace("f_turn")
                    turned(j, "h2T")
                    pace("f_kv")
                    act.wait_ge(d_sm.sem, d_sm.at(j, 1))
                    act.activation(bx[:, :, :].rearrange("p t (h d) -> p t h d", h=NH),
                                   sm[:, :, 2 * NH:3 * NH].unsqueeze(3).to_broadcast([P, NT, NH, HD]),
                                   ACT.Sigmoid).then_inc(d_bx.sem, 1)
                    act.activation(qx[:, :, :].rearrange("p t (h d) -> p t h d", h=NH),
                                   sm[:, :, 0:NH].unsqueeze(3).to_broadcast([P, NT, NH, HD]),
                                   ACT.Copy).then_inc(d_bx.sem, 1)
                    for k in range(KC):
                        b = take(act, j, f"kvT{k}")
                        act.activation(ca[:, k, :], b.t[:, :], ACT.Copy).then_inc(b.free, 1)
                    pace("j_turn")
                    turned(j, "xlT", 4, 6)
                    high(j, "xlT")
                    pace("k_proj")
                    for k in range(KC):
                        b = take(act, j, f"r{k}")
                        act.activation(cb[:, k, :], b.t[:, :], ACT.Sigmoid).then_inc(b.free, 1)
                    for k in range(KC):
                        b = take(act, j, f"s{k}")
                        act.activation(ca[:, k, :], b.t[:, :], ACT.Copy).then_inc(b.free, 1)
                    pace("l_out")
                    for k in range(KC):
                        b = take(act, j, f"sW{k}")
                        act.activation(cb[:, k, :], b.t[:, :], ACT.Sigmoid).then_inc(b.free, 1)
                    pace("m_turn")
                    turned(j, "hhT", 8, 10)
                    high(j, "hhT")
                    pace("n_bids")
                    to_rows(j, "bids")
                    used(act, j, "bidsT")
                    act.activation(sg[:, :, :], bl[:, :, 0:4], ACT.Sigmoid).then_inc(d_sg.sem, 1)
                    pace("n_trans")
                    for e in range(2):
                        for k in range(F // P):
                            use = f"{'op'[e]}{k}"
                            n = 8 * e + k
                            b = take(act, j, use)
                            block_used(act, j, NHB + n - HB)
                            act.activation(hid[:, k % HB, :], b.t[:, :], ACT.Relu).then_inc(d_rl.sem, 1)
                            pace(use)
                    pace("q_out")

                front(0)
                Pace(unit, 0).upto(SSM_UNITS)
                tail(0)
                with act.Fori(1, NCH) as i:
                    front(i)
                    dense(i - 1, Pace(unit, i))
                    tail(i)
                dense(NCH - 1, Pace(None, 0))

            @block.vector
            def _(dve):
                def stats(own, src, st, mv, sig):
                    for t in range(NT):
                        own.mark(dve.bn_stats(st[:, t, :], src[:, t, :]))
                    own.wait()
                    dve.memset(carrier[:, :], 0.0)
                    for t in range(NT):
                        ins = dve.bn_aggr(mv[:, t, :], st[:, t, :])
                    ins.then_inc(sig.sem, 1)

                def apply(dst, src, mv, rs, sig):
                    for t in range(NT):
                        ins = dve.tensor_scalar(dst[:, t, :], src[:, t, :], mv[:, t, 0:1], rs[:, t:t + 1],
                                                ALU.subtract, ALU.mult)
                    ins.then_inc(sig.sem, 1)

                def front(i):
                    own = Own(dve, o_dve_s, i)
                    dve.wait_ge(s_xin.sem, s_xin.at(i, 16))
                    stats(own, xin, st_s, mv_s, s_mv)
                    own.mark(dve.tensor_tensor(state[:, :, :].rearrange("p s d -> p (s d)").bitcast(I32),
                                               state[:, :, :].rearrange("p s d -> p (s d)").bitcast(I32),
                                               keep[:, bass.ds(i, 1)].to_broadcast([P, DS * DB]), ALU.bitwise_and))
                    dve.wait_ge(s_rs.sem, s_rs.at(i, 1))
                    apply(h0, xin, mv_s, rs_s, s_n)
                    dve.wait_ge(s_h0.sem, s_h0.at(i, 1))
                    stats(own, h0, st_s, mv_s, s_mv)
                    dve.wait_ge(s_rs.sem, s_rs.at(i, 2))
                    apply(n0, h0, mv_s, rs_s, s_n)
                    for k in range(KC):
                        dve.wait_ge(s_xnh.sem, s_xnh.at(i, k + 1))
                        dve.tensor_tensor(xnl[:, k, :], xnf[:, k, :], xnh[:, k, :].bitcast(F32), ALU.subtract)\
                           .then_inc(s_xnl.sem, 1)
                    for d in range(DB):
                        used(dve, i, f"z{d}")
                        dve.tensor_tensor(zl[:, d, :], z[:, d, :], zh[:, d, :].bitcast(F32), ALU.subtract)\
                           .then_inc(s_zl.sem, 1)
                    for d in range(DB):
                        b = take(dve, i, f"dt{d}")
                        dve.tensor_scalar(dt[:, d, :], b.t[:, :], bdt_col[:, d:d + 1], DT_CLAMP, ALU.add, ALU.min)\
                           .then_inc(b.free, 1)
                    for d in range(DB):
                        dve.wait_ge(s_sp.sem, s_sp.at(i, d + 1))
                        dve.tensor_scalar(dt[:, d, :], dt[:, d, :], DT_MIN, DT_MAX, ALU.max, ALU.min)\
                           .then_inc(s_dt.sem, 1)
                    own_s[0] = own

                own_s = [None]

                def read_out(i, s, t):
                    use = f"hT{s * NT + t}"
                    b = take(dve, i, use)
                    if s == 0:
                        if t == 0:
                            used(dve, i, "ct")
                        ins = dve.tensor_scalar(acc[:, t, :], b.t[:, :], ctok[:, t, s:s + 1], None, ALU.mult)
                    else:
                        used(dve, i, f"hT{(s - 1) * NT + t}")
                        ins = dve.scalar_tensor_tensor(out=acc[:, t, :], in0=b.t[:, :], scalar=ctok[:, t, s:s + 1],
                                                       in1=acc[:, t, :], op0=ALU.mult, op1=ALU.add)
                    ins.then_inc(b.free, 1)

                def unit(i, u):
                    s, d = u // DB, u % DB
                    if d == 0 and s >= 1:
                        for n in (u - 2, u - 1):
                            used(dve, i, f"dA{n}")
                        own_s[0].mark(dve.tensor_copy(state[:, s - 1, :], hs[:, (s - 1) % 2, :, CT - 1]))
                    if s < DS:
                        dve.wait_ge(s_bu.sem, s_bu.at(i, u + 1))
                        b = take(dve, i, f"dA{u}")
                        dve.tensor_tensor_scan(hs[:, s % 2, d, :], b.t[:, :], bu[:, u % 4, :],
                                               state[:, s, d:d + 1], ALU.mult, ALU.add).then_inc(b.free, 1)
                    if s >= 1:
                        read_out(i, s - 1, d)

                def tail(i):
                    own = own_s[0]
                    for t in range(NT):
                        used(dve, i, f"gt{t}")
                        used(dve, i, f"hT{(DS - 1) * NT + t}")
                    for t in range(NT):
                        ins = dve.tensor_tensor(acc[:, t, :], acc[:, t, :], gate[:, t, :], ALU.mult)
                    ins.then_inc(s_yg.sem, 1)
                    dve.wait_ge(s_xg.sem, s_xg.at(i, 1))
                    since(dve, d_x2, i)
                    for k in range(2):
                        b = take(dve, i, f"wo{k}")
                        tiles = x1[:, 2 * k:2 * k + 2, :]
                        dve.tensor_tensor(tiles, b.t[:, :].rearrange("p (t c) -> p t c", t=2),
                                          m_s("gA0").unsqueeze(1).to_broadcast([P, 2, C]), ALU.mult)\
                           .then_inc(b.free, 1)
                    for k in range(2):
                        used(dve, i, f"wo{k}")
                    ins = dve.tensor_tensor(x1[:, :, :], x1[:, :, :], xin[:, :, :], ALU.add)
                    ins.then_inc(s_x1.sem, 1)
                    own.end()

                def low(j, k):
                    for c in range(KC):
                        dve.wait_ge(d_fh.sem, d_fh.at(j, KC * k + c + 1))
                        dve.tensor_tensor(fl[:, c, :], ff[:, c, :], fh[:, c, :].bitcast(F32), ALU.subtract)\
                           .then_inc(d_fl.sem, 1)

                def pair(b):
                    return b.t[:, :].rearrange("p (t c) -> p t c", t=2)

                def dense(j, pace):
                    own = Own(dve, o_dve_d, j)
                    step = own.step
                    dve.wait_ge(s_x1.sem, s_x1.at(j, 1))
                    stats(own, x1, st_d, mv_d, d_mv)
                    pace("a_stats")
                    dve.wait_ge(d_rs.sem, d_rs.at(j, 1))
                    apply(hA, x1, mv_d, rs_d, d_n)
                    pace("a_norm")
                    pace("b_turn")
                    low(j, 0)
                    b = take(dve, j, "routerT")
                    dve.tensor_copy(lg[:, :, :], b.t[:, 0:NT * 8].rearrange("p (t e) -> p t e", t=NT))\
                       .then_inc(b.free, 1)
                    used(dve, j, "routerT")
                    step(dve.tensor_reduce(lg_m[:, :], lg[:, :, :], AX, ALU.max))
                    dve.tensor_tensor(lg[:, :, :], lg[:, :, :], lg_m[:, :].unsqueeze(2).to_broadcast([P, NT, E_MOE]),
                                      ALU.subtract).then_inc(d_lsub.sem, 1)
                    pace("b_router")
                    for k in range(8):
                        pace(f"c{k}")
                    dve.wait_ge(d_lexp.sem, d_lexp.at(j, 1))
                    step(dve.tensor_reduce(lg_m[:, :], lg[:, :, :], AX, ALU.add))
                    step(dve.reciprocal(lg_m[:, :], lg_m[:, :]))
                    step(dve.tensor_tensor(prob[:, :], lg_m[:, :], lg[:, :, E_MOE - 1], ALU.mult))
                    dve.wait_ge(s_modd[0].sem, s_modd[0].at(j, 16))
                    since(dve, s_out, j)
                    for p in range(2):
                        b = take(dve, j, f"ffn{p}")
                        dve.tensor_tensor(nn[:, 2 * p:2 * p + 2, :], pair(b),
                                          b2_row[:, :].unsqueeze(1).to_broadcast([P, 2, C]), ALU.add)\
                           .then_inc(b.free, 1)
                    for p in range(2):
                        used(dve, j, f"ffn{p}")
                        for t in (2 * p, 2 * p + 1):
                            own.mark(dve.scalar_tensor_tensor(out=nn[:, t, :], in0=nn[:, t, :], scalar=prob[:, t:t + 1],
                                                              in1=m_d("gB0"), op0=ALU.mult, op1=ALU.mult))
                    own.wait()
                    dve.tensor_tensor(xd[:, :, :], x1[:, :, :], nn[:, :, :], ALU.add).then_inc(d_x2.sem, 1)
                    pace("d_x2")
                    dve.wait_ge(d_x2.sem, d_x2.at(j, 1))
                    stats(own, xd, st_d, mv_d, d_mv)
                    pace("e_stats")
                    dve.wait_ge(d_rs.sem, d_rs.at(j, 2))
                    apply(hA, xd, mv_d, rs_d, d_n)
                    pace("e_norm")
                    pace("f_turn")
                    for t in range(NT):
                        use = f"kq{t}"
                        b = take(dve, j, use)
                        step(dve.tensor_copy(sm[:, t, :], b.t[:, C:NQ]))
                        ins = dve.tensor_tensor(nn[:, t, :].rearrange("p (h d) -> p h d", h=NH),
                                                b.t[:, 0:C].rearrange("p (h d) -> p h d", h=NH),
                                                sm[:, t, NH:2 * NH].unsqueeze(2).to_broadcast([P, NH, HD]), ALU.mult)
                        ins.then_inc(b.free, 1)
                    dve.tensor_tensor(sm[:, :, 2 * NH:3 * NH], sm[:, :, 2 * NH:3 * NH],
                                      bbeta_row[:, :].unsqueeze(1).to_broadcast([P, NT, NH]), ALU.add)\
                       .then_inc(d_sm.sem, 1)
                    own.mark(dve.tensor_tensor(state_l[:, :].bitcast(I32), state_l[:, :].bitcast(I32),
                                               keep[:, bass.ds(j, 1)].to_broadcast([P, KC]), ALU.bitwise_and))
                    pace("f_kv")
                    pace("g_turn")
                    own.wait()
                    for k in range(KC):
                        b = take(dve, j, f"btT{k}")
                        used(dve, j, f"kvT{k}")
                        dve.tensor_tensor_scan(cb[:, k, :], b.t[:, :], ca[:, k, :], state_l[:, k:k + 1],
                                               ALU.mult, ALU.add).then_inc(b.free, 1)
                        used(dve, j, f"btT{k}")
                        step(dve.tensor_copy(state_l[:, k:k + 1], cb[:, k, CT - 1:CT]))
                        b = take(dve, j, f"qsT{k}")
                        dve.tensor_tensor(cb[:, k, :], cb[:, k, :], b.t[:, :], ALU.mult).then_inc(b.free, 1)
                    pace("g_scan")
                    dve.wait_ge(d_hb.sem, d_hb.at(j, 1))
                    for p in range(2):
                        b = take(dve, j, f"ao{p}")
                        dve.tensor_tensor(hA[:, 2 * p:2 * p + 2, :], pair(b), hA[:, 2 * p:2 * p + 2, :], ALU.add)\
                           .then_inc(b.free, 1)
                    pace("h_out")
                    for p in range(2):
                        used(dve, j, f"ao{p}")
                    stats(own, hA, st_d, mv_d, d_mv)
                    pace("h_stats")
                    dve.wait_ge(d_rs.sem, d_rs.at(j, 3))
                    apply(nn, hA, mv_d, rs_d, d_n)
                    pace("h_norm")
                    dve.wait_ge(d_x3.sem, d_x3.at(j, 1))
                    stats(own, xd, st_d, mv_d, d_mv)
                    pace("i_stats")
                    dve.wait_ge(d_rs.sem, d_rs.at(j, 4))
                    apply(hA, xd, mv_d, rs_d, d_n)
                    pace("i_norm")
                    dve.wait_ge(d_h.sem, d_h.at(j, 3))
                    stats(own, hA, st_d, mv_d, d_mv)
                    pace("i_stats2")
                    dve.wait_ge(d_rs.sem, d_rs.at(j, 5))
                    apply(nn, hA, mv_d, rs_d, d_n)
                    pace("i_norm2")
                    pace("j_turn")
                    low(j, 1)
                    pace("k_proj")
                    for k in range(KC):
                        b = take(dve, j, f"v{k}")
                        used(dve, j, f"r{k}")
                        dve.tensor_tensor(cb[:, k, :], cb[:, k, :], b.t[:, :], ALU.mult).then_inc(b.free, 1)
                    pace("l_out")
                    for p in range(2):
                        b = take(dve, j, f"att{p}")
                        dve.tensor_tensor(hA[:, 2 * p:2 * p + 2, :], pair(b), hA[:, 2 * p:2 * p + 2, :], ALU.add)\
                           .then_inc(b.free, 1)
                    for p in range(2):
                        used(dve, j, f"att{p}")
                    stats(own, hA, st_d, mv_d, d_mv)
                    pace("m_stats")
                    dve.wait_ge(d_rs.sem, d_rs.at(j, 6))
                    apply(nn, hA, mv_d, rs_d, d_n)
                    pace("m_norm")
                    pace("m_turn")
                    low(j, 2)
                    pace("n_bids")
                    b = take(dve, j, "bidsT")
                    dve.tensor_copy(bl[:, :, :], b.t[:, 0:NT * 8].rearrange("p (t e) -> p t e", t=NT))\
                       .then_inc(b.free, 1)
                    for k in range(KC):
                        b = take(dve, j, f"tw{k}")
                        used(dve, j, f"sW{k}")
                        dve.tensor_tensor(cb[:, k, :], cb[:, k, :], b.t[:, :], ALU.mult).then_inc(b.free, 1)
                    dve.wait_ge(d_sg.sem, d_sg.at(j, 1))
                    step(dve.tensor_tensor(bid[:, :, :], sg[:, :, 0:3], cs_row[:, :].unsqueeze(1)
                                           .to_broadcast([P, NT, 3]), ALU.mult))
                    step(dve.tensor_tensor(bid[:, :, :], bid[:, :, :], sg[:, :, 3:4].to_broadcast([P, NT, 3]), ALU.mult))
                    step(dve.tensor_tensor(bid[:, :, :], bid[:, :, :], bl[:, :, 4:7], ALU.add))
                    step(dve.tensor_reduce(bmax[:, :], bid[:, :, :], AX, ALU.max))
                    step(dve.tensor_tensor(win[:, :, :], bid[:, :, :], bmax[:, :].unsqueeze(2)
                                           .to_broadcast([P, NT, 3]), ALU.is_equal))
                    step(dve.tensor_tensor(win[:, :, 1], win[:, :, 1], win[:, :, 0], ALU.is_gt))
                    step(dve.tensor_tensor(win[:, :, 2], win[:, :, 2], win[:, :, 0], ALU.is_gt))
                    step(dve.tensor_tensor(win[:, :, 2], win[:, :, 2], win[:, :, 1], ALU.is_gt))
                    step(dve.tensor_tensor(wc[:, :, :], win[:, :, :], sg[:, :, 0:3], ALU.mult))
                    step(dve.tensor_reduce(bmax[:, :], wc[:, :, :], AX, ALU.add))
                    step(dve.tensor_scalar(wcs[:, :], bmax[:, :], 1e-6, None, ALU.add))
                    step(dve.reciprocal(wcs[:, :], wcs[:, :]))
                    step(dve.tensor_tensor(wcs[:, :], wcs[:, :], bmax[:, :], ALU.mult))
                    step(dve.tensor_tensor(coef[:, :, :], win[:, :, :], wcs[:, :].unsqueeze(2)
                                           .to_broadcast([P, NT, 3]), ALU.mult))
                    pace("n_trans")
                    def add_expert(uses, e):
                        for t in range(NT):
                            b = bank_of[uses[t // 2]]
                            if t % 2 == 0:
                                take(dve, j, uses[t // 2])
                            ins = dve.scalar_tensor_tensor(out=hA[:, t, :], in0=b.t[:, t % 2 * C:(t % 2 + 1) * C],
                                                           scalar=coef[:, t, e:e + 1], in1=hA[:, t, :],
                                                           op0=ALU.mult, op1=ALU.add)
                            if t % 2:
                                ins.then_inc(b.free, 1)
                        for use in uses:
                            used(dve, j, use)

                    add_expert(["tr0", "tr1"], 2)
                    for e in range(2):
                        for k in range(NHB):
                            use = f"{'op'[e]}{k}"
                            b = bank_of[use]
                            dve.wait_ge(d_rl.sem, d_rl.at(j, NHB * e + k + 1))
                            dve.tensor_tensor(hid[:, k % HB, :], hid[:, k % HB, :], b.t[:, :], ALU.mult)\
                               .then_inc(b.free, 1)
                            pace(use)
                        add_expert([f"e{e}_0", f"e{e}_1"], e)
                        pace("o_out" if e == 0 else "p7")
                    step(dve.tensor_tensor(hA[:, :, :], hA[:, :, :], per_tile(m_d("gB1")), ALU.mult))
                    dve.tensor_tensor(xd[:, :, :], xd[:, :, :], hA[:, :, :], ALU.add).then_inc(d_x5.sem, 1)
                    pace("q_out")
                    own.end()

                front(0)
                Pace(unit, 0).upto(SSM_UNITS)
                tail(0)
                with dve.Fori(1, NCH) as i:
                    front(i)
                    dense(i - 1, Pace(unit, i))
                    tail(i)
                dense(NCH - 1, Pace(None, 0))

            @block.tensor
            def _(pe):
                def turn(dst, src):
                    return pe.transpose(dst, src, ident[:, :])

                def split3(dst, lh, ll, rh, rl):
                    prods = [(a, b) for k in range(len(lh)) for a, b in ((lh[k], rh[k]), (lh[k], rl[k]), (ll[k], rh[k]))]
                    for n, (a, b) in enumerate(prods):
                        last = pe.matmul(dst, a, b, start=n == 0, stop=n == len(prods) - 1)
                    return last

                def front(i):
                    pe.wait_ge(s_n.sem, s_n.at(i, 2))
                    for k in range(KC):
                        b = fill(pe, i, f"xn{k}")
                        for t in range(NT):
                            last = turn(b.t[:, t * P:(t + 1) * P], n0[:, t, k * P:(k + 1) * P])
                        last.then_inc(b.full, 1)
                    pe.wait_ge(s_xnl.sem, s_xnl.at(i, KC))
                    for d in range(DB):
                        b = fill(pe, i, f"z{d}")
                        split3(b.t[:, :], [w_in["h"][:, k, d * P:(d + 1) * P] for k in range(KC)],
                               [w_in["l"][:, k, d * P:(d + 1) * P] for k in range(KC)],
                               [xnh[:, k, :] for k in range(KC)], [xnl[:, k, :] for k in range(KC)])\
                            .then_inc(b.full, 1)
                    for t in range(NT):
                        b = fill(pe, i, f"gt{t}")
                        tok = slice(t * P, (t + 1) * P)
                        split3(b.t[:, :], [xnh[:, k, tok] for k in range(KC)], [xnl[:, k, tok] for k in range(KC)],
                               [w_in["h"][:, k, DI:2 * DI] for k in range(KC)],
                               [w_in["l"][:, k, DI:2 * DI] for k in range(KC)]).then_inc(b.full, 1)
                    used(pe, i, "z3")
                    b = fill(pe, i, "bc")
                    for k in range(DB):
                        last = pe.matmul(b.t[0:2 * DS, :], w_bc[:, k, :], z[:, k, :], start=k == 0, stop=k == DB - 1)
                    last.then_inc(b.full, 1)
                    pe.wait_ge(s_zl.sem, s_zl.at(i, DB))
                    bct = fill(pe, i, "ct")
                    used(pe, i, "bc")
                    for d in range(DB):
                        b = fill(pe, i, f"dt{d}")
                        split3(b.t[:, :], [w_dt["h"][:, k, d * P:(d + 1) * P] for k in range(DB)],
                               [w_dt["l"][:, k, d * P:(d + 1) * P] for k in range(DB)],
                               [zh[:, k, :] for k in range(DB)], [zl[:, k, :] for k in range(DB)])\
                            .then_inc(b.full, 1)
                        if d == 0:
                            for t in range(NT):
                                last = pe.transpose(bct.t[:, t * 2 * DS:(t + 1) * 2 * DS],
                                                    bcs[:, t * P:(t + 1) * P], ident[0:2 * DS, 0:2 * DS])
                            last.then_inc(bct.full, 1)

                def unit(i, u):
                    s, t = u // DB - 1, u % DB
                    if s < 0:
                        return
                    use = f"hT{s * NT + t}"
                    b = fill(pe, i, use)
                    if t == 0:
                        for n in (s * DB + DB - 2, s * DB + DB - 1):
                            used(pe, i, f"dA{n}")
                    for d in range(DB):
                        last = turn(b.t[:, d * P:(d + 1) * P], hs[:, s % 2, d, t * P:(t + 1) * P])
                    last.then_inc(b.full, 1)

                def tail(i):
                    pe.wait_ge(s_yg.sem, s_yg.at(i, 1))
                    for k in range(DB):
                        b = fill(pe, i, f"y{k}")
                        for t in range(NT):
                            last = turn(b.t[:, t * P:(t + 1) * P], acc[:, t, k * P:(k + 1) * P])
                        last.then_inc(b.full, 1)
                    used(pe, i, "y3")
                    by_token(i, ["wo0", "wo1"], z, w_out, DB)

                def by_token(j, uses, act, wt, kb):
                    for p in range(2):
                        b = fill(pe, j, uses[p])
                        for t in (2 * p, 2 * p + 1):
                            for k in range(kb):
                                last = pe.matmul(b.t[:, t % 2 * C:(t % 2 + 1) * C], act[:, k, t * P:(t + 1) * P],
                                                 wt[:, k, :], start=k == 0, stop=k == kb - 1)
                        last.then_inc(b.full, 1)

                def turns(j, uses, src):
                    for k in range(KC):
                        b = fill(pe, j, uses[k])
                        for t in range(NT):
                            last = turn(b.t[:, t * P:(t + 1) * P], src[:, t, k * P:(k + 1) * P])
                        last.then_inc(b.full, 1)

                def parts(j, k):
                    pe.wait_ge(d_fl.sem, d_fl.at(j, KC * (k + 1)))

                def from_f(j, use, wh, wl, lo, hi):
                    b = fill(pe, j, use)
                    return b, split3(b.t[:, :], [wh[:, k, lo:hi] for k in range(KC)], [wl[:, k, lo:hi] for k in range(KC)],
                                     [fh[:, k, :] for k in range(KC)], [fl[:, k, :] for k in range(KC)])

                def logits_ready(j, use, use_t):
                    fill(pe, j, use_t)
                    used(pe, j, use)

                def logits_by_token(use_t):
                    b = bank_of[use_t]
                    for t in range(NT):
                        last = pe.transpose(b.t[:, t * 8:(t + 1) * 8], rows8[:, t * P:(t + 1) * P], ident[0:8, 0:8])
                    last.then_inc(b.full, 1)

                def hidden(j, name, slots, outs, pace):
                    def up(k):
                        if k % HB == 0:
                            slot_ready(pe, j, slots[k // HB])
                        wt = ws_in[SLOTS.index(slots[k // HB]) % 2]
                        c = k % HB
                        b, last = from_f(j, f"{name}{k}", wt[:, 0], wt[:, 1], c * P, (c + 1) * P)
                        last.then_inc(b.full, 1)

                    def down(k):
                        used(pe, j, f"{name}{k}")
                        wt = ws_out[SLOTS.index(slots[k // HB]) % 2]
                        for t in range(NT):
                            b = bank_of[outs[t // 2]]
                            if k == 0 and t % 2 == 0:
                                fill(pe, j, outs[t // 2])
                            last = pe.matmul(b.t[:, t % 2 * C:(t % 2 + 1) * C], hid[:, k % HB, t * P:(t + 1) * P],
                                             wt[:, k % HB, :], start=k == 0 and t % 2 == 0,
                                             stop=k == NHB - 1, skip_group_check=True)
                            if k == NHB - 1 and t % 2:
                                last.then_inc(b.full, 1)
                        if k < NHB - 1:
                            last.then_inc(d_hfree.sem, 1)

                    up(0)
                    if name == "c":
                        logits_by_token("routerT")
                    for k in range(NHB):
                        if k < NHB - 1:
                            up(k + 1)
                        down(k)
                        pace(f"{name}{k}")

                def dense(j, pace):
                    pace("a_norm")
                    pe.wait_ge(d_h.sem, d_h.at(j, 1))
                    turns(j, ["h1T0", "h1T1"], hA)
                    pace("b_turn")
                    parts(j, 0)
                    b, last = from_f(j, "router", w_rt["h"], w_rt["l"], 0, P)
                    last.then_inc(b.full, 1)
                    logits_ready(j, "router", "routerT")
                    pace("b_router")
                    hidden(j, "c", ["ffn_0", "ffn_1"], ["ffn0", "ffn1"], pace)
                    pace("e_norm")
                    pe.wait_ge(d_h.sem, d_h.at(j, 2))
                    turns(j, ["h2T0", "h2T1"], hA)
                    pace("f_turn")
                    used(pe, j, "h2T1")
                    for t in range(NT):
                        b = fill(pe, j, f"kq{t}")
                        for k in range(KC):
                            last = pe.matmul(b.t[:, 0:NQ], ff[:, k, t * P:(t + 1) * P], w_kq[:, k, :],
                                             start=k == 0, stop=k == KC - 1)
                        last.then_inc(b.full, 1)
                    pace("f_kv")
                    used(pe, j, "kq2")
                    used(pe, j, "kq3")
                    turns(j, ["kvT0", "kvT1"], nn)
                    pe.wait_ge(d_bx.sem, d_bx.at(j, 2))
                    turns(j, ["btT0", "btT1"], bx)
                    turns(j, ["qsT0", "qsT1"], qx)
                    pace("g_turn")
                    pace("g_scan")
                    used(pe, j, "qsT1")
                    by_token(j, ["ao0", "ao1"], cb, w_ao, KC)
                    pace("i_norm2")
                    pe.wait_ge(d_n.sem, d_n.at(j, 5))
                    turns(j, ["xlT0", "xlT1"], nn)
                    pace("j_turn")
                    parts(j, 1)
                    slot_ready(pe, j, "rv")
                    rv, sw = ws_in[SLOTS.index("rv") % 2], ws_in[SLOTS.index("sw") % 2]
                    for k in range(KC):
                        b, last = from_f(j, f"r{k}", rv[:, 0], rv[:, 1], k * P, (k + 1) * P)
                        last.then_inc(b.full, 1)
                        b, last = from_f(j, f"v{k}", rv[:, 0], rv[:, 1], C + k * P, C + (k + 1) * P)
                        last.then_inc(b.full, 1)
                    slot_ready(pe, j, "sw")
                    for k in range(KC):
                        b, last = from_f(j, f"s{k}", sw[:, 0], sw[:, 1], k * P, (k + 1) * P)
                        last.then_inc(b.full, 1)
                    pace("k_proj")
                    used(pe, j, "v0")
                    used(pe, j, "v1")
                    by_token(j, ["att0", "att1"], cb, w_fo, KC)
                    used(pe, j, "s1")
                    for m in range(KC):
                        b = fill(pe, j, f"sW{m}")
                        for k in range(KC):
                            last = pe.matmul(b.t[:, :], w_2[:, k, m * P:(m + 1) * P], ca[:, k, :],
                                             start=k == 0, stop=k == KC - 1)
                        last.then_inc(b.full, 1)
                    pace("l_out")
                    pace("m_norm")
                    pe.wait_ge(d_n.sem, d_n.at(j, 6))
                    turns(j, ["hhT0", "hhT1"], nn)
                    pace("m_turn")
                    parts(j, 2)
                    b, last = from_f(j, "bids", w_bd["h"], w_bd["l"], 0, P)
                    last.then_inc(b.full, 1)
                    logits_ready(j, "bids", "bidsT")
                    for k in range(KC):
                        b, last = from_f(j, f"tw{k}", sw[:, 0], sw[:, 1], C + k * P, C + (k + 1) * P)
                        last.then_inc(b.full, 1)
                        if k == 0:
                            logits_by_token("bidsT")
                    pace("n_bids")
                    used(pe, j, "tw1")
                    by_token(j, ["tr0", "tr1"], cb, w_3, KC)
                    pace("n_trans")
                    hidden(j, "o", ["e0_0", "e0_1"], ["e0_0", "e0_1"], pace)
                    pace("o_out")
                    hidden(j, "p", ["e1_0", "e1_1"], ["e1_0", "e1_1"], pace)
                    pace("q_out")

                front(0)
                Pace(unit, 0).upto(SSM_UNITS)
                tail(0)
                with pe.Fori(1, NCH) as i:
                    front(i)
                    dense(i - 1, Pace(unit, i))
                    tail(i)
                dense(NCH - 1, Pace(None, 0))


OWN = {"dve_s": 25, "dve_d": 54, "pool_s": 4, "pool_d": 10, "act_s": 4}


def kernel(**inputs):
    import numpy as _np
    import concourse.bacc as _bacc
    from concourse import mybir as _mybir
    from concourse.bass_utils import run_bass_kernel_spmd as _run

    nc = _bacc.Bacc("TRN2", target_bir_lowering=False, num_devices=1)
    unused = {"L1_ffn_v_first"}
    arrays, args = {}, {}
    for name in inputs:
        if name in unused:
            continue
        a = _np.ascontiguousarray(inputs[name])
        arrays[f"in_{name}"] = a
        args[name] = nc.dram_tensor(f"in_{name}", a.shape, _mybir.dt.from_np(a.dtype), kind="ExternalInput").ap()
    out = nc.dram_tensor("out_0", (B, T, C), F32, kind="ExternalOutput").ap()
    build(nc, args, out)
    r = _run(nc, [arrays], core_ids=[0])
    return r.results[0]["out_0"]
```

```python
from contextlib import ExitStack

import concourse.bass as bass
from concourse import mybir

F32 = mybir.dt.float32
F32R = mybir.dt.float32r
I32 = mybir.dt.int32
ALU = mybir.AluOpType
ACT = mybir.ActivationFunctionType
AX = mybir.AxisListType.X

P = 128
B, T, C = 4, 2048, 256
CT = 512
NT = CT // P
NCH = B * T // CT
CPB = T // CT
KC = C // P
DI, DS = 512, 16
DB = DI // P
F = 1024
NH, HD = 16, 16
E_MOE = 8
EPS = 1e-5
DT_MIN, DT_MAX = 0.001, 1.0
DT_CLAMP = 20.0
GATE_MIN = 0.25
NQ = C + 3 * NH

ROWS = ["cA0", "sA0", "gA0", "cB0", "sB0", "gB0", "cA1", "sA1", "gA1w", "gA1b", "cB1", "sB1", "gB1"]
ROW = {name: k for k, name in enumerate(ROWS)}
NROW_S = 3
NROW_D = len(ROWS) - NROW_S

SLOTS = ["ffn_0", "ffn_1", "rv", "sw", "e0_0", "e0_1", "e1_0", "e1_1"]
NSLOT = len(SLOTS)
CREDIT = 1
HB = F // 2 // P
NHB = F // P

SSM_UNITS = DS * DB + DB
FRONT_STEPS = [("mean", 0), ("norm", 0), ("mean", 1), ("norm", 1), ("turn", 0)] + [("z", d) for d in range(DB)] \
    + [("gate", 0), ("gate", 1), ("bc", 0), ("gate", 2), ("gate", 3)] + [("dt", d) for d in range(DB)] \
    + [("softplus", 0)] + [("clip", d) for d in range(DB)]
TAIL_STEPS = [("gated", 0)] + [("y", k) for k in range(DB)] + [("out", 0), ("out", 1), ("x1", 0)]
S_STEPS = [("front",) + step for step in FRONT_STEPS] + [("unit", u) for u in range(SSM_UNITS)] \
    + [("tail",) + step for step in TAIL_STEPS]

PACE = {
    "sp": {
        "load_ffn_1": 37, "c3": 53, "c7": 54, "k_proj": 61, "n_trans": 86, "o3": 88, "o7": 89, "p3": 98,
        "q_out": 99,
    },
    "pool": {
        "a_stats": 0, "rstd0": 0, "scaled0": 0, "b_turn": 11, "e_stats": 34, "rstd1": 35, "scaled1": 36,
        "h2": 41, "f_kv": 41, "h_stats": 46, "rstd2": 47, "att_scaled": 47, "i_stats": 49, "rstd3": 50,
        "scaled2": 50, "i_stats2": 51, "rstd4": 56, "j_turn": 62, "m_stats": 65, "rstd5": 97, "m_turn": 99,
        "q_out": 99,
    },
    "act": {
        "b_turn": 0, "h1T0": 0, "h1T1": 1, "h1T0_high": 1, "h1T1_high": 1, "router": 1, "b_router": 4,
        "c0": 4, "c1": 13, "c2": 13, "c3": 22, "c4": 23, "c5": 25, "c6": 30, "c7": 38, "f_turn": 38,
        "h2T0": 38, "h2T1": 40, "f_kv": 40, "beta": 40, "q": 40, "kvT0": 40, "kvT1": 50, "j_turn": 53,
        "xlT0": 53, "xlT1": 53, "xlT0_high": 53, "xlT1_high": 58, "r0": 58, "r1": 63, "s0": 63, "s1": 63,
        "sW0": 63, "sW1": 63, "hhT0": 63, "hhT1": 63, "hhT0_high": 63, "hhT1_high": 66, "bids": 69, "o0": 71,
        "o1": 72, "o2": 74, "o3": 77, "o4": 81, "o5": 83, "o6": 84, "o7": 87, "p0": 87, "p1": 88, "p2": 91,
        "p3": 91, "p4": 91, "p5": 91, "p6": 93, "p7": 99, "q_out": 99,
    },
    "dve": {
        "a_stats": 0, "a_norm": 0, "b_turn": 2, "low0_0": 2, "low0_1": 3, "b_router": 29, "prob": 30,
        "ffn0": 30, "ffn1": 30, "ffn_scaled": 30, "d_x2": 30, "e_stats": 31, "e_norm": 32, "f_turn": 38,
        "kq0": 38, "kq1": 38, "kq2": 38, "kq3": 38, "f_kv": 38, "g_turn": 40, "qsT0": 40, "scan0": 40,
        "qsT1": 42, "g_scan": 42, "ao0": 42, "ao1": 42, "h_out": 42, "h_stats": 43, "h_norm": 46,
        "i_stats": 47, "i_norm": 50, "i_stats2": 51, "i_norm2": 53, "j_turn": 53, "low1_0": 53, "low1_1": 53,
        "k_proj": 57, "v0": 58, "v1": 61, "l_out": 61, "att0": 61, "att1": 61, "m_stats": 62, "m_norm": 62,
        "m_turn": 63, "low2_0": 63, "low2_1": 66, "n_bids": 66, "tw0": 66, "tw1": 68, "product": 68,
        "n_trans": 68, "o0": 70, "o1": 71, "o2": 75, "o3": 77, "o4": 80, "o5": 82, "o6": 83, "o7": 85,
        "o_out": 86, "p0": 88, "p1": 91, "p2": 91, "p3": 95, "p4": 95, "p5": 95, "p6": 95, "p7": 96,
        "scaled": 96, "q_out": 99,
    },
    "pe": {
        "a_norm": 0, "h1T0": 1, "h1T1": 1, "b_router": 1, "c0_up": 3, "c1_up": 4, "c0": 5, "c2_up": 5,
        "c1": 12, "c3_up": 18, "c2": 26, "c4_up": 26, "c3": 26, "c5_up": 26, "c4": 26, "c6_up": 27, "c5": 27,
        "c7_up": 27, "c6": 30, "c7": 36, "e_norm": 37, "h2T0": 37, "h2T1": 38, "kq0": 38, "kq1": 38,
        "kq2": 38, "kq3": 38, "f_kv": 39, "kvT0": 40, "kvT1": 41, "btT0": 41, "btT1": 41, "qsT0": 41,
        "qsT1": 41, "g_scan": 42, "ao0": 42, "ao1": 53, "i_norm2": 53, "xlT0": 53, "xlT1": 55, "r0": 55,
        "v0": 56, "r1": 58, "v1": 59, "s0": 59, "s1": 61, "att0": 61, "att1": 62, "sW0": 62, "sW1": 62,
        "m_norm": 62, "hhT0": 62, "hhT1": 65, "bids": 66, "tw0": 66, "tw1": 67, "tr0": 68, "tr1": 70,
        "o0_up": 70, "o1_up": 70, "o0": 71, "o2_up": 71, "o1": 73, "o3_up": 74, "o2": 75, "o4_up": 77,
        "o3": 77, "o5_up": 79, "o4": 81, "o6_up": 82, "o5": 82, "o7_up": 84, "o6": 85, "o7": 86, "o_out": 86,
        "p0_up": 87, "p1_up": 87, "p0": 89, "p2_up": 91, "p1": 92, "p3_up": 92, "p2": 92, "p4_up": 92,
        "p3": 95, "p5_up": 96, "p4": 96, "p6_up": 96, "p5": 96, "p7_up": 96, "p6": 96, "p7": 97, "q_out": 99,
    },
}

FRONT = ["xn0", "xn1", "z0", "z1", "z2", "z3", "gt0", "gt1", "bc", "gt2", "ct", "gt3", "dt0", "dt1", "dt2", "dt3"]
TAIL = ["y0", "y1", "y2", "y3", "wo0", "wo1"]
SCAN_BANKS = ["A0", "A1", "H0", "H1"]
BANK_USES = {
    "A0": FRONT[0::4] + [f"dA{u}" for u in range(0, DS * DB, 2)] + TAIL[0::4],
    "A1": FRONT[1::4] + [f"dA{u}" for u in range(1, DS * DB, 2)] + TAIL[1::4],
    "H0": FRONT[2::4] + [f"hT{u}" for u in range(0, DS * NT, 2)] + TAIL[2::4],
    "H1": FRONT[3::4] + [f"hT{u}" for u in range(1, DS * NT, 2)] + TAIL[3::4],
    "B0": ["h1T0"] + [f"c{k}" for k in (0, 2, 4, 6)] + ["h2T0", "kvT0", "qsT0", "xlT0", "r0", "s0", "sW0", "hhT0", "tw0"]
          + [f"o{k}" for k in (0, 2, 4, 6)] + [f"p{k}" for k in (0, 2, 4, 6)],
    "B1": ["h1T1"] + [f"c{k}" for k in (1, 3, 5, 7)] + ["h2T1", "kvT1", "qsT1", "xlT1", "r1", "s1", "sW1", "hhT1", "tw1"]
          + [f"o{k}" for k in (1, 3, 5, 7)] + [f"p{k}" for k in (1, 3, 5, 7)],
    "B2": ["router", "ffn0", "kq0", "kq2", "btT0", "ao0", "v0", "att0", "bids", "tr0", "e0_0", "e1_0"],
    "B3": ["routerT", "ffn1", "kq1", "kq3", "btT1", "ao1", "v1", "att1", "bidsT", "tr1", "e0_1", "e1_1"],
}


class Bank:

    def __init__(self, tensor, full, free, uses):
        self.t, self.full, self.free, self.uses = tensor, full, free, uses

    def fills_before(self, chunk, use):
        return chunk * len(self.uses) + self.uses.index(use) + CREDIT

    def fills_with(self, chunk, use):
        return self.fills_before(chunk, use) + 1


class Signal:

    def __init__(self, sem, n, credit=0):
        self.sem, self.n, self.credit = sem, n, credit

    def at(self, chunk, k):
        return chunk * self.n + k + self.credit


class Own:

    def __init__(self, eng, sig, chunk):
        self.eng, self.sig, self.chunk, self.k = eng, sig, chunk, 0

    def mark(self, instruction):
        self.k += 1
        instruction.then_inc(self.sig.sem, 1)
        return self.k

    def wait(self, k=None):
        self.eng.wait_ge(self.sig.sem, self.sig.at(self.chunk, self.k if k is None else k))

    def step(self, instruction):
        self.mark(instruction)
        self.wait()

    def end(self):
        assert self.k == self.sig.n, f"{self.k} own steps, {self.sig.n} stated"


class Pace:

    def __init__(self, pace, front, unit, tail, chunk):
        self.pace, self.front, self.unit, self.tail, self.chunk, self.at = pace, front, unit, tail, chunk, 0

    def __call__(self, name):
        self.upto(self.pace[name])

    def upto(self, n):
        while self.front is not None and self.at < n:
            part, *step = S_STEPS[self.at]
            {"front": self.front, "unit": self.unit, "tail": self.tail}[part](self.chunk, *step)
            self.at += 1


def since(eng, sig, chunk, k=0):
    if not (isinstance(chunk, int) and chunk == 0 and k == 0):
        eng.wait_ge(sig.sem, sig.at(chunk, k))


def build(nc, w, out):
    ctx = ExitStack()
    with ctx:
        ctx.enter_context(nc.allow_non_contiguous_dma("small constants, column by column"))
        place = [(nc.sbuf_base + 63) // 64 * 64]

        def sb(name, shape, dt=F32):
            size = 4
            for n in shape[1:]:
                size *= n
            t = nc.alloc_sbuf_tensor_at(name, list(shape), dt, offset=place[0])
            where[name] = place[0]
            place[0] += (size + 31) // 32 * 32
            return t

        def over(name, shape, at, dt=F32):
            return nc.alloc_sbuf_tensor_at(name, list(shape), dt, offset=where[at])

        where = {}

        def sem(name):
            return ctx.enter_context(nc.semaphore(name))

        credited = []

        def signal(name, n, credit=0):
            sig = Signal(sem(name), n, credit)
            if credit:
                credited.append(sig.sem)
            return sig

        w_in = {h: sb(f"w_in_{h}", [P, KC, 2 * DI], F32R) for h in "hl"}
        w_dt = {h: sb(f"w_dt_{h}", [P, DB, DI], F32R) for h in "hl"}
        w_bc = sb("w_bc", [P, DB, 2 * DS])
        w_out = sb("w_out", [P, DB, C])
        w_kq = sb("w_kq", [P, KC, NQ])
        w_ao = sb("w_ao", [P, KC, C])
        w_fo = sb("w_fo", [P, KC, C])
        w_2 = sb("w_2", [P, KC, C])
        w_3 = sb("w_3", [P, KC, C])
        w_rt = {h: sb(f"w_rt_{h}", [P, KC, P], F32R) for h in "hl"}
        w_bd = {h: sb(f"w_bd_{h}", [P, KC, P], F32R) for h in "hl"}
        ws_in = [sb(f"ws_in{k}", [P, 2, KC, HB * P], F32R) for k in range(2)]
        ws_out = [sb(f"ws_out{k}", [P, HB, C]) for k in range(2)]
        xnh = sb("xnh", [P, KC, CT], F32R)
        xnl = sb("xnl", [P, KC, CT], F32R)
        xnf = over("xnf", [P, KC, CT], "xnl")
        bu = over("bu", [P, 4, CT], "xnh")
        zh = sb("zh", [P, DB, CT], F32R)
        zl = sb("zl", [P, DB, CT], F32R)
        hs = over("hs", [P, 2, DB, CT], "zh")
        stage = [over("stage0", [P, 2048], "zh"), over("stage1", [P, 2048], "zl")]
        z = sb("z", [P, DB, CT])
        dt = sb("dt", [P, DB, CT])
        modrow = over("modrow", [B, len(ROWS) * C], "z")
        gate = sb("gate", [P, NT, DI])
        acc = sb("acc", [P, NT, DI])
        wm = over("wm", [P, KC, 6 * C], "gate")
        h0 = over("h0", [P, NT, C], "acc")
        where["acc_hi"] = where["acc"] + 4 * NT * C
        n0 = over("n0", [P, NT, C], "acc_hi")
        bb = sb("bb", [P, 4, CT])
        modraw = over("modraw", [B, 6 * C], "bb")
        fh = sb("fh", [P, KC, CT], F32R)
        fl = sb("fl", [P, KC, CT], F32R)
        ff = over("ff", [P, KC, CT], "fl")
        bx = over("bx", [P, NT, C], "fh")
        ca = sb("ca", [P, KC, CT])
        cb = sb("cb", [P, KC, CT])
        hid = sb("hid", [P, HB, CT])
        qx = over("qx", [P, NT, C], "hid")
        xin = sb("xin", [P, NT, C])
        x1 = sb("x1", [P, NT, C])
        hA = sb("hA", [P, NT, C])
        nn = sb("nn", [P, NT, C])
        xd = sb("xd", [P, NT, C])
        mod_s = sb("mod_s", [P, NROW_S, C])
        mod_d = sb("mod_d", [P, NROW_D, C])
        b2_row = sb("b2_row", [P, C])
        bo_row = sb("bo_row", [P, C])
        ident = sb("ident", [P, P])
        rows8 = sb("rows8", [8, CT])
        bcs = sb("bcs", [2 * DS, CT])
        ctok = sb("ctok", [P, NT, 2 * DS])
        a_neg = sb("a_neg", [P, DB, DS])
        state = sb("state", [P, DS, DB])
        state_l = sb("state_l", [P, KC])
        keep = sb("keep", [P, NCH], I32)
        mhalf = sb("mhalf", [P, NT])
        cols = sb("cols", [P, 16])
        bdt_col = sb("bdt_col", [P, DB])
        b1_col = sb("b1_col", [P, F // P])
        bbeta_row = sb("bbeta_row", [P, NH])
        cs_row = sb("cs_row", [P, 3])
        c_in = over("c_in", [B, 2 * C], "xd")
        c_t = sb("c_t", [P, 2, KC, B])
        lnw_row = over("lnw_row", [B, 2 * C], "nn")
        st_s, mv_s, rs_s = sb("st_s", [P, NT, 6]), sb("mv_s", [P, NT, 2]), sb("rs_s", [P, NT])
        st_d, mv_d, rs_d = sb("st_d", [P, NT, 6]), sb("mv_d", [P, NT, 2]), sb("rs_d", [P, NT])
        carrier = sb("carrier", [P, 2])
        eps_t = sb("eps_t", [P, NT])
        lg = sb("lg", [P, NT, E_MOE])
        lg_m = sb("lg_m", [P, NT])
        prob = sb("prob", [P, NT])
        sm = sb("sm", [P, NT, 3 * NH])
        bl = sb("bl", [P, NT, 8])
        sg = sb("sg", [P, NT, 4])
        bid = sb("bid", [P, NT, 3])
        bmax = sb("bmax", [P, NT])
        win = sb("win", [P, NT, 3])
        wc = sb("wc", [P, NT, 3])
        wcs = sb("wcs", [P, NT])
        coef = sb("coef", [P, NT, 3])
        assert place[0] <= nc.sbuf_usable_end, place[0]

        w_split = nc.dram_tensor("w_split", (NSLOT, P, 2 * KC * HB * P), F32, kind="Internal").ap()
        mods = nc.dram_tensor("mods", (NCH, len(ROWS) * C), F32, kind="Internal").ap()
        b_rows = nc.dram_tensor("b_rows", (DS, CT), F32, kind="Internal").ap()

        psum = {name: ctx.enter_context(nc.psum_tensor(f"ps_{name}", [P, CT], F32)) for name in BANK_USES}
        bank = {name: Bank(psum[name], sem(f"full_{name}"), sem(f"free_{name}"), uses)
                for name, uses in BANK_USES.items()}
        bank_of = {use: bank[name] for name in BANK_USES for use in BANK_USES[name]}

        def fill(eng, chunk, use):
            b = bank_of[use]
            n = b.fills_before(chunk, use)
            if not (isinstance(n, int) and n == CREDIT):
                eng.wait_ge(b.free, n)
            return b

        def take(eng, chunk, use):
            b = bank_of[use]
            eng.wait_ge(b.full, b.fills_with(chunk, use))
            return b

        def used(eng, chunk, use):
            b = bank_of[use]
            eng.wait_ge(b.free, b.fills_with(chunk, use))

        def kp(ap):
            return ap.rearrange("(k p) m -> p k m", p=P)

        def col(ap):
            return ap.rearrange("(k p) -> p k", p=P)

        def row(ap):
            return ap.rearrange("(a n) -> a n", a=1)

        s_xin = signal("s_xin", 16)
        s_mods = signal("s_mods", 16)
        s_modd = [signal(f"s_modd{k}", 16) for k in range(3)]
        s_bw = signal("s_bw", 16)
        s_bb = [signal(f"s_bb{k}", 16 * DS // 4) for k in range(4)]
        s_w = [signal(f"s_w{k}", 0) for k in range(2)]
        s_out = signal("s_out", 16, CREDIT)
        s_mv = signal("s_mv", 2)
        s_rs = signal("s_rs", 2)
        s_n = signal("s_n", 2)
        s_h0 = signal("s_h0", 1)
        s_xg = signal("s_xg", 1)
        s_xnh = signal("s_xnh", KC)
        s_xnl = signal("s_xnl", KC)
        s_zh = signal("s_zh", DB)
        s_zl = signal("s_zl", DB)
        s_sp = signal("s_sp", DB)
        s_dt = signal("s_dt", DB)
        s_u = signal("s_u", DB)
        s_bu = signal("s_bu", DS * DB)
        s_yg = signal("s_yg", 1)
        s_x1 = signal("s_x1", 1, CREDIT)
        d_mv = signal("d_mv", 6)
        d_rs = signal("d_rs", 6)
        d_n = signal("d_n", 6)
        d_h = signal("d_h", 3)
        d_fh = signal("d_fh", 3 * KC)
        d_fl = signal("d_fl", 3 * KC)
        d_lsub = signal("d_lsub", 1)
        d_lexp = signal("d_lexp", 1)
        d_rl = signal("d_rl", 16)
        d_hfree = signal("d_hfree", 3 * (NHB - 1), CREDIT)
        d_x2 = signal("d_x2", 1, CREDIT)
        d_sm = signal("d_sm", 1)
        d_bx = signal("d_bx", 2)
        d_hb = signal("d_hb", 1)
        d_y2 = signal("d_y2", 1)
        d_xb = signal("d_xb", 1)
        d_x3 = signal("d_x3", 1, CREDIT)
        d_sg = signal("d_sg", 1)
        d_x5 = signal("d_x5", 1, CREDIT)
        o_dve_s = signal("o_dve_s", OWN["dve_s"])
        o_dve_d = signal("o_dve_d", OWN["dve_d"])
        o_pool_s = signal("o_pool_s", OWN["pool_s"])
        o_pool_d = signal("o_pool_d", OWN["pool_d"])
        o_act_s = signal("o_act_s", OWN["act_s"])

        u_load = sem("u_load")
        u_stage = [sem("u_stage0"), sem("u_stage1")]
        u_wm = sem("u_wm")
        u_split = sem("u_split")
        u_store = [sem("u_store0"), sem("u_store1")]
        u_dve = sem("u_dve")
        u_id = sem("u_id")
        u_silu = sem("u_silu")
        u_exp = sem("u_exp")
        u_ct = sem("u_ct")
        u_ctc = sem("u_ctc")
        u_mm = sem("u_mm")
        u_raw = sem("u_raw")
        u_rows = sem("u_rows")
        u_sum = sem("u_sum")
        u_zero = sem("u_zero")
        u_mods = sem("u_mods")
        u_wsm = sem("u_wsm")

        e_last = E_MOE - 1
        k_r, v_r = w["L1_ffn_K_rwkv"], w["L1_ffn_V_rwkv"]
        pieces = [
            [(0, DI, kp(w["L0_attn_W_in"])), (DI, DI, kp(w["L0_attn_W_gate"]))],
            [(0, DI, kp(w["L0_attn_W_dt"]))],
            [(0, HB * P, kp(w["L0_ffn_W1"][e_last])[:, :, 0:HB * P])],
            [(0, HB * P, kp(w["L0_ffn_W1"][e_last])[:, :, HB * P:F])],
            [(0, C, kp(w["L1_ffn_Wr"])), (C, C, kp(w["L1_ffn_Wv"]))],
            [(0, C, kp(w["L1_ffn_Ws"])), (C, C, kp(w["L1_ffn_W1"]))],
            [(0, HB * P, kp(k_r[0])[:, :, 0:HB * P])],
            [(0, HB * P, kp(k_r[0])[:, :, HB * P:F])],
            [(0, HB * P, kp(k_r[1])[:, :, 0:HB * P])],
            [(0, HB * P, kp(k_r[1])[:, :, HB * P:F])],
        ]
        shapes = [(KC, 2 * DI), (DB, DI)] + [(KC, HB * P)] * NSLOT
        w_down = {"ffn_0": w["L0_ffn_W2"][e_last][0:HB * P], "ffn_1": w["L0_ffn_W2"][e_last][HB * P:F],
                  "e0_0": v_r[0][0:HB * P], "e0_1": v_r[0][HB * P:F],
                  "e1_0": v_r[1][0:HB * P], "e1_1": v_r[1][HB * P:F]}

        def staged(n, shape):
            k, m = shape
            return stage[n % 2][:, 0:k * m].rearrange("p (k m) -> p k m", k=k)

        small = [
            (w_bc[:, :, 0:DS], kp(w["L0_attn_W_C"])), (w_bc[:, :, DS:2 * DS], kp(w["L0_attn_W_B"])),
            (w_out[:, :, :], kp(w["L0_attn_W_out"])), (w_kq[:, :, 0:C], kp(w["L1_attn_Wk"])),
            (w_kq[:, :, C + 2 * NH:NQ], kp(w["L1_attn_Wbeta"])), (w_ao[:, :, :], kp(w["L1_attn_Wo"])),
            (w_fo[:, :, :], kp(w["L1_ffn_Wo"])), (w_2[:, :, :], kp(w["L1_ffn_W2"])),
            (w_3[:, :, :], kp(w["L1_ffn_W3"])),
            (cols[:, 0:2], col(w["L0_attn_norm_w"])), (cols[:, 2:4], col(w["L0_attn_norm_b"])),
            (cols[:, 4:6], col(w["L1_ffn_ln1_w"])), (cols[:, 6:8], col(w["L1_ffn_ln1_b"])),
            (cols[:, 8:10], col(w["L1_ffn_ln2_w"])), (cols[:, 10:12], col(w["L1_ffn_ln2_b"])),
            (bdt_col[:, :], col(w["L0_attn_b_dt"])), (b1_col[:, :], col(w["L0_ffn_b1"][e_last])),
            (bbeta_row[:, :], row(w["L1_attn_b_beta"]).to_broadcast([P, NH])),
            (cs_row[:, :], row(w["L1_ffn_capital_shares"]).to_broadcast([P, 3])),
            (b2_row[:, :], row(w["L0_ffn_b2"][e_last]).to_broadcast([P, C])),
            (bo_row[:, :], row(w["L1_attn_b_o"]).to_broadcast([P, C])),
            (lnw_row[:, 0:C], row(w["L1_attn_ln_g"]).to_broadcast([B, C])),
            (lnw_row[:, C:2 * C], row(w["L1_attn_ln_b"]).to_broadcast([B, C])),
            (c_in[:, 0:C], w["L0_c"]), (c_in[:, C:2 * C], w["L1_c"]),
            (a_neg[:, :, :], w["L0_attn_A_log"].rearrange("(d p) s -> p d s", p=P)),
        ]
        pad = [ca[:, 0, 0:KC * P].rearrange("p (k m) -> p k m", k=KC),
               ca[:, 1, 0:KC * P].rearrange("p (k m) -> p k m", k=KC)]
        padded = []
        for k in range(KC):
            ch = slice(k * P, (k + 1) * P)
            padded += [(pad[0][:, k, 0:E_MOE], w["L0_ffn_Wr"][:, ch].rearrange("e p -> p e")),
                       (pad[1][:, k, 0:2], w["L1_ffn_conf_rwkv"][:, ch].rearrange("e p -> p e")),
                       (pad[1][:, k, 2:3], w["L1_ffn_conf_trans"][ch].rearrange("(p a) -> p a", a=1)),
                       (pad[1][:, k, 3:4], w["L1_ffn_w_diff"][ch].rearrange("(p a) -> p a", a=1)),
                       (pad[1][:, k, 4:7], w["L1_ffn_W_aff"][ch, :])]
        qv = [hid[:, 0:1, :], hid[:, 1:2, :]]
        wq_st = cb[:, :, 0:C]
        wv_st = cb[:, :, C:2 * C]

        with nc.Block() as block:

            def store_split(sp, n):
                if n < 2:
                    return
                sp.wait_ge(u_split, n + 1)
                sp.dma_start(w_split[n - 2], ws_in[n % 2][:, :, :, :].bitcast(F32).rearrange("p h k m -> p (h k m)"))\
                  .then_inc(u_store[n % 2], 16)

            @block.sync
            def _(sp):
                for semaphore in credited + [x for b in bank.values() for x in (b.full, b.free)]:
                    sp.sem_inc(semaphore, CREDIT)
                for dst, src in small:
                    sp.dma_start(dst, src).then_inc(u_load, 16)
                for k, name in enumerate(["L1_attn_Wq", "L1_attn_Wv"]):
                    sp.dma_start((wq_st, wv_st)[k], kp(w[name])).then_inc(u_load, 16)
                sp.wait_ge(u_zero, 1)
                for dst, src in padded:
                    sp.dma_start(dst, src).then_inc(u_load, 16)
                for n, (loads, shape) in enumerate(zip(pieces, shapes)):
                    if n >= 2:
                        sp.wait_ge(u_split, n - 1)
                    for at, m, src in loads:
                        sp.dma_start(staged(n, shape)[:, :, at:at + m], src).then_inc(u_stage[n % 2], 16)
                    if n >= 3:
                        store_split(sp, n - 1)
                store_split(sp, len(pieces) - 1)
                for k in range(2):
                    sp.wait_ge(u_store[k], 16 * NSLOT // 2)
                sp.wait_ge(u_rows, 2)
                for b in range(B):
                    for c in range(CPB):
                        sp.dma_start(mods[b * CPB + c:b * CPB + c + 1, :], modrow[b:b + 1, :]).then_inc(u_mods, 16)
                sp.wait_ge(u_mods, 16 * NCH)

            @block.gpsimd
            def _(pool):
                pool.memset(ca[:, :, :], 0.0).then_inc(u_zero, 1)
                pool.memset(ident[:, :], 0.0).then_inc(u_id, 1)
                pool.memset(keep[:, :], -1).then_inc(u_id, 1)
                pool.memset(mhalf[:, :], -0.5).then_inc(u_id, 1)
                pool.memset(eps_t[:, :], EPS)
                pool.wait_ge(u_id, 3)
                pool.affine_select(out=ident[:, :], in_=ident[:, :], compare_op=ALU.not_equal, fill=1.0,
                                   base=0, pattern=[[-1, P]], channel_multiplier=1).then_inc(u_id, 1)
                pool.memset(keep[:, 0:NCH:CPB], 0).then_inc(u_id, 1)
                pool.memset(state[:, :, :], 0.0).then_inc(u_id, 1)
                pool.memset(state_l[:, :], 0.0).then_inc(u_id, 1)

            n_small = 16 * (len(small) + 2 + len(padded))

            @block.scalar
            def _(act):
                act.wait_ge(u_load, n_small)
                act.activation(c_in[:, :], c_in[:, :], ACT.Silu).then_inc(u_silu, 1)
                act.activation(a_neg[:, :, :], a_neg[:, :, :], ACT.Exp).then_inc(u_exp, 1)
                for layer in range(2):
                    if layer:
                        act.wait_ge(u_mm, 3)
                    act.dma_start(wm[:, :, :], kp(w[f"L{layer}_wmod"])).then_inc(u_wm, 16)

            @block.tensor
            def _(pe):
                pe.wait_ge(u_silu, 1)
                pe.wait_ge(u_id, 7)
                for layer in range(2):
                    for k in range(KC):
                        at = layer * C + k * P
                        last = pe.transpose(psum["A0"][:, (layer * KC + k) * B:(layer * KC + k + 1) * B],
                                            c_in[:, at:at + P], ident[0:B, 0:B])
                last.then_inc(u_ct, 1)
                pe.wait_ge(u_ctc, 1)
                for layer in range(2):
                    pe.wait_ge(u_wm, 16 * (layer + 1))
                    for g in range(3):
                        name = ["B0", "B1", "B2"][g]
                        if layer:
                            pe.wait_ge(u_raw, g + 1)
                        for k in range(KC):
                            last = pe.matmul(psum[name][0:B, :], c_t[:, layer, k, :],
                                             wm[:, k, g * 2 * C:(g + 1) * 2 * C], start=k == 0, stop=k == KC - 1)
                        last.then_inc(u_mm, 1)

            @block.vector
            def _(dve):
                done = [0]

                def step(ins):
                    done[0] += 1
                    ins.then_inc(u_dve, 1)
                    dve.wait_ge(u_dve, done[0])

                for n, (loads, shape) in enumerate(zip(pieces, shapes)):
                    earlier = sum(len(l) for l, _ in list(zip(pieces, shapes))[n % 2:n:2])
                    dve.wait_ge(u_stage[n % 2], 16 * (earlier + len(loads)))
                    src = staged(n, shape)
                    if n == 0:
                        high, low = w_in["h"][:, :, :], w_in["l"][:, :, :]
                    elif n == 1:
                        high, low = w_dt["h"][:, :, :], w_dt["l"][:, :, :]
                    else:
                        high, low = ws_in[n % 2][:, 0], ws_in[n % 2][:, 1]
                        if n >= 4:
                            dve.wait_ge(u_store[n % 2], 16 * ((n - 2) // 2))
                    step(dve.tensor_copy(high, src))
                    dve.tensor_tensor(low, src, high.bitcast(F32), ALU.subtract).then_inc(u_split, 1)
                dve.wait_ge(u_load, n_small)
                for k, wt in enumerate((w_rt, w_bd)):
                    step(dve.tensor_copy(wt["h"][:, :, :], pad[k]))
                    step(dve.tensor_tensor(wt["l"][:, :, :], pad[k], wt["h"][:, :, :].bitcast(F32), ALU.subtract))
                for k, wt in enumerate((wq_st, wv_st)):
                    for c in range(KC):
                        step(dve.tensor_reduce(w_kq[:, c, C + k * NH:C + (k + 1) * NH],
                                               wt[:, c, :].rearrange("p (h d) -> p h d", h=NH), AX, ALU.add))
                dve.wait_ge(u_exp, 1)
                step(dve.tensor_scalar(a_neg[:, :, :], a_neg[:, :, :], 1e-6, 1.0, ALU.max, ALU.min))
                step(dve.tensor_scalar(a_neg[:, :, :], a_neg[:, :, :], -1.0, None, ALU.mult))
                dve.wait_ge(u_ct, 1)
                dve.tensor_copy(c_t[:, :, :, :], psum["A0"][:, 0:2 * KC * B]
                                .rearrange("p (l k b) -> p l k b", l=2, k=KC)).then_inc(u_ctc, 1)

                def mrow(name):
                    return modrow[:, ROW[name] * C:(ROW[name] + 1) * C]

                for layer in range(2):
                    for g in range(3):
                        dve.wait_ge(u_mm, 3 * layer + g + 1)
                        dve.tensor_copy(modraw[:, g * 2 * C:(g + 1) * 2 * C], psum[["B0", "B1", "B2"][g]][0:B, :])\
                           .then_inc(u_raw, 1)
                    dve.wait_ge(u_raw, 3 * layer + 3)
                    raw = [modraw[:, k * C:(k + 1) * C] for k in range(6)]
                    for part, (sa, ca_, ga) in enumerate((raw[0:3], raw[3:6])):
                        p_ = "AB"[part]
                        if part == 0:
                            dve.tensor_copy(mrow(f"sA{layer}"), sa)
                        step(dve.tensor_scalar(mrow(f"c{p_}{layer}"), ca_, 1.0, None, ALU.add))
                        goal = mrow("gA1w") if (layer, part) == (1, 0) else mrow(f"g{p_}{layer}")
                        step(dve.tensor_scalar(ca_, ga, 0.0, 2.0, ALU.is_ge, ALU.mult))
                        step(dve.tensor_scalar(ca_, ca_, -1.0, None, ALU.add))
                        step(dve.scalar_tensor_tensor(out=ga, in0=ga, scalar=-1.0, in1=ga, op0=ALU.mult, op1=ALU.max))
                        step(dve.tensor_scalar(ga, ga, GATE_MIN, None, ALU.max))
                        step(dve.tensor_tensor(ga, ga, ca_, ALU.mult))
                        if (layer, part) == (1, 0):
                            step(dve.tensor_tensor(mrow("gA1b"), ga, lnw_row[:, C:2 * C], ALU.mult))
                            step(dve.tensor_tensor(goal, ga, lnw_row[:, 0:C], ALU.mult))
                        else:
                            step(dve.tensor_copy(goal, ga))
                    dve.tensor_copy(mrow(f"sB{layer}"), raw[3]).then_inc(u_rows, 1)
                    dve.wait_ge(u_rows, layer + 1)

        x_v = w["L0_attn_x"].rearrange("b (c t p) m -> (b c) p t m", t=NT, p=P)
        out_v = out.rearrange("b (c t p) m -> (b c) p t m", t=NT, p=P)

        slot_dmas = [2 if name in w_down else 1 for name in SLOTS]
        for k in range(2):
            s_w[k].n = 16 * sum(slot_dmas[k::2])

        def slot_ready(eng, j, name):
            q = SLOTS.index(name)
            eng.wait_ge(s_w[q % 2].sem, s_w[q % 2].at(j, 16 * sum(slot_dmas[q % 2:q + 1:2])))

        def block_used(eng, j, n):
            k, e = n % NHB, n // NHB
            if k == NHB - 1:
                take(eng, j, ["ffn1", "e0_1", "e1_1"][e])
            else:
                eng.wait_ge(d_hfree.sem, d_hfree.at(j, (NHB - 1) * e + k + 1))

        def per_tile(m):
            return m.unsqueeze(1).to_broadcast([P, NT, C])

        def m_s(name):
            return mod_s[:, ROW[name], :]

        def m_d(name):
            return mod_d[:, ROW[name] - NROW_S, :]

        with nc.Block() as block:

            @block.sync
            def _(sp):
                def load_x(i):
                    since(sp, s_x1, i)
                    sp.dma_start(xin[:, :, :], x_v[bass.ds(i, 1)].rearrange("a p t m -> p (a t) m"))\
                      .then_inc(s_xin.sem, 16)
                    sp.dma_start(mod_s[:, :, :].rearrange("p r m -> p (r m)"),
                                 mods[bass.ds(i, 1), 0:NROW_S * C].to_broadcast([P, NROW_S * C]))\
                      .then_inc(s_mods.sem, 16)

                def front(i, step, k):
                    if step == "mean" and k == 0:
                        load_x(i)
                    if step == "bc":
                        used(sp, i, "bc")
                        sp.dma_start(b_rows[:, :], bcs[DS:2 * DS, :]).then_inc(s_bw.sem, 16)
                    if step == "dt" and k == 0:
                        sp.wait_ge(s_bw.sem, s_bw.at(i, 16))
                        load_b(i, 0)

                def load_b(i, s):
                    sp.dma_start(bb[:, s % 4, :], b_rows[s:s + 1, :].to_broadcast([P, CT]))\
                      .then_inc(s_bb[s % 4].sem, 16)

                def unit(i, u):
                    s = u // DB
                    if u % DB == 0 and 1 <= s < DS:
                        if s >= 4:
                            sp.wait_ge(s_bu.sem, s_bu.at(i, DB * (s - 3)))
                        load_b(i, s)

                def tail(i, step, k):
                    pass

                def load_mod(j, k):
                    lo, hi = [(0, 3), (3, 7), (7, 10)][k]
                    since(sp, (d_x2, d_x3, d_x5)[k], j)
                    sp.dma_start(mod_d[:, lo:hi, :].rearrange("p r m -> p (r m)"),
                                 mods[bass.ds(j, 1), (NROW_S + lo) * C:(NROW_S + hi) * C]
                                 .to_broadcast([P, (hi - lo) * C])).then_inc(s_modd[k].sem, 16)

                def load_slot(j, name):
                    q = SLOTS.index(name)
                    before = {"ffn_1": ("start", "B3"), "rv": ("block", 3), "sw": ("full", "ffn1"),
                              "e0_0": ("full", "v1"), "e0_1": ("full", "tw1"), "e1_0": ("block", NHB + 3),
                              "e1_1": ("full", "e0_1")}
                    kind, what = before.get(name, ("start", None))
                    if kind == "full":
                        take(sp, j, what)
                    elif kind == "block":
                        block_used(sp, j, what)
                    elif what is None:
                        if not (isinstance(j, int) and j == 0):
                            block_used(sp, j - 1, 2 * NHB + 3)
                    else:
                        last = bank[what]
                        sp.wait_ge(last.full, j * len(last.uses) + CREDIT)
                    sp.dma_start(ws_in[q % 2][:, :, :, :].bitcast(F32).rearrange("p h k m -> p (h k m)"), w_split[q])\
                      .then_inc(s_w[q % 2].sem, 16)
                    if name in w_down:
                        sp.dma_start(ws_out[q % 2][:, :, :], kp(w_down[name])).then_inc(s_w[q % 2].sem, 16)

                def dense(j, pace, last=False):
                    load_mod(j, 0)
                    load_mod(j, 1)
                    load_slot(j, "ffn_1")
                    pace("load_ffn_1")
                    load_mod(j, 2)
                    pace("c3")
                    load_slot(j, "rv")
                    pace("c7")
                    load_slot(j, "sw")
                    pace("k_proj")
                    load_slot(j, "e0_0")
                    pace("n_trans")
                    load_slot(j, "e0_1")
                    pace("o3")
                    load_slot(j, "e1_0")
                    pace("o7")
                    load_slot(j, "e1_1")
                    pace("p3")
                    if not last:
                        load_slot(j + 1, "ffn_0")
                    pace("q_out")
                    sp.wait_ge(d_x5.sem, d_x5.at(j, 1))
                    sp.dma_start(out_v[bass.ds(j, 1)].rearrange("a p t m -> p (a t) m"), xd[:, :, :])\
                      .then_inc(s_out.sem, 16)

                load_slot(0, "ffn_0")
                Pace(PACE["sp"], front, unit, tail, 0).upto(len(S_STEPS))
                with sp.Fori(1, NCH) as i:
                    dense(i - 1, Pace(PACE["sp"], front, unit, tail, i))
                dense(NCH - 1, Pace(PACE["sp"], None, None, None, NCH), last=True)
                sp.wait_ge(s_out.sem, s_out.at(NCH, 0))

            @block.gpsimd
            def _(pool):
                def rstd(own, mv, rs, mv_at, sig):
                    own.step(pool.tensor_tensor(rs[:, :], mv[:, :, 1], eps_t[:, :], ALU.add))
                    pool.tensor_tensor(rs[:, :], rs[:, :], mhalf[:, :], ALU.pow).then_inc(sig.sem, 1)

                own_s = [None]

                def front(i, step, k):
                    if (step, k) == ("mean", 0):
                        own_s[0] = Own(pool, o_pool_s, i)
                    own = own_s[0]
                    if step == "mean":
                        pool.wait_ge(s_mv.sem, s_mv.at(i, k + 1))
                        rstd(own, mv_s, rs_s, k + 1, s_rs)
                    if (step, k) == ("norm", 0):
                        pool.wait_ge(s_mods.sem, s_mods.at(i, 16))
                        pool.wait_ge(s_n.sem, s_n.at(i, 1))
                        own.step(pool.tensor_tensor(h0[:, :, :], h0[:, :, :], per_tile(m_s("cA0")), ALU.mult))
                        pool.tensor_tensor(h0[:, :, :], h0[:, :, :], per_tile(m_s("sA0")), ALU.add)\
                            .then_inc(s_h0.sem, 1)
                    if (step, k) == ("norm", 1):
                        pool.wait_ge(s_n.sem, s_n.at(i, 2))
                        own.step(pool.tensor_tensor(h0[:, :, :], h0[:, :, :], per_tile(m_s("gA0")), ALU.mult))
                        pool.tensor_tensor(xin[:, :, :], xin[:, :, :], h0[:, :, :], ALU.add).then_inc(s_xg.sem, 1)
                        own.end()
                    if step == "clip":
                        pool.wait_ge(s_dt.sem, s_dt.at(i, k + 1))
                        pool.tensor_tensor(z[:, k, :], z[:, k, :], dt[:, k, :], ALU.mult).then_inc(s_u.sem, 1)

                def tail(i, step, k):
                    pass

                def unit(i, u):
                    s, d = u // DB, u % DB
                    if s == DS:
                        return
                    if s == 0:
                        pool.wait_ge(s_u.sem, s_u.at(i, d + 1))
                    if d == 0:
                        pool.wait_ge(s_bb[s % 4].sem, s_bb[s % 4].at(i, 16 * (s // 4 + 1)))
                    if u >= 4:
                        used(pool, i, f"dA{u - 4}")
                    ins = pool.tensor_tensor(bu[:, u % 4, :], z[:, d, :], bb[:, s % 4, :], ALU.mult)
                    ins.then_inc(s_bu.sem, 1)

                def modulate(own, j, k, scale, shift, pace):
                    own.mark(pool.tensor_tensor(hA[:, :, :], hA[:, :, :], per_tile(m_d(scale)), ALU.mult))
                    pace(f"scaled{k}")
                    own.wait()
                    pool.tensor_tensor(hA[:, :, :], hA[:, :, :], per_tile(m_d(shift)), ALU.add).then_inc(d_h.sem, 1)

                def norm(own, j, k, pace):
                    pool.wait_ge(d_mv.sem, d_mv.at(j, k + 1))
                    rstd(own, mv_d, rs_d, k + 1, d_rs)
                    pace(f"rstd{k}")

                def dense(j, pace):
                    own = Own(pool, o_pool_d, j)
                    pace("a_stats")
                    norm(own, j, 0, pace)
                    pool.wait_ge(s_modd[0].sem, s_modd[0].at(j, 16))
                    pool.wait_ge(d_n.sem, d_n.at(j, 1))
                    modulate(own, j, 0, "cB0", "sB0", pace)
                    pace("b_turn")
                    pace("e_stats")
                    norm(own, j, 1, pace)
                    pool.wait_ge(s_modd[1].sem, s_modd[1].at(j, 16))
                    pool.wait_ge(d_n.sem, d_n.at(j, 2))
                    modulate(own, j, 1, "cA1", "sA1", pace)
                    pace("h2")
                    pool.tensor_tensor(xd[:, :, :], xd[:, :, :], per_tile(m_d("gA1b")), ALU.add).then_inc(d_xb.sem, 1)
                    pace("f_kv")
                    used(pool, j, "h2T1")
                    pool.tensor_tensor(hA[:, :, :], hA[:, :, :], per_tile(bo_row[:, :]), ALU.add).then_inc(d_hb.sem, 1)
                    pace("h_stats")
                    norm(own, j, 2, pace)
                    pool.wait_ge(d_n.sem, d_n.at(j, 3))
                    own.mark(pool.tensor_tensor(nn[:, :, :], nn[:, :, :], per_tile(m_d("gA1w")), ALU.mult))
                    pace("att_scaled")
                    own.wait()
                    pool.wait_ge(d_xb.sem, d_xb.at(j, 1))
                    pool.tensor_tensor(xd[:, :, :], xd[:, :, :], nn[:, :, :], ALU.add).then_inc(d_x3.sem, 1)
                    pace("i_stats")
                    norm(own, j, 3, pace)
                    pool.wait_ge(s_modd[2].sem, s_modd[2].at(j, 16))
                    pool.wait_ge(d_n.sem, d_n.at(j, 4))
                    modulate(own, j, 2, "cB1", "sB1", pace)
                    pace("i_stats2")
                    norm(own, j, 4, pace)
                    pace("j_turn")
                    pace("m_stats")
                    norm(own, j, 5, pace)
                    pace("m_turn")
                    pace("q_out")
                    own.end()

                Pace(PACE["pool"], front, unit, tail, 0).upto(len(S_STEPS))
                with pool.Fori(1, NCH) as i:
                    dense(i - 1, Pace(PACE["pool"], front, unit, tail, i))
                dense(NCH - 1, Pace(PACE["pool"], None, None, None, NCH))

            @block.scalar
            def _(act):
                def front(i, step, k):
                    if step == "turn":
                        for c in range(KC):
                            b = take(act, i, f"xn{c}")
                            act.activation(xnf[:, c, :], b.t[:, :], ACT.Identity, scale=cols[:, c:c + 1],
                                           bias=cols[:, 2 + c:3 + c]).then_inc(b.free, 1)
                        for c in range(KC):
                            used(act, i, f"xn{c}")
                            act.activation(xnh[:, c, :], xnf[:, c, :], ACT.Copy).then_inc(s_xnh.sem, 1)
                    if step == "z":
                        b = take(act, i, f"z{k}")
                        act.activation(zh[:, k, :], b.t[:, :], ACT.Copy).then_inc(s_zh.sem, 1)
                        act.activation(z[:, k, :], b.t[:, :], ACT.Copy).then_inc(b.free, 1)
                    if step == "gate":
                        b = take(act, i, f"gt{k}")
                        act.activation(gate[:, k, :], b.t[:, :], ACT.Silu).then_inc(b.free, 1)
                    if step == "bc":
                        b = take(act, i, "bc")
                        act.activation(bcs[:, :], b.t[0:2 * DS, :], ACT.Copy).then_inc(b.free, 1)
                    if (step, k) == ("gate", 2):
                        b = take(act, i, "ct")
                        act.activation(ctok[:, :, :], b.t[:, 0:NT * 2 * DS].rearrange("p (t c) -> p t c", t=NT),
                                       ACT.Copy).then_inc(b.free, 1)
                    if step == "softplus":
                        own = Own(act, o_act_s, i)
                        for d in range(DB):
                            used(act, i, f"dt{d}")
                            own.mark(act.activation(dt[:, d, :], dt[:, d, :], ACT.Exp))
                        for d in range(DB):
                            own.wait(d + 1)
                            act.activation(dt[:, d, :], dt[:, d, :], ACT.Ln, bias=1.0).then_inc(s_sp.sem, 1)
                        own.end()

                def unit(i, u):
                    s, d = u // DB, u % DB
                    if s == DS:
                        return
                    if s == 0:
                        act.wait_ge(s_dt.sem, s_dt.at(i, d + 1))
                    b = fill(act, i, f"dA{u}")
                    act.activation(b.t[:, :], dt[:, d, :], ACT.Exp, scale=a_neg[:, d, s:s + 1]).then_inc(b.full, 1)

                def tail(i, step, k):
                    if step == "y":
                        b = take(act, i, f"y{k}")
                        act.activation(z[:, k, :], b.t[:, :], ACT.Copy).then_inc(b.free, 1)

                def turned(j, use, pace, scale=None, shift=None):
                    for k in range(KC):
                        b = take(act, j, f"{use}{k}")
                        if scale is None:
                            ins = act.activation(ff[:, k, :], b.t[:, :], ACT.Copy)
                        else:
                            ins = act.activation(ff[:, k, :], b.t[:, :], ACT.Identity,
                                                 scale=cols[:, scale + k:scale + k + 1],
                                                 bias=cols[:, shift + k:shift + k + 1])
                        ins.then_inc(b.free, 1)
                        pace(f"{use}{k}")

                def high(j, use, pace):
                    for k in range(KC):
                        used(act, j, f"{use}{k}")
                        act.activation(fh[:, k, :], ff[:, k, :], ACT.Copy).then_inc(d_fh.sem, 1)
                        pace(f"{use}{k}_high")

                def to_rows(j, use, pace):
                    b = take(act, j, use)
                    act.activation(rows8[:, :], b.t[0:8, :], ACT.Copy).then_inc(b.free, 1)
                    pace(use)

                def dense(j, pace):
                    pace("b_turn")
                    turned(j, "h1T", pace)
                    high(j, "h1T", pace)
                    to_rows(j, "router", pace)
                    act.wait_ge(d_lsub.sem, d_lsub.at(j, 1))
                    act.activation(lg[:, :, :], lg[:, :, :], ACT.Exp).then_inc(d_lexp.sem, 1)
                    pace("b_router")
                    for k in range(F // P):
                        b = take(act, j, f"c{k}")
                        if k >= HB:
                            block_used(act, j, k - HB)
                        act.activation(hid[:, k % HB, :], b.t[:, :], ACT.Gelu, bias=b1_col[:, k:k + 1])\
                           .then_inc(b.free, 1)
                        pace(f"c{k}")
                    pace("f_turn")
                    turned(j, "h2T", pace)
                    pace("f_kv")
                    act.wait_ge(d_sm.sem, d_sm.at(j, 1))
                    act.activation(bx[:, :, :].rearrange("p t (h d) -> p t h d", h=NH),
                                   sm[:, :, 2 * NH:3 * NH].unsqueeze(3).to_broadcast([P, NT, NH, HD]),
                                   ACT.Sigmoid).then_inc(d_bx.sem, 1)
                    pace("beta")
                    act.activation(qx[:, :, :].rearrange("p t (h d) -> p t h d", h=NH),
                                   sm[:, :, 0:NH].unsqueeze(3).to_broadcast([P, NT, NH, HD]),
                                   ACT.Copy).then_inc(d_bx.sem, 1)
                    pace("q")
                    for k in range(KC):
                        b = take(act, j, f"kvT{k}")
                        act.activation(ca[:, k, :], b.t[:, :], ACT.Copy).then_inc(b.free, 1)
                        pace(f"kvT{k}")
                    pace("j_turn")
                    turned(j, "xlT", pace, 4, 6)
                    high(j, "xlT", pace)
                    for k in range(KC):
                        b = take(act, j, f"r{k}")
                        act.activation(cb[:, k, :], b.t[:, :], ACT.Sigmoid).then_inc(b.free, 1)
                        pace(f"r{k}")
                    for k in range(KC):
                        b = take(act, j, f"s{k}")
                        act.activation(ca[:, k, :], b.t[:, :], ACT.Copy).then_inc(b.free, 1)
                        pace(f"s{k}")
                    for k in range(KC):
                        b = take(act, j, f"sW{k}")
                        act.activation(cb[:, k, :], b.t[:, :], ACT.Sigmoid).then_inc(b.free, 1)
                        pace(f"sW{k}")
                    turned(j, "hhT", pace, 8, 10)
                    high(j, "hhT", pace)
                    to_rows(j, "bids", pace)
                    used(act, j, "bidsT")
                    act.activation(sg[:, :, :], bl[:, :, 0:4], ACT.Sigmoid).then_inc(d_sg.sem, 1)
                    for e in range(2):
                        for k in range(F // P):
                            use = f"{'op'[e]}{k}"
                            n = 8 * e + k
                            b = take(act, j, use)
                            block_used(act, j, NHB + n - HB)
                            act.activation(hid[:, k % HB, :], b.t[:, :], ACT.Relu).then_inc(d_rl.sem, 1)
                            pace(use)
                    pace("q_out")

                Pace(PACE["act"], front, unit, tail, 0).upto(len(S_STEPS))
                with act.Fori(1, NCH) as i:
                    dense(i - 1, Pace(PACE["act"], front, unit, tail, i))
                dense(NCH - 1, Pace(PACE["act"], None, None, None, NCH))

            @block.vector
            def _(dve):
                def stats(own, src, st, mv, sig):
                    for t in range(NT):
                        own.mark(dve.bn_stats(st[:, t, :], src[:, t, :]))
                    own.wait()
                    dve.memset(carrier[:, :], 0.0)
                    for t in range(NT):
                        ins = dve.bn_aggr(mv[:, t, :], st[:, t, :])
                    ins.then_inc(sig.sem, 1)

                def apply(dst, src, mv, rs, sig):
                    for t in range(NT):
                        ins = dve.tensor_scalar(dst[:, t, :], src[:, t, :], mv[:, t, 0:1], rs[:, t:t + 1],
                                                ALU.subtract, ALU.mult)
                    ins.then_inc(sig.sem, 1)

                own_s = [None]

                def front(i, step, k):
                    if (step, k) == ("mean", 0):
                        own_s[0] = Own(dve, o_dve_s, i)
                    own = own_s[0]
                    if (step, k) == ("mean", 0):
                        dve.wait_ge(s_xin.sem, s_xin.at(i, 16))
                        stats(own, xin, st_s, mv_s, s_mv)
                        own.mark(dve.tensor_tensor(state[:, :, :].rearrange("p s d -> p (s d)").bitcast(I32),
                                                   state[:, :, :].rearrange("p s d -> p (s d)").bitcast(I32),
                                                   keep[:, bass.ds(i, 1)].to_broadcast([P, DS * DB]), ALU.bitwise_and))
                    if (step, k) == ("mean", 1):
                        dve.wait_ge(s_h0.sem, s_h0.at(i, 1))
                        stats(own, h0, st_s, mv_s, s_mv)
                    if step == "norm":
                        dve.wait_ge(s_rs.sem, s_rs.at(i, k + 1))
                        apply((h0, n0)[k], (xin, h0)[k], mv_s, rs_s, s_n)
                    if step == "turn":
                        for c in range(KC):
                            dve.wait_ge(s_xnh.sem, s_xnh.at(i, c + 1))
                            dve.tensor_tensor(xnl[:, c, :], xnf[:, c, :], xnh[:, c, :].bitcast(F32), ALU.subtract)\
                               .then_inc(s_xnl.sem, 1)
                    if step == "z":
                        used(dve, i, f"z{k}")
                        dve.tensor_tensor(zl[:, k, :], z[:, k, :], zh[:, k, :].bitcast(F32), ALU.subtract)\
                           .then_inc(s_zl.sem, 1)
                    if step == "dt":
                        b = take(dve, i, f"dt{k}")
                        dve.tensor_scalar(dt[:, k, :], b.t[:, :], bdt_col[:, k:k + 1], DT_CLAMP, ALU.add, ALU.min)\
                           .then_inc(b.free, 1)
                    if step == "clip":
                        dve.wait_ge(s_sp.sem, s_sp.at(i, k + 1))
                        dve.tensor_scalar(dt[:, k, :], dt[:, k, :], DT_MIN, DT_MAX, ALU.max, ALU.min)\
                           .then_inc(s_dt.sem, 1)

                def read_out(i, s, t):
                    use = f"hT{s * NT + t}"
                    b = take(dve, i, use)
                    if s == 0:
                        if t == 0:
                            used(dve, i, "ct")
                        ins = dve.tensor_scalar(acc[:, t, :], b.t[:, :], ctok[:, t, s:s + 1], None, ALU.mult)
                    else:
                        used(dve, i, f"hT{(s - 1) * NT + t}")
                        ins = dve.scalar_tensor_tensor(out=acc[:, t, :], in0=b.t[:, :], scalar=ctok[:, t, s:s + 1],
                                                       in1=acc[:, t, :], op0=ALU.mult, op1=ALU.add)
                    ins.then_inc(b.free, 1)

                def unit(i, u):
                    s, d = u // DB, u % DB
                    if d == 0 and s >= 1:
                        for n in (u - 2, u - 1):
                            used(dve, i, f"dA{n}")
                        own_s[0].mark(dve.tensor_copy(state[:, s - 1, :], hs[:, (s - 1) % 2, :, CT - 1]))
                    if s < DS:
                        dve.wait_ge(s_bu.sem, s_bu.at(i, u + 1))
                        b = take(dve, i, f"dA{u}")
                        dve.tensor_tensor_scan(hs[:, s % 2, d, :], b.t[:, :], bu[:, u % 4, :],
                                               state[:, s, d:d + 1], ALU.mult, ALU.add).then_inc(b.free, 1)
                    if s >= 1:
                        read_out(i, s - 1, d)

                def tail(i, step, k):
                    own = own_s[0]
                    if step == "gated":
                        for t in range(NT):
                            used(dve, i, f"gt{t}")
                            used(dve, i, f"hT{(DS - 1) * NT + t}")
                        for t in range(NT):
                            ins = dve.tensor_tensor(acc[:, t, :], acc[:, t, :], gate[:, t, :], ALU.mult)
                        ins.then_inc(s_yg.sem, 1)
                    if step == "out":
                        if k == 0:
                            since(dve, d_x2, i)
                        b = take(dve, i, f"wo{k}")
                        tiles = x1[:, 2 * k:2 * k + 2, :]
                        dve.tensor_tensor(tiles, b.t[:, :].rearrange("p (t c) -> p t c", t=2),
                                          m_s("gA0").unsqueeze(1).to_broadcast([P, 2, C]), ALU.mult)\
                           .then_inc(b.free, 1)
                    if step == "x1":
                        dve.wait_ge(s_xg.sem, s_xg.at(i, 1))
                        for p in range(2):
                            used(dve, i, f"wo{p}")
                        dve.tensor_tensor(x1[:, :, :], x1[:, :, :], xin[:, :, :], ALU.add).then_inc(s_x1.sem, 1)
                        own.end()

                def low(j, k, pace):
                    for c in range(KC):
                        dve.wait_ge(d_fh.sem, d_fh.at(j, KC * k + c + 1))
                        dve.tensor_tensor(fl[:, c, :], ff[:, c, :], fh[:, c, :].bitcast(F32), ALU.subtract)\
                           .then_inc(d_fl.sem, 1)
                        pace(f"low{k}_{c}")

                def pair(b):
                    return b.t[:, :].rearrange("p (t c) -> p t c", t=2)

                def dense(j, pace):
                    own = Own(dve, o_dve_d, j)
                    step = own.step
                    dve.wait_ge(s_x1.sem, s_x1.at(j, 1))
                    stats(own, x1, st_d, mv_d, d_mv)
                    pace("a_stats")
                    dve.wait_ge(d_rs.sem, d_rs.at(j, 1))
                    apply(hA, x1, mv_d, rs_d, d_n)
                    pace("a_norm")
                    pace("b_turn")
                    low(j, 0, pace)
                    b = take(dve, j, "routerT")
                    dve.tensor_copy(lg[:, :, :], b.t[:, 0:NT * 8].rearrange("p (t e) -> p t e", t=NT))\
                       .then_inc(b.free, 1)
                    used(dve, j, "routerT")
                    step(dve.tensor_reduce(lg_m[:, :], lg[:, :, :], AX, ALU.max))
                    dve.tensor_tensor(lg[:, :, :], lg[:, :, :], lg_m[:, :].unsqueeze(2).to_broadcast([P, NT, E_MOE]),
                                      ALU.subtract).then_inc(d_lsub.sem, 1)
                    pace("b_router")
                    dve.wait_ge(d_lexp.sem, d_lexp.at(j, 1))
                    step(dve.tensor_reduce(lg_m[:, :], lg[:, :, :], AX, ALU.add))
                    step(dve.reciprocal(lg_m[:, :], lg_m[:, :]))
                    step(dve.tensor_tensor(prob[:, :], lg_m[:, :], lg[:, :, E_MOE - 1], ALU.mult))
                    pace("prob")
                    dve.wait_ge(s_modd[0].sem, s_modd[0].at(j, 16))
                    since(dve, s_out, j)
                    for p in range(2):
                        b = take(dve, j, f"ffn{p}")
                        dve.tensor_tensor(nn[:, 2 * p:2 * p + 2, :], pair(b),
                                          b2_row[:, :].unsqueeze(1).to_broadcast([P, 2, C]), ALU.add)\
                           .then_inc(b.free, 1)
                        pace(f"ffn{p}")
                    for p in range(2):
                        used(dve, j, f"ffn{p}")
                        for t in (2 * p, 2 * p + 1):
                            own.mark(dve.scalar_tensor_tensor(out=nn[:, t, :], in0=nn[:, t, :], scalar=prob[:, t:t + 1],
                                                              in1=m_d("gB0"), op0=ALU.mult, op1=ALU.mult))
                    pace("ffn_scaled")
                    own.wait()
                    dve.tensor_tensor(xd[:, :, :], x1[:, :, :], nn[:, :, :], ALU.add).then_inc(d_x2.sem, 1)
                    pace("d_x2")
                    dve.wait_ge(d_x2.sem, d_x2.at(j, 1))
                    stats(own, xd, st_d, mv_d, d_mv)
                    pace("e_stats")
                    dve.wait_ge(d_rs.sem, d_rs.at(j, 2))
                    apply(hA, xd, mv_d, rs_d, d_n)
                    pace("e_norm")
                    pace("f_turn")
                    for t in range(NT):
                        use = f"kq{t}"
                        b = take(dve, j, use)
                        step(dve.tensor_copy(sm[:, t, :], b.t[:, C:NQ]))
                        ins = dve.tensor_tensor(nn[:, t, :].rearrange("p (h d) -> p h d", h=NH),
                                                b.t[:, 0:C].rearrange("p (h d) -> p h d", h=NH),
                                                sm[:, t, NH:2 * NH].unsqueeze(2).to_broadcast([P, NH, HD]), ALU.mult)
                        ins.then_inc(b.free, 1)
                        pace(f"kq{t}")
                    dve.tensor_tensor(sm[:, :, 2 * NH:3 * NH], sm[:, :, 2 * NH:3 * NH],
                                      bbeta_row[:, :].unsqueeze(1).to_broadcast([P, NT, NH]), ALU.add)\
                       .then_inc(d_sm.sem, 1)
                    own.mark(dve.tensor_tensor(state_l[:, :].bitcast(I32), state_l[:, :].bitcast(I32),
                                               keep[:, bass.ds(j, 1)].to_broadcast([P, KC]), ALU.bitwise_and))
                    pace("f_kv")
                    pace("g_turn")
                    own.wait()
                    for k in range(KC):
                        if k:
                            pace("scan0")
                        b = take(dve, j, f"btT{k}")
                        used(dve, j, f"kvT{k}")
                        dve.tensor_tensor_scan(cb[:, k, :], b.t[:, :], ca[:, k, :], state_l[:, k:k + 1],
                                               ALU.mult, ALU.add).then_inc(b.free, 1)
                        used(dve, j, f"btT{k}")
                        step(dve.tensor_copy(state_l[:, k:k + 1], cb[:, k, CT - 1:CT]))
                        b = take(dve, j, f"qsT{k}")
                        dve.tensor_tensor(cb[:, k, :], cb[:, k, :], b.t[:, :], ALU.mult).then_inc(b.free, 1)
                        pace(f"qsT{k}")
                    pace("g_scan")
                    dve.wait_ge(d_hb.sem, d_hb.at(j, 1))
                    for p in range(2):
                        b = take(dve, j, f"ao{p}")
                        dve.tensor_tensor(hA[:, 2 * p:2 * p + 2, :], pair(b), hA[:, 2 * p:2 * p + 2, :], ALU.add)\
                           .then_inc(b.free, 1)
                        pace(f"ao{p}")
                    pace("h_out")
                    for p in range(2):
                        used(dve, j, f"ao{p}")
                    stats(own, hA, st_d, mv_d, d_mv)
                    pace("h_stats")
                    dve.wait_ge(d_rs.sem, d_rs.at(j, 3))
                    apply(nn, hA, mv_d, rs_d, d_n)
                    pace("h_norm")
                    dve.wait_ge(d_x3.sem, d_x3.at(j, 1))
                    stats(own, xd, st_d, mv_d, d_mv)
                    pace("i_stats")
                    dve.wait_ge(d_rs.sem, d_rs.at(j, 4))
                    apply(hA, xd, mv_d, rs_d, d_n)
                    pace("i_norm")
                    dve.wait_ge(d_h.sem, d_h.at(j, 3))
                    stats(own, hA, st_d, mv_d, d_mv)
                    pace("i_stats2")
                    dve.wait_ge(d_rs.sem, d_rs.at(j, 5))
                    apply(nn, hA, mv_d, rs_d, d_n)
                    pace("i_norm2")
                    pace("j_turn")
                    low(j, 1, pace)
                    pace("k_proj")
                    for k in range(KC):
                        b = take(dve, j, f"v{k}")
                        used(dve, j, f"r{k}")
                        dve.tensor_tensor(cb[:, k, :], cb[:, k, :], b.t[:, :], ALU.mult).then_inc(b.free, 1)
                        pace(f"v{k}")
                    pace("l_out")
                    for p in range(2):
                        b = take(dve, j, f"att{p}")
                        dve.tensor_tensor(hA[:, 2 * p:2 * p + 2, :], pair(b), hA[:, 2 * p:2 * p + 2, :], ALU.add)\
                           .then_inc(b.free, 1)
                        pace(f"att{p}")
                    for p in range(2):
                        used(dve, j, f"att{p}")
                    stats(own, hA, st_d, mv_d, d_mv)
                    pace("m_stats")
                    dve.wait_ge(d_rs.sem, d_rs.at(j, 6))
                    apply(nn, hA, mv_d, rs_d, d_n)
                    pace("m_norm")
                    pace("m_turn")
                    low(j, 2, pace)
                    pace("n_bids")
                    b = take(dve, j, "bidsT")
                    dve.tensor_copy(bl[:, :, :], b.t[:, 0:NT * 8].rearrange("p (t e) -> p t e", t=NT))\
                       .then_inc(b.free, 1)
                    for k in range(KC):
                        b = take(dve, j, f"tw{k}")
                        used(dve, j, f"sW{k}")
                        dve.tensor_tensor(cb[:, k, :], cb[:, k, :], b.t[:, :], ALU.mult).then_inc(b.free, 1)
                        pace(f"tw{k}")
                    pace("product")
                    dve.wait_ge(d_sg.sem, d_sg.at(j, 1))
                    step(dve.tensor_tensor(bid[:, :, :], sg[:, :, 0:3], cs_row[:, :].unsqueeze(1)
                                           .to_broadcast([P, NT, 3]), ALU.mult))
                    step(dve.tensor_tensor(bid[:, :, :], bid[:, :, :], sg[:, :, 3:4].to_broadcast([P, NT, 3]), ALU.mult))
                    step(dve.tensor_tensor(bid[:, :, :], bid[:, :, :], bl[:, :, 4:7], ALU.add))
                    step(dve.tensor_reduce(bmax[:, :], bid[:, :, :], AX, ALU.max))
                    step(dve.tensor_tensor(win[:, :, :], bid[:, :, :], bmax[:, :].unsqueeze(2)
                                           .to_broadcast([P, NT, 3]), ALU.is_equal))
                    step(dve.tensor_tensor(win[:, :, 1], win[:, :, 1], win[:, :, 0], ALU.is_gt))
                    step(dve.tensor_tensor(win[:, :, 2], win[:, :, 2], win[:, :, 0], ALU.is_gt))
                    step(dve.tensor_tensor(win[:, :, 2], win[:, :, 2], win[:, :, 1], ALU.is_gt))
                    step(dve.tensor_tensor(wc[:, :, :], win[:, :, :], sg[:, :, 0:3], ALU.mult))
                    step(dve.tensor_reduce(bmax[:, :], wc[:, :, :], AX, ALU.add))
                    step(dve.tensor_scalar(wcs[:, :], bmax[:, :], 1e-6, None, ALU.add))
                    step(dve.reciprocal(wcs[:, :], wcs[:, :]))
                    step(dve.tensor_tensor(wcs[:, :], wcs[:, :], bmax[:, :], ALU.mult))
                    step(dve.tensor_tensor(coef[:, :, :], win[:, :, :], wcs[:, :].unsqueeze(2)
                                           .to_broadcast([P, NT, 3]), ALU.mult))
                    pace("n_trans")
                    def add_expert(uses, e):
                        for t in range(NT):
                            b = bank_of[uses[t // 2]]
                            if t % 2 == 0:
                                take(dve, j, uses[t // 2])
                            ins = dve.scalar_tensor_tensor(out=hA[:, t, :], in0=b.t[:, t % 2 * C:(t % 2 + 1) * C],
                                                           scalar=coef[:, t, e:e + 1], in1=hA[:, t, :],
                                                           op0=ALU.mult, op1=ALU.add)
                            if t % 2:
                                ins.then_inc(b.free, 1)
                        for use in uses:
                            used(dve, j, use)

                    add_expert(["tr0", "tr1"], 2)
                    for e in range(2):
                        for k in range(NHB):
                            use = f"{'op'[e]}{k}"
                            b = bank_of[use]
                            dve.wait_ge(d_rl.sem, d_rl.at(j, NHB * e + k + 1))
                            dve.tensor_tensor(hid[:, k % HB, :], hid[:, k % HB, :], b.t[:, :], ALU.mult)\
                               .then_inc(b.free, 1)
                            pace(use)
                        add_expert([f"e{e}_0", f"e{e}_1"], e)
                        pace("o_out" if e == 0 else "p7")
                    step(dve.tensor_tensor(hA[:, :, :], hA[:, :, :], per_tile(m_d("gB1")), ALU.mult))
                    pace("scaled")
                    dve.tensor_tensor(xd[:, :, :], xd[:, :, :], hA[:, :, :], ALU.add).then_inc(d_x5.sem, 1)
                    pace("q_out")
                    own.end()

                Pace(PACE["dve"], front, unit, tail, 0).upto(len(S_STEPS))
                with dve.Fori(1, NCH) as i:
                    dense(i - 1, Pace(PACE["dve"], front, unit, tail, i))
                dense(NCH - 1, Pace(PACE["dve"], None, None, None, NCH))

            @block.tensor
            def _(pe):
                def turn(dst, src):
                    return pe.transpose(dst, src, ident[:, :])

                def split3(dst, lh, ll, rh, rl):
                    prods = [(a, b) for k in range(len(lh)) for a, b in ((lh[k], rh[k]), (lh[k], rl[k]), (ll[k], rh[k]))]
                    for n, (a, b) in enumerate(prods):
                        last = pe.matmul(dst, a, b, start=n == 0, stop=n == len(prods) - 1)
                    return last

                def front(i, step, k):
                    if step == "turn":
                        pe.wait_ge(s_n.sem, s_n.at(i, 2))
                        for c in range(KC):
                            b = fill(pe, i, f"xn{c}")
                            for t in range(NT):
                                last = turn(b.t[:, t * P:(t + 1) * P], n0[:, t, c * P:(c + 1) * P])
                            last.then_inc(b.full, 1)
                    if step == "z":
                        pe.wait_ge(s_xnl.sem, s_xnl.at(i, KC))
                        b = fill(pe, i, f"z{k}")
                        split3(b.t[:, :], [w_in["h"][:, c, k * P:(k + 1) * P] for c in range(KC)],
                               [w_in["l"][:, c, k * P:(k + 1) * P] for c in range(KC)],
                               [xnh[:, c, :] for c in range(KC)], [xnl[:, c, :] for c in range(KC)])\
                            .then_inc(b.full, 1)
                    if step == "gate":
                        b = fill(pe, i, f"gt{k}")
                        tok = slice(k * P, (k + 1) * P)
                        if k == 2:
                            bct = fill(pe, i, "ct")
                            used(pe, i, "bc")
                        split3(b.t[:, :], [xnh[:, c, tok] for c in range(KC)], [xnl[:, c, tok] for c in range(KC)],
                               [w_in["h"][:, c, DI:2 * DI] for c in range(KC)],
                               [w_in["l"][:, c, DI:2 * DI] for c in range(KC)]).then_inc(b.full, 1)
                        if k == 2:
                            for t in range(NT):
                                last = pe.transpose(bct.t[:, t * 2 * DS:(t + 1) * 2 * DS],
                                                    bcs[:, t * P:(t + 1) * P], ident[0:2 * DS, 0:2 * DS])
                            last.then_inc(bct.full, 1)
                    if step == "bc":
                        used(pe, i, "z3")
                        b = fill(pe, i, "bc")
                        for c in range(DB):
                            last = pe.matmul(b.t[0:2 * DS, :], w_bc[:, c, :], z[:, c, :], start=c == 0, stop=c == DB - 1)
                        last.then_inc(b.full, 1)
                    if step == "dt":
                        pe.wait_ge(s_zl.sem, s_zl.at(i, DB))
                        b = fill(pe, i, f"dt{k}")
                        split3(b.t[:, :], [w_dt["h"][:, c, k * P:(k + 1) * P] for c in range(DB)],
                               [w_dt["l"][:, c, k * P:(k + 1) * P] for c in range(DB)],
                               [zh[:, c, :] for c in range(DB)], [zl[:, c, :] for c in range(DB)])\
                            .then_inc(b.full, 1)

                def unit(i, u):
                    s, t = u // DB - 1, u % DB
                    if s < 0:
                        return
                    use = f"hT{s * NT + t}"
                    b = fill(pe, i, use)
                    if t == 0:
                        for n in (s * DB + DB - 2, s * DB + DB - 1):
                            used(pe, i, f"dA{n}")
                    for d in range(DB):
                        last = turn(b.t[:, d * P:(d + 1) * P], hs[:, s % 2, d, t * P:(t + 1) * P])
                    last.then_inc(b.full, 1)

                def tail(i, step, k):
                    if step == "y":
                        pe.wait_ge(s_yg.sem, s_yg.at(i, 1))
                        b = fill(pe, i, f"y{k}")
                        for t in range(NT):
                            last = turn(b.t[:, t * P:(t + 1) * P], acc[:, t, k * P:(k + 1) * P])
                        last.then_inc(b.full, 1)
                    if step == "out":
                        used(pe, i, "y3")
                        by_token(i, [f"wo{k}"], z, w_out, DB, [k])

                def by_token(j, uses, act, wt, kb, pairs=(0, 1), pace=None):
                    for use, p in zip(uses, pairs):
                        b = fill(pe, j, use)
                        for t in (2 * p, 2 * p + 1):
                            for k in range(kb):
                                last = pe.matmul(b.t[:, t % 2 * C:(t % 2 + 1) * C], act[:, k, t * P:(t + 1) * P],
                                                 wt[:, k, :], start=k == 0, stop=k == kb - 1)
                        last.then_inc(b.full, 1)
                        if pace:
                            pace(use)

                def turns(j, uses, src, pace):
                    for k in range(KC):
                        b = fill(pe, j, uses[k])
                        for t in range(NT):
                            last = turn(b.t[:, t * P:(t + 1) * P], src[:, t, k * P:(k + 1) * P])
                        last.then_inc(b.full, 1)
                        pace(uses[k])

                def parts(j, k):
                    pe.wait_ge(d_fl.sem, d_fl.at(j, KC * (k + 1)))

                def from_f(j, use, wh, wl, lo, hi):
                    b = fill(pe, j, use)
                    return b, split3(b.t[:, :], [wh[:, k, lo:hi] for k in range(KC)], [wl[:, k, lo:hi] for k in range(KC)],
                                     [fh[:, k, :] for k in range(KC)], [fl[:, k, :] for k in range(KC)])

                def logits_ready(j, use, use_t):
                    fill(pe, j, use_t)
                    used(pe, j, use)

                def logits_by_token(use_t):
                    b = bank_of[use_t]
                    for t in range(NT):
                        last = pe.transpose(b.t[:, t * 8:(t + 1) * 8], rows8[:, t * P:(t + 1) * P], ident[0:8, 0:8])
                    last.then_inc(b.full, 1)

                def hidden(j, name, slots, outs, pace):
                    def up(k):
                        if k % HB == 0:
                            slot_ready(pe, j, slots[k // HB])
                        wt = ws_in[SLOTS.index(slots[k // HB]) % 2]
                        c = k % HB
                        b, last = from_f(j, f"{name}{k}", wt[:, 0], wt[:, 1], c * P, (c + 1) * P)
                        last.then_inc(b.full, 1)
                        pace(f"{name}{k}_up")

                    def down(k):
                        used(pe, j, f"{name}{k}")
                        wt = ws_out[SLOTS.index(slots[k // HB]) % 2]
                        for t in range(NT):
                            b = bank_of[outs[t // 2]]
                            if k == 0 and t % 2 == 0:
                                fill(pe, j, outs[t // 2])
                            last = pe.matmul(b.t[:, t % 2 * C:(t % 2 + 1) * C], hid[:, k % HB, t * P:(t + 1) * P],
                                             wt[:, k % HB, :], start=k == 0 and t % 2 == 0,
                                             stop=k == NHB - 1, skip_group_check=True)
                            if k == NHB - 1 and t % 2:
                                last.then_inc(b.full, 1)
                        if k < NHB - 1:
                            last.then_inc(d_hfree.sem, 1)
                        pace(f"{name}{k}")

                    up(0)
                    if name == "c":
                        logits_by_token("routerT")
                    for k in range(NHB):
                        if k < NHB - 1:
                            up(k + 1)
                        down(k)

                def dense(j, pace):
                    pace("a_norm")
                    pe.wait_ge(d_h.sem, d_h.at(j, 1))
                    turns(j, ["h1T0", "h1T1"], hA, pace)
                    parts(j, 0)
                    b, last = from_f(j, "router", w_rt["h"], w_rt["l"], 0, P)
                    last.then_inc(b.full, 1)
                    logits_ready(j, "router", "routerT")
                    pace("b_router")
                    hidden(j, "c", ["ffn_0", "ffn_1"], ["ffn0", "ffn1"], pace)
                    pace("e_norm")
                    pe.wait_ge(d_h.sem, d_h.at(j, 2))
                    turns(j, ["h2T0", "h2T1"], hA, pace)
                    used(pe, j, "h2T1")
                    for t in range(NT):
                        b = fill(pe, j, f"kq{t}")
                        for k in range(KC):
                            last = pe.matmul(b.t[:, 0:NQ], ff[:, k, t * P:(t + 1) * P], w_kq[:, k, :],
                                             start=k == 0, stop=k == KC - 1)
                        last.then_inc(b.full, 1)
                        pace(f"kq{t}")
                    pace("f_kv")
                    used(pe, j, "kq2")
                    used(pe, j, "kq3")
                    turns(j, ["kvT0", "kvT1"], nn, pace)
                    pe.wait_ge(d_bx.sem, d_bx.at(j, 2))
                    turns(j, ["btT0", "btT1"], bx, pace)
                    turns(j, ["qsT0", "qsT1"], qx, pace)
                    pace("g_scan")
                    used(pe, j, "qsT1")
                    by_token(j, ["ao0", "ao1"], cb, w_ao, KC, pace=pace)
                    pace("i_norm2")
                    pe.wait_ge(d_n.sem, d_n.at(j, 5))
                    turns(j, ["xlT0", "xlT1"], nn, pace)
                    parts(j, 1)
                    slot_ready(pe, j, "rv")
                    rv, sw = ws_in[SLOTS.index("rv") % 2], ws_in[SLOTS.index("sw") % 2]
                    for k in range(KC):
                        b, last = from_f(j, f"r{k}", rv[:, 0], rv[:, 1], k * P, (k + 1) * P)
                        last.then_inc(b.full, 1)
                        pace(f"r{k}")
                        b, last = from_f(j, f"v{k}", rv[:, 0], rv[:, 1], C + k * P, C + (k + 1) * P)
                        last.then_inc(b.full, 1)
                        pace(f"v{k}")
                    slot_ready(pe, j, "sw")
                    for k in range(KC):
                        b, last = from_f(j, f"s{k}", sw[:, 0], sw[:, 1], k * P, (k + 1) * P)
                        last.then_inc(b.full, 1)
                        pace(f"s{k}")
                    used(pe, j, "v0")
                    used(pe, j, "v1")
                    by_token(j, ["att0", "att1"], cb, w_fo, KC, pace=pace)
                    used(pe, j, "s1")
                    for m in range(KC):
                        b = fill(pe, j, f"sW{m}")
                        for k in range(KC):
                            last = pe.matmul(b.t[:, :], w_2[:, k, m * P:(m + 1) * P], ca[:, k, :],
                                             start=k == 0, stop=k == KC - 1)
                        last.then_inc(b.full, 1)
                        pace(f"sW{m}")
                    pace("m_norm")
                    pe.wait_ge(d_n.sem, d_n.at(j, 6))
                    turns(j, ["hhT0", "hhT1"], nn, pace)
                    parts(j, 2)
                    b, last = from_f(j, "bids", w_bd["h"], w_bd["l"], 0, P)
                    last.then_inc(b.full, 1)
                    pace("bids")
                    logits_ready(j, "bids", "bidsT")
                    for k in range(KC):
                        b, last = from_f(j, f"tw{k}", sw[:, 0], sw[:, 1], C + k * P, C + (k + 1) * P)
                        last.then_inc(b.full, 1)
                        if k == 0:
                            logits_by_token("bidsT")
                        pace(f"tw{k}")
                    used(pe, j, "tw1")
                    by_token(j, ["tr0", "tr1"], cb, w_3, KC, pace=pace)
                    hidden(j, "o", ["e0_0", "e0_1"], ["e0_0", "e0_1"], pace)
                    pace("o_out")
                    hidden(j, "p", ["e1_0", "e1_1"], ["e1_0", "e1_1"], pace)
                    pace("q_out")

                Pace(PACE["pe"], front, unit, tail, 0).upto(len(S_STEPS))
                with pe.Fori(1, NCH) as i:
                    dense(i - 1, Pace(PACE["pe"], front, unit, tail, i))
                dense(NCH - 1, Pace(PACE["pe"], None, None, None, NCH))


OWN = {"dve_s": 25, "dve_d": 54, "pool_s": 4, "pool_d": 10, "act_s": 4}


def kernel(**inputs):
    import numpy as _np
    import concourse.bacc as _bacc
    from concourse import mybir as _mybir
    from concourse.bass_utils import run_bass_kernel_spmd as _run

    nc = _bacc.Bacc("TRN2", target_bir_lowering=False, num_devices=1)
    unused = {"L1_ffn_v_first"}
    arrays, args = {}, {}
    for name in inputs:
        if name in unused:
            continue
        a = _np.ascontiguousarray(inputs[name])
        arrays[f"in_{name}"] = a
        args[name] = nc.dram_tensor(f"in_{name}", a.shape, _mybir.dt.from_np(a.dtype), kind="ExternalInput").ap()
    out = nc.dram_tensor("out_0", (B, T, C), F32, kind="ExternalOutput").ap()
    build(nc, args, out)
    r = _run(nc, [arrays], core_ids=[0])
    return r.results[0]["out_0"]
```

```python
from contextlib import ExitStack

import concourse.bass as bass
from concourse import mybir

F32 = mybir.dt.float32
F32R = mybir.dt.float32r
I32 = mybir.dt.int32
ALU = mybir.AluOpType
ACT = mybir.ActivationFunctionType
AX = mybir.AxisListType.X

P = 128
B, T, C = 4, 2048, 256
CT = 512
NT = CT // P
NCH = B * T // CT
CPB = T // CT
KC = C // P
DI, DS = 512, 16
DB = DI // P
F = 1024
NH, HD = 16, 16
E_MOE = 8
EPS = 1e-5
DT_MIN, DT_MAX = 0.001, 1.0
DT_CLAMP = 20.0
GATE_MIN = 0.25
NQ = C + 3 * NH

ROWS = ["cA0", "sA0", "gA0", "cB0", "sB0", "gB0", "cA1", "sA1", "gA1w", "gA1b", "cB1", "sB1", "gB1"]
ROW = {name: k for k, name in enumerate(ROWS)}
NROW_S = 3
NROW_D = len(ROWS) - NROW_S

SLOTS = ["ffn_0", "ffn_1", "rv", "sw", "e0_0", "e0_1", "e1_0", "e1_1"]
NSLOT = len(SLOTS)
CREDIT = 1
HB = F // 2 // P
NHB = F // P

SSM_UNITS = DS * DB + DB
FRONT_STEPS = [("mean", 0), ("norm", 0), ("mean", 1), ("norm", 1), ("turn", 0)] + [("z", d) for d in range(DB)] \
    + [("gate", 0), ("gate", 1), ("bc", 0), ("gate", 2), ("gate", 3)] + [("dt", d) for d in range(DB)] \
    + [("softplus", 0)] + [("clip", d) for d in range(DB)]
TAIL_STEPS = [("gated", 0)] + [("y", k) for k in range(DB)] + [("out", 0), ("out", 1), ("x1", 0)]
S_STEPS = [("front",) + step for step in FRONT_STEPS] + [("unit", u) for u in range(SSM_UNITS)] \
    + [("tail",) + step for step in TAIL_STEPS]

PACE = {
    "sp": {
        "k_proj": 20, "n_trans": 33, "o3": 54, "o7": 70, "p3": 83, "q_out": 86, "load_ffn_1": 87, "c3": 87,
        "c7": 89, "load_sw": 99,
    },
    "pool": {
        "rstd1": 2, "f_kv": 7, "h_bias": 8, "rstd2": 16, "rstd3": 19, "rstd4": 27, "rstd5": 54, "q_out": 77,
        "rstd0": 99,
    },
    "act": {
        "f_turn": 1, "h2T0": 1, "h2T1": 1, "f_kv": 1, "beta": 1, "q": 3, "kvT0": 3, "kvT1": 6, "j_turn": 13,
        "xlT0": 14, "xlT1": 16, "xlT0_high": 17, "xlT1_high": 21, "r0": 21, "r1": 24, "s0": 26, "s1": 28,
        "sW0": 28, "sW1": 29, "hhT0": 29, "hhT1": 29, "hhT0_high": 29, "hhT1_high": 33, "bids": 35, "o0": 37,
        "o1": 40, "o2": 42, "o3": 44, "o4": 48, "o5": 48, "o6": 50, "o7": 54, "p0": 56, "p1": 57, "p2": 61,
        "p3": 63, "p4": 69, "p5": 70, "p6": 72, "p7": 73, "q_out": 77, "b_turn": 78, "h1T0": 78, "h1T1": 78,
        "h1T0_high": 78, "h1T1_high": 81, "router": 84, "b_router": 84, "c0": 84, "c1": 87, "c2": 87,
        "c3": 87, "c4": 88, "c5": 90, "c6": 90, "c7": 99,
    },
    "dve": {
        "e_stats": 0, "e_norm": 1, "f_turn": 2, "kq0": 2, "kq1": 2, "kq2": 2, "kq3": 2, "f_kv": 4,
        "g_turn": 4, "qsT0": 4, "scan0": 4, "qsT1": 5, "g_scan": 5, "ao0": 5, "ao1": 5, "h_out": 5,
        "h_stats": 7, "h_norm": 7, "i_stats": 9, "i_norm": 10, "i_stats2": 13, "i_norm2": 14, "j_turn": 16,
        "low1_0": 19, "low1_1": 22, "k_proj": 23, "v0": 23, "v1": 24, "l_out": 25, "att0": 26, "att1": 26,
        "m_stats": 27, "m_norm": 28, "m_turn": 29, "low2_0": 29, "low2_1": 30, "n_bids": 33, "tw0": 33,
        "tw1": 34, "product": 34, "n_trans": 35, "tr_out": 51, "o_out": 73, "p_out": 73, "scaled": 73,
        "q_out": 74, "a_stats": 75, "a_norm": 75, "b_turn": 77, "low0_0": 77, "low0_1": 82, "b_router": 94,
        "prob": 94, "ffn0": 94, "ffn1": 94, "ffn_scaled": 95, "d_x2": 99,
    },
    "pe": {
        "e_norm": 0, "h2T0": 0, "h2T1": 0, "kq0": 0, "kq1": 0, "kq2": 2, "kq3": 2, "f_kv": 2, "kvT0": 2,
        "kvT1": 2, "btT0": 3, "btT1": 3, "qsT0": 4, "qsT1": 4, "g_scan": 5, "ao0": 5, "ao1": 6, "i_norm2": 16,
        "xlT0": 16, "xlT1": 21, "r0": 21, "v0": 21, "r1": 21, "v1": 21, "s0": 21, "s1": 21, "att0": 21,
        "att1": 25, "sW0": 25, "sW1": 26, "m_norm": 29, "hhT0": 29, "hhT1": 31, "bids": 33, "tw0": 33,
        "tw1": 35, "tr0": 35, "tr1": 35, "o0_up": 35, "o1_up": 36, "o0": 37, "o2_up": 38, "o1": 39,
        "o3_up": 40, "o2": 42, "o4_up": 43, "o3": 44, "o5_up": 46, "o4": 46, "o6_up": 48, "o5": 48,
        "o7_up": 50, "o6": 51, "o7": 53, "o_out": 53, "p0_up": 53, "p1_up": 54, "p0": 56, "p2_up": 57,
        "p1": 58, "p3_up": 60, "p2": 61, "p4_up": 63, "p3": 65, "p5_up": 66, "p4": 67, "p6_up": 69, "p5": 71,
        "p7_up": 72, "p6": 73, "p7": 76, "q_out": 76, "a_norm": 76, "h1T0": 76, "h1T1": 79, "b_router": 81,
        "c0_up": 82, "c1_up": 85, "c0": 86, "c2_up": 86, "c1": 87, "c3_up": 89, "c2": 90, "c4_up": 90,
        "c3": 91, "c5_up": 92, "c4": 92, "c6_up": 92, "c5": 94, "c7_up": 96, "c6": 96, "c7": 99,
    },
}

FRONT = ["xn0", "xn1", "z0", "z1", "z2", "z3", "gt0", "gt1", "bc", "gt2", "ct", "gt3", "dt0", "dt1", "dt2", "dt3"]
TAIL = ["y0", "y1", "y2", "y3", "wo0", "wo1"]
SCAN_BANKS = ["A0", "A1", "H0", "H1"]
BANK_USES = {
    "A0": FRONT[0::4] + [f"dA{u}" for u in range(0, DS * DB, 2)] + TAIL[0::4],
    "A1": FRONT[1::4] + [f"dA{u}" for u in range(1, DS * DB, 2)] + TAIL[1::4],
    "H0": FRONT[2::4] + [f"hT{u}" for u in range(0, DS * NT, 2)] + TAIL[2::4],
    "H1": FRONT[3::4] + [f"hT{u}" for u in range(1, DS * NT, 2)] + TAIL[3::4],
    "B0": ["h1T0"] + [f"c{k}" for k in (0, 2, 4, 6)] + ["h2T0", "kvT0", "qsT0", "xlT0", "r0", "s0", "sW0", "hhT0", "tw0"]
          + [f"o{k}" for k in (0, 2, 4, 6)] + [f"p{k}" for k in (0, 2, 4, 6)],
    "B1": ["h1T1"] + [f"c{k}" for k in (1, 3, 5, 7)] + ["h2T1", "kvT1", "qsT1", "xlT1", "r1", "s1", "sW1", "hhT1", "tw1"]
          + [f"o{k}" for k in (1, 3, 5, 7)] + [f"p{k}" for k in (1, 3, 5, 7)],
    "B2": ["router", "ffn0", "kq0", "kq2", "btT0", "ao0", "v0", "att0", "bids", "tr0", "e0_0", "e1_0"],
    "B3": ["routerT", "ffn1", "kq1", "kq3", "btT1", "ao1", "v1", "att1", "bidsT", "tr1", "e0_1", "e1_1"],
}


class Bank:

    def __init__(self, tensor, full, free, uses):
        self.t, self.full, self.free, self.uses = tensor, full, free, uses

    def fills_before(self, chunk, use):
        return chunk * len(self.uses) + self.uses.index(use) + CREDIT

    def fills_with(self, chunk, use):
        return self.fills_before(chunk, use) + 1


class Signal:

    def __init__(self, sem, n, credit=0):
        self.sem, self.n, self.credit = sem, n, credit

    def at(self, chunk, k):
        return chunk * self.n + k + self.credit


class Own:

    def __init__(self, eng, sig, chunk):
        self.eng, self.sig, self.chunk, self.k = eng, sig, chunk, 0

    def mark(self, instruction):
        self.k += 1
        instruction.then_inc(self.sig.sem, 1)
        return self.k

    def wait(self, k=None):
        self.eng.wait_ge(self.sig.sem, self.sig.at(self.chunk, self.k if k is None else k))

    def step(self, instruction):
        self.mark(instruction)
        self.wait()

    def end(self):
        assert self.k == self.sig.n, f"{self.k} own steps, {self.sig.n} stated"


class Pace:

    def __init__(self, pace, front, unit, tail, chunk):
        self.pace, self.front, self.unit, self.tail, self.chunk, self.at = pace, front, unit, tail, chunk, 0

    def __call__(self, name):
        self.upto(self.pace[name])

    def upto(self, n):
        while self.front is not None and self.at < n:
            part, *step = S_STEPS[self.at]
            {"front": self.front, "unit": self.unit, "tail": self.tail}[part](self.chunk, *step)
            self.at += 1


def since(eng, sig, chunk, k=0):
    if not (isinstance(chunk, int) and chunk == 0 and k == 0):
        eng.wait_ge(sig.sem, sig.at(chunk, k))


def build(nc, w, out):
    ctx = ExitStack()
    with ctx:
        ctx.enter_context(nc.allow_non_contiguous_dma("small constants, column by column"))
        place = [(nc.sbuf_base + 63) // 64 * 64]

        def sb(name, shape, dt=F32):
            size = 4
            for n in shape[1:]:
                size *= n
            t = nc.alloc_sbuf_tensor_at(name, list(shape), dt, offset=place[0])
            where[name] = place[0]
            place[0] += (size + 31) // 32 * 32
            return t

        def over(name, shape, at, dt=F32):
            return nc.alloc_sbuf_tensor_at(name, list(shape), dt, offset=where[at])

        where = {}

        def sem(name):
            return ctx.enter_context(nc.semaphore(name))

        credited = []

        def signal(name, n, credit=0):
            sig = Signal(sem(name), n, credit)
            if credit:
                credited.append(sig.sem)
            return sig

        w_in = {h: sb(f"w_in_{h}", [P, KC, 2 * DI], F32R) for h in "hl"}
        w_dt = {h: sb(f"w_dt_{h}", [P, DB, DI], F32R) for h in "hl"}
        w_bc = sb("w_bc", [P, DB, 2 * DS])
        w_out = sb("w_out", [P, DB, C])
        w_kq = sb("w_kq", [P, KC, NQ])
        w_ao = sb("w_ao", [P, KC, C])
        w_fo = sb("w_fo", [P, KC, C])
        w_2 = sb("w_2", [P, KC, C])
        w_3 = sb("w_3", [P, KC, C])
        w_rt = {h: sb(f"w_rt_{h}", [P, KC, P], F32R) for h in "hl"}
        w_bd = {h: sb(f"w_bd_{h}", [P, KC, P], F32R) for h in "hl"}
        ws_in = [sb(f"ws_in{k}", [P, 2, KC, HB * P], F32R) for k in range(2)]
        ws_out = [sb(f"ws_out{k}", [P, HB, C]) for k in range(2)]
        xnh = sb("xnh", [P, KC, CT], F32R)
        xnl = sb("xnl", [P, KC, CT], F32R)
        xnf = over("xnf", [P, KC, CT], "xnl")
        bu = over("bu", [P, 4, CT], "xnh")
        zh = sb("zh", [P, DB, CT], F32R)
        zl = sb("zl", [P, DB, CT], F32R)
        hs = over("hs", [P, 2, DB, CT], "zh")
        stage = [over("stage0", [P, 2048], "zh"), over("stage1", [P, 2048], "zl")]
        z = sb("z", [P, DB, CT])
        dt = sb("dt", [P, DB, CT])
        modrow = over("modrow", [B, len(ROWS) * C], "z")
        gate = sb("gate", [P, NT, DI])
        acc = sb("acc", [P, NT, DI])
        wm = over("wm", [P, KC, 6 * C], "gate")
        h0 = over("h0", [P, NT, C], "acc")
        where["acc_hi"] = where["acc"] + 4 * NT * C
        n0 = over("n0", [P, NT, C], "acc_hi")
        bb = sb("bb", [P, 4, CT])
        modraw = over("modraw", [B, 6 * C], "bb")
        fh = sb("fh", [P, KC, CT], F32R)
        fl = sb("fl", [P, KC, CT], F32R)
        ff = over("ff", [P, KC, CT], "fl")
        bx = over("bx", [P, NT, C], "fh")
        ca = sb("ca", [P, KC, CT])
        cb = sb("cb", [P, KC, CT])
        hid = sb("hid", [P, HB, CT])
        qx = over("qx", [P, NT, C], "hid")
        xin = sb("xin", [P, NT, C])
        x1 = sb("x1", [P, NT, C])
        hA = sb("hA", [P, NT, C])
        nn = sb("nn", [P, NT, C])
        xd = sb("xd", [P, NT, C])
        mod_s = sb("mod_s", [P, NROW_S, C])
        mod_d = sb("mod_d", [P, NROW_D, C])
        b2_row = sb("b2_row", [P, C])
        bo_row = sb("bo_row", [P, C])
        ident = sb("ident", [P, P])
        rows8 = sb("rows8", [8, CT])
        bcs = sb("bcs", [2 * DS, CT])
        ctok = sb("ctok", [P, NT, 2 * DS])
        a_neg = sb("a_neg", [P, DB, DS])
        state = sb("state", [P, DS, DB])
        state_l = sb("state_l", [P, KC])
        keep = sb("keep", [P, NCH], I32)
        mhalf = sb("mhalf", [P, NT])
        cols = sb("cols", [P, 16])
        bdt_col = sb("bdt_col", [P, DB])
        b1_col = sb("b1_col", [P, F // P])
        bbeta_row = sb("bbeta_row", [P, NH])
        cs_row = sb("cs_row", [P, 3])
        c_in = over("c_in", [B, 2 * C], "xd")
        c_t = sb("c_t", [P, 2, KC, B])
        lnw_row = over("lnw_row", [B, 2 * C], "nn")
        st_s, mv_s, rs_s = sb("st_s", [P, NT, 6]), sb("mv_s", [P, NT, 2]), sb("rs_s", [P, NT])
        st_d, mv_d, rs_d = sb("st_d", [P, NT, 6]), sb("mv_d", [P, NT, 2]), sb("rs_d", [P, NT])
        carrier = sb("carrier", [P, 2])
        lg = sb("lg", [P, NT, E_MOE])
        lg_m = sb("lg_m", [P, NT])
        prob = sb("prob", [P, NT])
        sm = sb("sm", [P, NT, 3 * NH])
        bl = sb("bl", [P, NT, 8])
        sg = sb("sg", [P, NT, 4])
        bid = sb("bid", [P, NT, 3])
        bmax = sb("bmax", [P, NT])
        win = sb("win", [P, NT, 3])
        wc = sb("wc", [P, NT, 3])
        wcs = sb("wcs", [P, NT])
        coef = sb("coef", [P, NT, 3])
        assert place[0] <= nc.sbuf_usable_end, place[0]

        w_split = nc.dram_tensor("w_split", (NSLOT, P, 2 * KC * HB * P), F32, kind="Internal").ap()
        mods = nc.dram_tensor("mods", (NCH, len(ROWS) * C), F32, kind="Internal").ap()
        b_rows = nc.dram_tensor("b_rows", (DS, CT), F32, kind="Internal").ap()

        psum = {name: ctx.enter_context(nc.psum_tensor(f"ps_{name}", [P, CT], F32)) for name in BANK_USES}
        bank = {name: Bank(psum[name], sem(f"full_{name}"), sem(f"free_{name}"), uses)
                for name, uses in BANK_USES.items()}
        bank_of = {use: bank[name] for name in BANK_USES for use in BANK_USES[name]}

        def fill(eng, chunk, use):
            b = bank_of[use]
            n = b.fills_before(chunk, use)
            if not (isinstance(n, int) and n == CREDIT):
                eng.wait_ge(b.free, n)
            return b

        def take(eng, chunk, use):
            b = bank_of[use]
            eng.wait_ge(b.full, b.fills_with(chunk, use))
            return b

        def used(eng, chunk, use):
            b = bank_of[use]
            eng.wait_ge(b.free, b.fills_with(chunk, use))

        def kp(ap):
            return ap.rearrange("(k p) m -> p k m", p=P)

        def col(ap):
            return ap.rearrange("(k p) -> p k", p=P)

        def row(ap):
            return ap.rearrange("(a n) -> a n", a=1)

        s_xin = signal("s_xin", 16)
        s_mods = signal("s_mods", 16)
        s_modd = [signal(f"s_modd{k}", 16) for k in range(3)]
        s_bw = signal("s_bw", 16)
        s_bb = [signal(f"s_bb{k}", 16 * DS // 4) for k in range(4)]
        s_w = [signal(f"s_w{k}", 0) for k in range(2)]
        s_out = signal("s_out", 16, CREDIT)
        s_mv = signal("s_mv", 2)
        s_rs = signal("s_rs", 2)
        s_n = signal("s_n", 1)
        s_h0 = signal("s_h0", 1)
        s_xg = signal("s_xg", 1)
        s_xnh = signal("s_xnh", KC)
        s_xnl = signal("s_xnl", KC)
        s_zh = signal("s_zh", DB)
        s_zl = signal("s_zl", DB)
        s_sp = signal("s_sp", DB)
        s_dt = signal("s_dt", DB)
        s_u = signal("s_u", DB)
        s_bu = signal("s_bu", DS * DB)
        s_yg = signal("s_yg", 1)
        s_x1 = signal("s_x1", 1, CREDIT)
        d_mv = signal("d_mv", 6)
        d_rs = signal("d_rs", 6)
        d_n = signal("d_n", 2)
        d_h = signal("d_h", 3)
        d_fh = signal("d_fh", 3 * KC)
        d_fl = signal("d_fl", 3 * KC)
        d_lsub = signal("d_lsub", 1)
        d_lexp = signal("d_lexp", 1)
        d_sq = signal("d_sq", 2 * NHB)
        d_hfree = signal("d_hfree", 3 * (NHB - 1), CREDIT)
        d_x2 = signal("d_x2", 1, CREDIT)
        d_sm = signal("d_sm", 1)
        d_bx = signal("d_bx", 2)
        d_hb = signal("d_hb", 1)
        d_xb = signal("d_xb", 1)
        d_x3 = signal("d_x3", 1, CREDIT)
        d_sg = signal("d_sg", 1)
        d_x5 = signal("d_x5", 1, CREDIT)
        o_dve_s = signal("o_dve_s", OWN["dve_s"])
        o_dve_f = signal("o_dve_f", OWN["dve_f"])
        o_dve_d = signal("o_dve_d", OWN["dve_d"])
        o_pool_s = signal("o_pool_s", OWN["pool_s"])
        o_act_s = signal("o_act_s", OWN["act_s"])

        u_load = sem("u_load")
        u_c = sem("u_c")
        u_stage = [sem("u_stage0"), sem("u_stage1")]
        u_wm = sem("u_wm")
        u_split = sem("u_split")
        u_store = [sem("u_store0"), sem("u_store1")]
        u_dve = sem("u_dve")
        u_id = sem("u_id")
        u_silu = sem("u_silu")
        u_exp = sem("u_exp")
        u_ct = sem("u_ct")
        u_ctc = sem("u_ctc")
        u_mm = sem("u_mm")
        u_raw = sem("u_raw")
        u_rows = sem("u_rows")
        u_sum = sem("u_sum")
        u_zero = sem("u_zero")
        u_mods = sem("u_mods")
        u_wsm = sem("u_wsm")

        e_last = E_MOE - 1
        k_r, v_r = w["L1_ffn_K_rwkv"], w["L1_ffn_V_rwkv"]
        pieces = [
            [(0, DI, kp(w["L0_attn_W_in"])), (DI, DI, kp(w["L0_attn_W_gate"]))],
            [(0, DI, kp(w["L0_attn_W_dt"]))],
            [(0, HB * P, kp(w["L0_ffn_W1"][e_last])[:, :, 0:HB * P])],
            [(0, HB * P, kp(w["L0_ffn_W1"][e_last])[:, :, HB * P:F])],
            [(0, C, kp(w["L1_ffn_Wr"])), (C, C, kp(w["L1_ffn_Wv"]))],
            [(0, C, kp(w["L1_ffn_Ws"])), (C, C, kp(w["L1_ffn_W1"]))],
            [(0, HB * P, kp(k_r[0])[:, :, 0:HB * P])],
            [(0, HB * P, kp(k_r[0])[:, :, HB * P:F])],
            [(0, HB * P, kp(k_r[1])[:, :, 0:HB * P])],
            [(0, HB * P, kp(k_r[1])[:, :, HB * P:F])],
        ]
        shapes = [(KC, 2 * DI), (DB, DI)] + [(KC, HB * P)] * NSLOT
        w_down = {"ffn_0": w["L0_ffn_W2"][e_last][0:HB * P], "ffn_1": w["L0_ffn_W2"][e_last][HB * P:F],
                  "e0_0": v_r[0][0:HB * P], "e0_1": v_r[0][HB * P:F],
                  "e1_0": v_r[1][0:HB * P], "e1_1": v_r[1][HB * P:F]}

        def staged(n, shape):
            k, m = shape
            return stage[n % 2][:, 0:k * m].rearrange("p (k m) -> p k m", k=k)

        small = [
            (w_bc[:, :, 0:DS], kp(w["L0_attn_W_C"])), (w_bc[:, :, DS:2 * DS], kp(w["L0_attn_W_B"])),
            (w_out[:, :, :], kp(w["L0_attn_W_out"])), (w_kq[:, :, 0:C], kp(w["L1_attn_Wk"])),
            (w_kq[:, :, C + 2 * NH:NQ], kp(w["L1_attn_Wbeta"])), (w_ao[:, :, :], kp(w["L1_attn_Wo"])),
            (w_fo[:, :, :], kp(w["L1_ffn_Wo"])), (w_2[:, :, :], kp(w["L1_ffn_W2"])),
            (w_3[:, :, :], kp(w["L1_ffn_W3"])),
            (cols[:, 0:2], col(w["L0_attn_norm_w"])), (cols[:, 2:4], col(w["L0_attn_norm_b"])),
            (cols[:, 4:6], col(w["L1_ffn_ln1_w"])), (cols[:, 6:8], col(w["L1_ffn_ln1_b"])),
            (cols[:, 8:10], col(w["L1_ffn_ln2_w"])), (cols[:, 10:12], col(w["L1_ffn_ln2_b"])),
            (bdt_col[:, :], col(w["L0_attn_b_dt"])), (b1_col[:, :], col(w["L0_ffn_b1"][e_last])),
            (bbeta_row[:, :], row(w["L1_attn_b_beta"]).to_broadcast([P, NH])),
            (cs_row[:, :], row(w["L1_ffn_capital_shares"]).to_broadcast([P, 3])),
            (b2_row[:, :], row(w["L0_ffn_b2"][e_last]).to_broadcast([P, C])),
            (bo_row[:, :], row(w["L1_attn_b_o"]).to_broadcast([P, C])),
            (lnw_row[:, 0:C], row(w["L1_attn_ln_g"]).to_broadcast([B, C])),
            (lnw_row[:, C:2 * C], row(w["L1_attn_ln_b"]).to_broadcast([B, C])),
            (a_neg[:, :, :], w["L0_attn_A_log"].rearrange("(d p) s -> p d s", p=P)),
        ]
        pad = [ca[:, 0, 0:KC * P].rearrange("p (k m) -> p k m", k=KC),
               ca[:, 1, 0:KC * P].rearrange("p (k m) -> p k m", k=KC)]
        padded = []
        for k in range(KC):
            ch = slice(k * P, (k + 1) * P)
            padded += [(pad[0][:, k, 0:E_MOE], w["L0_ffn_Wr"][:, ch].rearrange("e p -> p e")),
                       (pad[1][:, k, 0:2], w["L1_ffn_conf_rwkv"][:, ch].rearrange("e p -> p e")),
                       (pad[1][:, k, 2:3], w["L1_ffn_conf_trans"][ch].rearrange("(p a) -> p a", a=1)),
                       (pad[1][:, k, 3:4], w["L1_ffn_w_diff"][ch].rearrange("(p a) -> p a", a=1)),
                       (pad[1][:, k, 4:7], w["L1_ffn_W_aff"][ch, :])]
        wq_st = cb[:, :, 0:C]
        wv_st = cb[:, :, C:2 * C]

        with nc.Block() as block:

            def store_split(sp, n):
                if n < 2:
                    return
                sp.wait_ge(u_split, n + 1)
                sp.dma_start(w_split[n - 2], ws_in[n % 2][:, :, :, :].bitcast(F32).rearrange("p h k m -> p (h k m)"))\
                  .then_inc(u_store[n % 2], 16)

            @block.sync
            def _(sp):
                for semaphore in credited + [x for b in bank.values() for x in (b.full, b.free)]:
                    sp.sem_inc(semaphore, CREDIT)
                for layer in range(2):
                    sp.dma_start(c_in[:, layer * C:(layer + 1) * C], w[f"L{layer}_c"]).then_inc(u_c, 16)
                for dst, src in small:
                    sp.dma_start(dst, src).then_inc(u_load, 16)
                for k, name in enumerate(["L1_attn_Wq", "L1_attn_Wv"]):
                    sp.dma_start((wq_st, wv_st)[k], kp(w[name])).then_inc(u_load, 16)
                sp.wait_ge(u_zero, 1)
                for dst, src in padded:
                    sp.dma_start(dst, src).then_inc(u_load, 16)
                for n, (loads, shape) in enumerate(zip(pieces, shapes)):
                    if n >= 2:
                        sp.wait_ge(u_split, n - 1)
                    for at, m, src in loads:
                        sp.dma_start(staged(n, shape)[:, :, at:at + m], src).then_inc(u_stage[n % 2], 16)
                    if n >= 3:
                        store_split(sp, n - 1)
                store_split(sp, len(pieces) - 1)
                for k in range(2):
                    sp.wait_ge(u_store[k], 16 * NSLOT // 2)
                sp.wait_ge(u_rows, 2)
                for b in range(B):
                    for c in range(CPB):
                        sp.dma_start(mods[b * CPB + c:b * CPB + c + 1, :], modrow[b:b + 1, :]).then_inc(u_mods, 16)
                sp.wait_ge(u_mods, 16 * NCH)

            @block.gpsimd
            def _(pool):
                pool.memset(ca[:, :, :], 0.0).then_inc(u_zero, 1)
                pool.memset(ident[:, :], 0.0).then_inc(u_id, 1)
                pool.memset(keep[:, :], -1).then_inc(u_id, 1)
                pool.memset(mhalf[:, :], -0.5).then_inc(u_id, 1)
                pool.wait_ge(u_id, 3)
                pool.affine_select(out=ident[:, :], in_=ident[:, :], compare_op=ALU.not_equal, fill=1.0,
                                   base=0, pattern=[[-1, P]], channel_multiplier=1).then_inc(u_id, 1)
                pool.memset(keep[:, 0:NCH:CPB], 0).then_inc(u_id, 1)
                pool.memset(state[:, :, :], 0.0).then_inc(u_id, 1)
                pool.memset(state_l[:, :], 0.0).then_inc(u_id, 1)

            n_small = 16 * (len(small) + 2 + len(padded))

            @block.scalar
            def _(act):
                for layer in range(2):
                    if layer:
                        act.wait_ge(u_mm, 3)
                    act.dma_start(wm[:, :, :], kp(w[f"L{layer}_wmod"])).then_inc(u_wm, 16)
                    if layer == 0:
                        act.wait_ge(u_c, 32)
                        act.activation(c_in[:, :], c_in[:, :], ACT.Silu).then_inc(u_silu, 1)
                act.wait_ge(u_load, n_small)
                act.activation(a_neg[:, :, :], a_neg[:, :, :], ACT.Exp).then_inc(u_exp, 1)

            @block.tensor
            def _(pe):
                pe.wait_ge(u_silu, 1)
                pe.wait_ge(u_id, 7)
                for layer in range(2):
                    for k in range(KC):
                        at = layer * C + k * P
                        last = pe.transpose(psum["A0"][:, (layer * KC + k) * B:(layer * KC + k + 1) * B],
                                            c_in[:, at:at + P], ident[0:B, 0:B])
                last.then_inc(u_ct, 1)
                pe.wait_ge(u_ctc, 1)
                for layer in range(2):
                    pe.wait_ge(u_wm, 16 * (layer + 1))
                    for g in range(3):
                        name = ["B0", "B1", "B2"][g]
                        if layer:
                            pe.wait_ge(u_raw, g + 1)
                        for k in range(KC):
                            last = pe.matmul(psum[name][0:B, :], c_t[:, layer, k, :],
                                             wm[:, k, g * 2 * C:(g + 1) * 2 * C], start=k == 0, stop=k == KC - 1)
                        last.then_inc(u_mm, 1)

            @block.vector
            def _(dve):
                done = [0]

                def step(ins):
                    done[0] += 1
                    ins.then_inc(u_dve, 1)
                    dve.wait_ge(u_dve, done[0])

                dve.wait_ge(u_ct, 1)
                dve.tensor_copy(c_t[:, :, :, :], psum["A0"][:, 0:2 * KC * B]
                                .rearrange("p (l k b) -> p l k b", l=2, k=KC)).then_inc(u_ctc, 1)

                def mrow(name):
                    return modrow[:, ROW[name] * C:(ROW[name] + 1) * C]

                def rows_of(layer):
                    for g in range(3):
                        dve.wait_ge(u_mm, 3 * layer + g + 1)
                        dve.tensor_copy(modraw[:, g * 2 * C:(g + 1) * 2 * C], psum[["B0", "B1", "B2"][g]][0:B, :])\
                           .then_inc(u_raw, 1)
                    dve.wait_ge(u_raw, 3 * layer + 3)
                    raw = [modraw[:, k * C:(k + 1) * C] for k in range(6)]
                    for part, (sa, ca_, ga) in enumerate((raw[0:3], raw[3:6])):
                        p_ = "AB"[part]
                        if part == 0:
                            dve.tensor_copy(mrow(f"sA{layer}"), sa)
                        step(dve.tensor_scalar(mrow(f"c{p_}{layer}"), ca_, 1.0, None, ALU.add))
                        goal = mrow("gA1w") if (layer, part) == (1, 0) else mrow(f"g{p_}{layer}")
                        step(dve.tensor_scalar(ca_, ga, 0.0, 2.0, ALU.is_ge, ALU.mult))
                        step(dve.tensor_scalar(ca_, ca_, -1.0, None, ALU.add))
                        step(dve.scalar_tensor_tensor(out=ga, in0=ga, scalar=-1.0, in1=ga, op0=ALU.mult, op1=ALU.max))
                        step(dve.tensor_scalar(ga, ga, GATE_MIN, None, ALU.max))
                        step(dve.tensor_tensor(ga, ga, ca_, ALU.mult))
                        if (layer, part) == (1, 0):
                            step(dve.tensor_tensor(mrow("gA1b"), ga, lnw_row[:, C:2 * C], ALU.mult))
                            step(dve.tensor_tensor(goal, ga, lnw_row[:, 0:C], ALU.mult))
                        else:
                            step(dve.tensor_copy(goal, ga))
                    dve.tensor_copy(mrow(f"sB{layer}"), raw[3]).then_inc(u_rows, 1)
                    dve.wait_ge(u_rows, layer + 1)

                def split(n):
                    loads, shape = pieces[n], shapes[n]
                    earlier = sum(len(l) for l, _ in list(zip(pieces, shapes))[n % 2:n:2])
                    dve.wait_ge(u_stage[n % 2], 16 * (earlier + len(loads)))
                    src = staged(n, shape)
                    if n == 0:
                        high, low = w_in["h"][:, :, :], w_in["l"][:, :, :]
                    elif n == 1:
                        high, low = w_dt["h"][:, :, :], w_dt["l"][:, :, :]
                    else:
                        high, low = ws_in[n % 2][:, 0], ws_in[n % 2][:, 1]
                        if n >= 4:
                            dve.wait_ge(u_store[n % 2], 16 * ((n - 2) // 2))
                    step(dve.tensor_copy(high, src))
                    dve.tensor_tensor(low, src, high.bitcast(F32), ALU.subtract).then_inc(u_split, 1)

                for n in range(3):
                    split(n)
                rows_of(0)
                for n in range(3, len(pieces) // 2 + 2):
                    split(n)
                rows_of(1)
                for n in range(len(pieces) // 2 + 2, len(pieces)):
                    split(n)
                dve.wait_ge(u_load, n_small)
                for k, wt in enumerate((w_rt, w_bd)):
                    step(dve.tensor_copy(wt["h"][:, :, :], pad[k]))
                    step(dve.tensor_tensor(wt["l"][:, :, :], pad[k], wt["h"][:, :, :].bitcast(F32), ALU.subtract))
                for k, wt in enumerate((wq_st, wv_st)):
                    for c in range(KC):
                        step(dve.tensor_reduce(w_kq[:, c, C + k * NH:C + (k + 1) * NH],
                                               wt[:, c, :].rearrange("p (h d) -> p h d", h=NH), AX, ALU.add))
                dve.wait_ge(u_exp, 1)
                step(dve.tensor_scalar(a_neg[:, :, :], a_neg[:, :, :], 1e-6, 1.0, ALU.max, ALU.min))
                step(dve.tensor_scalar(a_neg[:, :, :], a_neg[:, :, :], -1.0, None, ALU.mult))

        x_v = w["L0_attn_x"].rearrange("b (c t p) m -> (b c) p t m", t=NT, p=P)
        out_v = out.rearrange("b (c t p) m -> (b c) p t m", t=NT, p=P)

        slot_dmas = [2 if name in w_down else 1 for name in SLOTS]
        for k in range(2):
            s_w[k].n = 16 * sum(slot_dmas[k::2])

        def slot_ready(eng, j, name):
            q = SLOTS.index(name)
            eng.wait_ge(s_w[q % 2].sem, s_w[q % 2].at(j, 16 * sum(slot_dmas[q % 2:q + 1:2])))

        def block_used(eng, j, n):
            k, e = n % NHB, n // NHB
            if k == NHB - 1:
                take(eng, j, ["ffn1", "e0_1", "e1_1"][e])
            else:
                eng.wait_ge(d_hfree.sem, d_hfree.at(j, (NHB - 1) * e + k + 1))

        def per_tile(m):
            return m.unsqueeze(1).to_broadcast([P, NT, C])

        def m_s(name):
            return mod_s[:, ROW[name], :]

        def m_d(name):
            return mod_d[:, ROW[name] - NROW_S, :]

        with nc.Block() as block:

            @block.sync
            def _(sp):
                def load_x(i):
                    since(sp, s_x1, i)
                    sp.dma_start(xin[:, :, :], x_v[bass.ds(i, 1)].rearrange("a p t m -> p (a t) m"))\
                      .then_inc(s_xin.sem, 16)
                    sp.dma_start(mod_s[:, :, :].rearrange("p r m -> p (r m)"),
                                 mods[bass.ds(i, 1), 0:NROW_S * C].to_broadcast([P, NROW_S * C]))\
                      .then_inc(s_mods.sem, 16)

                def front(i, step, k):
                    if step == "mean" and k == 0:
                        load_x(i)
                    if step == "bc":
                        used(sp, i, "bc")
                        sp.dma_start(b_rows[:, :], bcs[DS:2 * DS, :]).then_inc(s_bw.sem, 16)
                    if step == "dt" and k == 0:
                        sp.wait_ge(s_bw.sem, s_bw.at(i, 16))
                        load_b(i, 0)

                def load_b(i, s):
                    sp.dma_start(bb[:, s % 4, :], b_rows[s:s + 1, :].to_broadcast([P, CT]))\
                      .then_inc(s_bb[s % 4].sem, 16)

                def unit(i, u):
                    s = u // DB
                    if u % DB == 0 and 1 <= s < DS:
                        if s >= 4:
                            sp.wait_ge(s_bu.sem, s_bu.at(i, DB * (s - 3)))
                        load_b(i, s)

                def tail(i, step, k):
                    pass

                def load_mod(j, k):
                    lo, hi = [(0, 3), (3, 7), (7, 10)][k]
                    since(sp, (d_x2, d_x3, d_x5)[k], j)
                    sp.dma_start(mod_d[:, lo:hi, :].rearrange("p r m -> p (r m)"),
                                 mods[bass.ds(j, 1), (NROW_S + lo) * C:(NROW_S + hi) * C]
                                 .to_broadcast([P, (hi - lo) * C])).then_inc(s_modd[k].sem, 16)

                def load_slot(j, name):
                    q = SLOTS.index(name)
                    before = {"ffn_1": ("start", "B3"), "rv": ("block", 3), "sw": ("full", "ffn1"),
                              "e0_0": ("full", "v1"), "e0_1": ("full", "tw1"), "e1_0": ("block", NHB + 3),
                              "e1_1": ("full", "e0_1")}
                    kind, what = before.get(name, ("start", None))
                    if kind == "full":
                        take(sp, j, what)
                    elif kind == "block":
                        block_used(sp, j, what)
                    elif what is None:
                        if not (isinstance(j, int) and j == 0):
                            block_used(sp, j - 1, 2 * NHB + 3)
                    else:
                        last = bank[what]
                        sp.wait_ge(last.full, j * len(last.uses) + CREDIT)
                    sp.dma_start(ws_in[q % 2][:, :, :, :].bitcast(F32).rearrange("p h k m -> p (h k m)"), w_split[q])\
                      .then_inc(s_w[q % 2].sem, 16)
                    if name in w_down:
                        sp.dma_start(ws_out[q % 2][:, :, :], kp(w_down[name])).then_inc(s_w[q % 2].sem, 16)

                def first_ffn(j, pace):
                    load_mod(j, 0)
                    load_slot(j, "ffn_1")
                    pace("load_ffn_1")
                    load_mod(j, 1)
                    pace("c3")
                    load_slot(j, "rv")
                    pace("c7")
                    load_slot(j, "sw")
                    pace("load_sw")

                def attention_on(j, pace, last=False):
                    load_mod(j, 2)
                    pace("k_proj")
                    load_slot(j, "e0_0")
                    pace("n_trans")
                    load_slot(j, "e0_1")
                    pace("o3")
                    load_slot(j, "e1_0")
                    pace("o7")
                    load_slot(j, "e1_1")
                    pace("p3")
                    if not last:
                        load_slot(j + 1, "ffn_0")
                    pace("q_out")
                    sp.wait_ge(d_x5.sem, d_x5.at(j, 1))
                    sp.dma_start(out_v[bass.ds(j, 1)].rearrange("a p t m -> p (a t) m"), xd[:, :, :])\
                      .then_inc(s_out.sem, 16)

                load_slot(0, "ffn_0")
                Pace(PACE["sp"], front, unit, tail, 0).upto(len(S_STEPS))
                first_ffn(0, Pace(PACE["sp"], front, unit, tail, 1))
                with sp.Fori(2, NCH) as i:
                    pace = Pace(PACE["sp"], front, unit, tail, i)
                    attention_on(i - 2, pace)
                    first_ffn(i - 1, pace)
                pace = Pace(PACE["sp"], None, None, None, NCH)
                attention_on(NCH - 2, pace)
                first_ffn(NCH - 1, pace)
                attention_on(NCH - 1, Pace(PACE["sp"], None, None, None, NCH + 1), last=True)
                sp.wait_ge(s_out.sem, s_out.at(NCH, 0))

            @block.gpsimd
            def _(pool):
                def rstd(rs, sig):
                    pool.tensor_tensor(rs[:, :], rs[:, :], mhalf[:, :], ALU.pow).then_inc(sig.sem, 1)

                def front(i, step, k):
                    if step == "mean":
                        pool.wait_ge(s_mv.sem, s_mv.at(i, k + 1))
                        rstd(rs_s, s_rs)
                    if (step, k) == ("norm", 1):
                        own = Own(pool, o_pool_s, i)
                        pool.wait_ge(s_mods.sem, s_mods.at(i, 16))
                        pool.wait_ge(s_n.sem, s_n.at(i, 1))
                        own.step(pool.tensor_tensor(h0[:, :, :], h0[:, :, :], per_tile(m_s("gA0")), ALU.mult))
                        pool.tensor_tensor(xin[:, :, :], xin[:, :, :], h0[:, :, :], ALU.add).then_inc(s_xg.sem, 1)
                        own.end()
                    if step == "clip":
                        pool.wait_ge(s_dt.sem, s_dt.at(i, k + 1))
                        pool.tensor_tensor(z[:, k, :], z[:, k, :], dt[:, k, :], ALU.mult).then_inc(s_u.sem, 1)

                def tail(i, step, k):
                    pass

                def unit(i, u):
                    s, d = u // DB, u % DB
                    if s == DS:
                        return
                    if s == 0:
                        pool.wait_ge(s_u.sem, s_u.at(i, d + 1))
                    if d == 0:
                        pool.wait_ge(s_bb[s % 4].sem, s_bb[s % 4].at(i, 16 * (s // 4 + 1)))
                    if u >= 4:
                        used(pool, i, f"dA{u - 4}")
                    ins = pool.tensor_tensor(bu[:, u % 4, :], z[:, d, :], bb[:, s % 4, :], ALU.mult)
                    ins.then_inc(s_bu.sem, 1)

                def norm(j, k, pace):
                    pool.wait_ge(d_mv.sem, d_mv.at(j, k + 1))
                    rstd(rs_d, d_rs)
                    pace(f"rstd{k}")

                def first_ffn(j, pace):
                    norm(j, 0, pace)

                def attention_on(j, pace):
                    norm(j, 1, pace)
                    pool.wait_ge(s_modd[1].sem, s_modd[1].at(j, 16))
                    pool.wait_ge(d_h.sem, d_h.at(j, 2))
                    pool.tensor_tensor(xd[:, :, :], xd[:, :, :], per_tile(m_d("gA1b")), ALU.add).then_inc(d_xb.sem, 1)
                    pace("f_kv")
                    used(pool, j, "h2T1")
                    pool.tensor_tensor(hA[:, :, :], hA[:, :, :], per_tile(bo_row[:, :]), ALU.add).then_inc(d_hb.sem, 1)
                    pace("h_bias")
                    for k in (2, 3, 4, 5):
                        norm(j, k, pace)
                    pace("q_out")

                Pace(PACE["pool"], front, unit, tail, 0).upto(len(S_STEPS))
                first_ffn(0, Pace(PACE["pool"], front, unit, tail, 1))
                with pool.Fori(2, NCH) as i:
                    pace = Pace(PACE["pool"], front, unit, tail, i)
                    attention_on(i - 2, pace)
                    first_ffn(i - 1, pace)
                pace = Pace(PACE["pool"], None, None, None, NCH)
                attention_on(NCH - 2, pace)
                first_ffn(NCH - 1, pace)
                attention_on(NCH - 1, Pace(PACE["pool"], None, None, None, NCH + 1))

            @block.scalar
            def _(act):
                def front(i, step, k):
                    if step == "turn":
                        for c in range(KC):
                            b = take(act, i, f"xn{c}")
                            act.activation(xnf[:, c, :], b.t[:, :], ACT.Identity, scale=cols[:, c:c + 1],
                                           bias=cols[:, 2 + c:3 + c]).then_inc(b.free, 1)
                        for c in range(KC):
                            used(act, i, f"xn{c}")
                            act.activation(xnh[:, c, :], xnf[:, c, :], ACT.Copy).then_inc(s_xnh.sem, 1)
                    if step == "z":
                        b = take(act, i, f"z{k}")
                        act.activation(zh[:, k, :], b.t[:, :], ACT.Copy).then_inc(s_zh.sem, 1)
                        act.activation(z[:, k, :], b.t[:, :], ACT.Copy).then_inc(b.free, 1)
                    if step == "gate":
                        b = take(act, i, f"gt{k}")
                        act.activation(gate[:, k, :], b.t[:, :], ACT.Silu).then_inc(b.free, 1)
                    if step == "bc":
                        b = take(act, i, "bc")
                        act.activation(bcs[:, :], b.t[0:2 * DS, :], ACT.Copy).then_inc(b.free, 1)
                    if (step, k) == ("gate", 2):
                        b = take(act, i, "ct")
                        act.activation(ctok[:, :, :], b.t[:, 0:NT * 2 * DS].rearrange("p (t c) -> p t c", t=NT),
                                       ACT.Copy).then_inc(b.free, 1)
                    if step == "softplus":
                        own = Own(act, o_act_s, i)
                        for d in range(DB):
                            used(act, i, f"dt{d}")
                            own.mark(act.activation(dt[:, d, :], dt[:, d, :], ACT.Exp))
                        for d in range(DB):
                            own.wait(d + 1)
                            act.activation(dt[:, d, :], dt[:, d, :], ACT.Ln, bias=1.0).then_inc(s_sp.sem, 1)
                        own.end()

                def unit(i, u):
                    s, d = u // DB, u % DB
                    if s == DS:
                        return
                    if s == 0:
                        act.wait_ge(s_dt.sem, s_dt.at(i, d + 1))
                    b = fill(act, i, f"dA{u}")
                    act.activation(b.t[:, :], dt[:, d, :], ACT.Exp, scale=a_neg[:, d, s:s + 1]).then_inc(b.full, 1)

                def tail(i, step, k):
                    if step == "y":
                        b = take(act, i, f"y{k}")
                        act.activation(z[:, k, :], b.t[:, :], ACT.Copy).then_inc(b.free, 1)

                def turned(j, use, pace, scale=None, shift=None):
                    for k in range(KC):
                        b = take(act, j, f"{use}{k}")
                        if scale is None:
                            ins = act.activation(ff[:, k, :], b.t[:, :], ACT.Copy)
                        else:
                            ins = act.activation(ff[:, k, :], b.t[:, :], ACT.Identity,
                                                 scale=cols[:, scale + k:scale + k + 1],
                                                 bias=cols[:, shift + k:shift + k + 1])
                        ins.then_inc(b.free, 1)
                        pace(f"{use}{k}")

                def high(j, use, pace):
                    for k in range(KC):
                        used(act, j, f"{use}{k}")
                        act.activation(fh[:, k, :], ff[:, k, :], ACT.Copy).then_inc(d_fh.sem, 1)
                        pace(f"{use}{k}_high")

                def to_rows(j, use, pace):
                    b = take(act, j, use)
                    act.activation(rows8[:, :], b.t[0:8, :], ACT.Copy).then_inc(b.free, 1)
                    pace(use)

                def first_ffn(j, pace):
                    pace("b_turn")
                    turned(j, "h1T", pace)
                    high(j, "h1T", pace)
                    to_rows(j, "router", pace)
                    act.wait_ge(d_lsub.sem, d_lsub.at(j, 1))
                    act.activation(lg[:, :, :], lg[:, :, :], ACT.Exp).then_inc(d_lexp.sem, 1)
                    pace("b_router")
                    for k in range(F // P):
                        b = take(act, j, f"c{k}")
                        if k >= HB:
                            block_used(act, j, k - HB)
                        act.activation(hid[:, k % HB, :], b.t[:, :], ACT.Gelu, bias=b1_col[:, k:k + 1])\
                           .then_inc(b.free, 1)
                        pace(f"c{k}")

                def attention_on(j, pace):
                    pace("f_turn")
                    turned(j, "h2T", pace)
                    pace("f_kv")
                    act.wait_ge(d_sm.sem, d_sm.at(j, 1))
                    act.activation(bx[:, :, :].rearrange("p t (h d) -> p t h d", h=NH),
                                   sm[:, :, 2 * NH:3 * NH].unsqueeze(3).to_broadcast([P, NT, NH, HD]),
                                   ACT.Sigmoid).then_inc(d_bx.sem, 1)
                    pace("beta")
                    act.activation(qx[:, :, :].rearrange("p t (h d) -> p t h d", h=NH),
                                   sm[:, :, 0:NH].unsqueeze(3).to_broadcast([P, NT, NH, HD]),
                                   ACT.Copy).then_inc(d_bx.sem, 1)
                    pace("q")
                    for k in range(KC):
                        b = take(act, j, f"kvT{k}")
                        act.activation(ca[:, k, :], b.t[:, :], ACT.Copy).then_inc(b.free, 1)
                        pace(f"kvT{k}")
                    pace("j_turn")
                    turned(j, "xlT", pace, 4, 6)
                    high(j, "xlT", pace)
                    for k in range(KC):
                        b = take(act, j, f"r{k}")
                        act.activation(cb[:, k, :], b.t[:, :], ACT.Sigmoid).then_inc(b.free, 1)
                        pace(f"r{k}")
                    for k in range(KC):
                        b = take(act, j, f"s{k}")
                        act.activation(ca[:, k, :], b.t[:, :], ACT.Copy).then_inc(b.free, 1)
                        pace(f"s{k}")
                    for k in range(KC):
                        b = take(act, j, f"sW{k}")
                        act.activation(cb[:, k, :], b.t[:, :], ACT.Sigmoid).then_inc(b.free, 1)
                        pace(f"sW{k}")
                    turned(j, "hhT", pace, 8, 10)
                    high(j, "hhT", pace)
                    to_rows(j, "bids", pace)
                    used(act, j, "bidsT")
                    act.activation(sg[:, :, :], bl[:, :, 0:4], ACT.Sigmoid).then_inc(d_sg.sem, 1)
                    for e in range(2):
                        for k in range(F // P):
                            use = f"{'op'[e]}{k}"
                            n = 8 * e + k
                            b = take(act, j, use)
                            block_used(act, j, NHB + n - HB)
                            act.activation(hid[:, k % HB, :], b.t[:, :], ACT.Relu).then_inc(b.free, 1)
                            used(act, j, use)
                            act.activation(hid[:, k % HB, :], hid[:, k % HB, :], ACT.Square).then_inc(d_sq.sem, 1)
                            pace(use)
                    pace("q_out")

                Pace(PACE["act"], front, unit, tail, 0).upto(len(S_STEPS))
                first_ffn(0, Pace(PACE["act"], front, unit, tail, 1))
                with act.Fori(2, NCH) as i:
                    pace = Pace(PACE["act"], front, unit, tail, i)
                    attention_on(i - 2, pace)
                    first_ffn(i - 1, pace)
                pace = Pace(PACE["act"], None, None, None, NCH)
                attention_on(NCH - 2, pace)
                first_ffn(NCH - 1, pace)
                attention_on(NCH - 1, Pace(PACE["act"], None, None, None, NCH + 1))

            @block.vector
            def _(dve):
                def stats(own, src, st, mv, rs, sig):
                    for t in range(NT):
                        own.mark(dve.bn_stats(st[:, t, :], src[:, t, :]))
                    own.wait()
                    dve.memset(carrier[:, :], 0.0)
                    for t in range(NT):
                        ins = dve.bn_aggr(mv[:, t, :], st[:, t, :])
                    own.step(ins)
                    dve.tensor_scalar(rs[:, :], mv[:, :, 1], EPS, None, ALU.add).then_inc(sig.sem, 1)

                def apply(dst, src, mv, rs, sig):
                    for t in range(NT):
                        ins = dve.tensor_scalar(dst[:, t, :], src[:, t, :], mv[:, t, 0:1], rs[:, t:t + 1],
                                                ALU.subtract, ALU.mult)
                    ins.then_inc(sig.sem, 1)

                def centre(own, dst, src, mv, scale):
                    for t in range(NT):
                        own.mark(dve.scalar_tensor_tensor(out=dst[:, t, :], in0=src[:, t, :], scalar=mv[:, t, 0:1],
                                                          in1=scale, op0=ALU.subtract, op1=ALU.mult))

                def finish(dst, src, rs, shift, sig):
                    for t in range(NT):
                        ins = dve.scalar_tensor_tensor(out=dst[:, t, :], in0=src[:, t, :], scalar=rs[:, t:t + 1],
                                                       in1=shift(t), op0=ALU.mult, op1=ALU.add)
                    ins.then_inc(sig.sem, 1)

                own_s = [None]

                def front(i, step, k):
                    if (step, k) == ("mean", 0):
                        own_s[0] = Own(dve, o_dve_s, i)
                    own = own_s[0]
                    if (step, k) == ("mean", 0):
                        dve.wait_ge(s_xin.sem, s_xin.at(i, 16))
                        stats(own, xin, st_s, mv_s, rs_s, s_mv)
                        own.mark(dve.tensor_tensor(state[:, :, :].rearrange("p s d -> p (s d)").bitcast(I32),
                                                   state[:, :, :].rearrange("p s d -> p (s d)").bitcast(I32),
                                                   keep[:, bass.ds(i, 1)].to_broadcast([P, DS * DB]), ALU.bitwise_and))
                    if (step, k) == ("norm", 0):
                        dve.wait_ge(s_mods.sem, s_mods.at(i, 16))
                        centre(own, h0, xin, mv_s, m_s("cA0"))
                        own.wait()
                        dve.wait_ge(s_rs.sem, s_rs.at(i, 1))
                        finish(h0, h0, rs_s, lambda t: m_s("sA0"), s_h0)
                    if (step, k) == ("mean", 1):
                        dve.wait_ge(s_h0.sem, s_h0.at(i, 1))
                        stats(own, h0, st_s, mv_s, rs_s, s_mv)
                    if (step, k) == ("norm", 1):
                        dve.wait_ge(s_rs.sem, s_rs.at(i, 2))
                        apply(n0, h0, mv_s, rs_s, s_n)
                    if step == "turn":
                        for c in range(KC):
                            dve.wait_ge(s_xnh.sem, s_xnh.at(i, c + 1))
                            dve.tensor_tensor(xnl[:, c, :], xnf[:, c, :], xnh[:, c, :].bitcast(F32), ALU.subtract)\
                               .then_inc(s_xnl.sem, 1)
                    if step == "z":
                        used(dve, i, f"z{k}")
                        dve.tensor_tensor(zl[:, k, :], z[:, k, :], zh[:, k, :].bitcast(F32), ALU.subtract)\
                           .then_inc(s_zl.sem, 1)
                    if step == "dt":
                        b = take(dve, i, f"dt{k}")
                        dve.tensor_scalar(dt[:, k, :], b.t[:, :], bdt_col[:, k:k + 1], DT_CLAMP, ALU.add, ALU.min)\
                           .then_inc(b.free, 1)
                    if step == "clip":
                        dve.wait_ge(s_sp.sem, s_sp.at(i, k + 1))
                        dve.tensor_scalar(dt[:, k, :], dt[:, k, :], DT_MIN, DT_MAX, ALU.max, ALU.min)\
                           .then_inc(s_dt.sem, 1)

                def read_out(i, s, t):
                    use = f"hT{s * NT + t}"
                    b = take(dve, i, use)
                    if s == 0:
                        if t == 0:
                            used(dve, i, "ct")
                        ins = dve.tensor_scalar(acc[:, t, :], b.t[:, :], ctok[:, t, s:s + 1], None, ALU.mult)
                    else:
                        used(dve, i, f"hT{(s - 1) * NT + t}")
                        ins = dve.scalar_tensor_tensor(out=acc[:, t, :], in0=b.t[:, :], scalar=ctok[:, t, s:s + 1],
                                                       in1=acc[:, t, :], op0=ALU.mult, op1=ALU.add)
                    ins.then_inc(b.free, 1)

                def unit(i, u):
                    s, d = u // DB, u % DB
                    if d == 0 and s >= 1:
                        for n in (u - 2, u - 1):
                            used(dve, i, f"dA{n}")
                        own_s[0].mark(dve.tensor_copy(state[:, s - 1, :], hs[:, (s - 1) % 2, :, CT - 1]))
                    if s < DS:
                        dve.wait_ge(s_bu.sem, s_bu.at(i, u + 1))
                        b = take(dve, i, f"dA{u}")
                        dve.tensor_tensor_scan(hs[:, s % 2, d, :], b.t[:, :], bu[:, u % 4, :],
                                               state[:, s, d:d + 1], ALU.mult, ALU.add).then_inc(b.free, 1)
                    if s >= 1:
                        read_out(i, s - 1, d)

                def tail(i, step, k):
                    own = own_s[0]
                    if step == "gated":
                        for t in range(NT):
                            used(dve, i, f"gt{t}")
                            used(dve, i, f"hT{(DS - 1) * NT + t}")
                        for t in range(NT):
                            ins = dve.tensor_tensor(acc[:, t, :], acc[:, t, :], gate[:, t, :], ALU.mult)
                        ins.then_inc(s_yg.sem, 1)
                    if step == "out":
                        if k == 0:
                            since(dve, d_x2, i)
                        b = take(dve, i, f"wo{k}")
                        tiles = x1[:, 2 * k:2 * k + 2, :]
                        dve.tensor_tensor(tiles, b.t[:, :].rearrange("p (t c) -> p t c", t=2),
                                          m_s("gA0").unsqueeze(1).to_broadcast([P, 2, C]), ALU.mult)\
                           .then_inc(b.free, 1)
                    if step == "x1":
                        dve.wait_ge(s_xg.sem, s_xg.at(i, 1))
                        for p in range(2):
                            used(dve, i, f"wo{p}")
                        dve.tensor_tensor(x1[:, :, :], x1[:, :, :], xin[:, :, :], ALU.add).then_inc(s_x1.sem, 1)
                        own.end()

                def low(j, k, pace):
                    for c in range(KC):
                        dve.wait_ge(d_fh.sem, d_fh.at(j, KC * k + c + 1))
                        dve.tensor_tensor(fl[:, c, :], ff[:, c, :], fh[:, c, :].bitcast(F32), ALU.subtract)\
                           .then_inc(d_fl.sem, 1)
                        pace(f"low{k}_{c}")

                def pair(b):
                    return b.t[:, :].rearrange("p (t c) -> p t c", t=2)

                def first_ffn(j, pace):
                    own = Own(dve, o_dve_f, j)
                    step = own.step
                    dve.wait_ge(s_x1.sem, s_x1.at(j, 1))
                    stats(own, x1, st_d, mv_d, rs_d, d_mv)
                    pace("a_stats")
                    dve.wait_ge(s_modd[0].sem, s_modd[0].at(j, 16))
                    centre(own, hA, x1, mv_d, m_d("cB0"))
                    own.wait()
                    dve.wait_ge(d_rs.sem, d_rs.at(j, 1))
                    finish(hA, hA, rs_d, lambda t: m_d("sB0"), d_h)
                    pace("a_norm")
                    pace("b_turn")
                    low(j, 0, pace)
                    b = take(dve, j, "routerT")
                    dve.tensor_copy(lg[:, :, :], b.t[:, 0:NT * 8].rearrange("p (t e) -> p t e", t=NT))\
                       .then_inc(b.free, 1)
                    used(dve, j, "routerT")
                    step(dve.tensor_reduce(lg_m[:, :], lg[:, :, :], AX, ALU.max))
                    dve.tensor_tensor(lg[:, :, :], lg[:, :, :], lg_m[:, :].unsqueeze(2).to_broadcast([P, NT, E_MOE]),
                                      ALU.subtract).then_inc(d_lsub.sem, 1)
                    pace("b_router")
                    dve.wait_ge(d_lexp.sem, d_lexp.at(j, 1))
                    step(dve.tensor_reduce(lg_m[:, :], lg[:, :, :], AX, ALU.add))
                    step(dve.reciprocal(lg_m[:, :], lg_m[:, :]))
                    step(dve.tensor_tensor(prob[:, :], lg_m[:, :], lg[:, :, E_MOE - 1], ALU.mult))
                    pace("prob")
                    dve.wait_ge(s_modd[0].sem, s_modd[0].at(j, 16))
                    since(dve, s_out, j)
                    for p in range(2):
                        b = take(dve, j, f"ffn{p}")
                        dve.tensor_tensor(nn[:, 2 * p:2 * p + 2, :], pair(b),
                                          b2_row[:, :].unsqueeze(1).to_broadcast([P, 2, C]), ALU.add)\
                           .then_inc(b.free, 1)
                        pace(f"ffn{p}")
                    for p in range(2):
                        used(dve, j, f"ffn{p}")
                        for t in (2 * p, 2 * p + 1):
                            own.mark(dve.scalar_tensor_tensor(out=nn[:, t, :], in0=nn[:, t, :], scalar=prob[:, t:t + 1],
                                                              in1=m_d("gB0"), op0=ALU.mult, op1=ALU.mult))
                    pace("ffn_scaled")
                    own.wait()
                    dve.tensor_tensor(xd[:, :, :], x1[:, :, :], nn[:, :, :], ALU.add).then_inc(d_x2.sem, 1)
                    pace("d_x2")
                    own.end()

                def attention_on(j, pace):
                    own = Own(dve, o_dve_d, j)
                    step = own.step
                    dve.wait_ge(d_x2.sem, d_x2.at(j, 1))
                    stats(own, xd, st_d, mv_d, rs_d, d_mv)
                    pace("e_stats")
                    dve.wait_ge(s_modd[1].sem, s_modd[1].at(j, 16))
                    centre(own, hA, xd, mv_d, m_d("cA1"))
                    own.wait()
                    dve.wait_ge(d_rs.sem, d_rs.at(j, 2))
                    finish(hA, hA, rs_d, lambda t: m_d("sA1"), d_h)
                    pace("e_norm")
                    pace("f_turn")
                    for t in range(NT):
                        use = f"kq{t}"
                        b = take(dve, j, use)
                        step(dve.tensor_copy(sm[:, t, :], b.t[:, C:NQ]))
                        ins = dve.tensor_tensor(nn[:, t, :].rearrange("p (h d) -> p h d", h=NH),
                                                b.t[:, 0:C].rearrange("p (h d) -> p h d", h=NH),
                                                sm[:, t, NH:2 * NH].unsqueeze(2).to_broadcast([P, NH, HD]), ALU.mult)
                        ins.then_inc(b.free, 1)
                        pace(f"kq{t}")
                    dve.tensor_tensor(sm[:, :, 2 * NH:3 * NH], sm[:, :, 2 * NH:3 * NH],
                                      bbeta_row[:, :].unsqueeze(1).to_broadcast([P, NT, NH]), ALU.add)\
                       .then_inc(d_sm.sem, 1)
                    own.mark(dve.tensor_tensor(state_l[:, :].bitcast(I32), state_l[:, :].bitcast(I32),
                                               keep[:, bass.ds(j, 1)].to_broadcast([P, KC]), ALU.bitwise_and))
                    pace("f_kv")
                    pace("g_turn")
                    own.wait()
                    for k in range(KC):
                        if k:
                            pace("scan0")
                        b = take(dve, j, f"btT{k}")
                        used(dve, j, f"kvT{k}")
                        dve.tensor_tensor_scan(cb[:, k, :], b.t[:, :], ca[:, k, :], state_l[:, k:k + 1],
                                               ALU.mult, ALU.add).then_inc(b.free, 1)
                        used(dve, j, f"btT{k}")
                        step(dve.tensor_copy(state_l[:, k:k + 1], cb[:, k, CT - 1:CT]))
                        b = take(dve, j, f"qsT{k}")
                        dve.tensor_tensor(cb[:, k, :], cb[:, k, :], b.t[:, :], ALU.mult).then_inc(b.free, 1)
                        pace(f"qsT{k}")
                    pace("g_scan")
                    dve.wait_ge(d_hb.sem, d_hb.at(j, 1))
                    for p in range(2):
                        b = take(dve, j, f"ao{p}")
                        dve.tensor_tensor(hA[:, 2 * p:2 * p + 2, :], pair(b), hA[:, 2 * p:2 * p + 2, :], ALU.add)\
                           .then_inc(b.free, 1)
                        pace(f"ao{p}")
                    pace("h_out")
                    for p in range(2):
                        used(dve, j, f"ao{p}")
                    stats(own, hA, st_d, mv_d, rs_d, d_mv)
                    pace("h_stats")
                    centre(own, nn, hA, mv_d, m_d("gA1w"))
                    own.wait()
                    dve.wait_ge(d_xb.sem, d_xb.at(j, 1))
                    dve.wait_ge(d_rs.sem, d_rs.at(j, 3))
                    finish(xd, nn, rs_d, lambda t: xd[:, t, :], d_x3)
                    pace("h_norm")
                    dve.wait_ge(d_x3.sem, d_x3.at(j, 1))
                    stats(own, xd, st_d, mv_d, rs_d, d_mv)
                    pace("i_stats")
                    dve.wait_ge(s_modd[2].sem, s_modd[2].at(j, 16))
                    centre(own, hA, xd, mv_d, m_d("cB1"))
                    own.wait()
                    dve.wait_ge(d_rs.sem, d_rs.at(j, 4))
                    finish(hA, hA, rs_d, lambda t: m_d("sB1"), d_h)
                    pace("i_norm")
                    dve.wait_ge(d_h.sem, d_h.at(j, 3))
                    stats(own, hA, st_d, mv_d, rs_d, d_mv)
                    pace("i_stats2")
                    dve.wait_ge(d_rs.sem, d_rs.at(j, 5))
                    apply(nn, hA, mv_d, rs_d, d_n)
                    pace("i_norm2")
                    pace("j_turn")
                    low(j, 1, pace)
                    pace("k_proj")
                    for k in range(KC):
                        b = take(dve, j, f"v{k}")
                        used(dve, j, f"r{k}")
                        dve.tensor_tensor(cb[:, k, :], cb[:, k, :], b.t[:, :], ALU.mult).then_inc(b.free, 1)
                        pace(f"v{k}")
                    pace("l_out")
                    for p in range(2):
                        b = take(dve, j, f"att{p}")
                        dve.tensor_tensor(hA[:, 2 * p:2 * p + 2, :], pair(b), hA[:, 2 * p:2 * p + 2, :], ALU.add)\
                           .then_inc(b.free, 1)
                        pace(f"att{p}")
                    for p in range(2):
                        used(dve, j, f"att{p}")
                    stats(own, hA, st_d, mv_d, rs_d, d_mv)
                    pace("m_stats")
                    dve.wait_ge(d_rs.sem, d_rs.at(j, 6))
                    apply(nn, hA, mv_d, rs_d, d_n)
                    pace("m_norm")
                    pace("m_turn")
                    low(j, 2, pace)
                    pace("n_bids")
                    b = take(dve, j, "bidsT")
                    dve.tensor_copy(bl[:, :, :], b.t[:, 0:NT * 8].rearrange("p (t e) -> p t e", t=NT))\
                       .then_inc(b.free, 1)
                    for k in range(KC):
                        b = take(dve, j, f"tw{k}")
                        used(dve, j, f"sW{k}")
                        dve.tensor_tensor(cb[:, k, :], cb[:, k, :], b.t[:, :], ALU.mult).then_inc(b.free, 1)
                        pace(f"tw{k}")
                    pace("product")
                    dve.wait_ge(d_sg.sem, d_sg.at(j, 1))
                    step(dve.tensor_tensor(bid[:, :, :], sg[:, :, 0:3], cs_row[:, :].unsqueeze(1)
                                           .to_broadcast([P, NT, 3]), ALU.mult))
                    step(dve.tensor_tensor(bid[:, :, :], bid[:, :, :], sg[:, :, 3:4].to_broadcast([P, NT, 3]), ALU.mult))
                    step(dve.tensor_tensor(bid[:, :, :], bid[:, :, :], bl[:, :, 4:7], ALU.add))
                    step(dve.tensor_reduce(bmax[:, :], bid[:, :, :], AX, ALU.max))
                    step(dve.tensor_tensor(win[:, :, :], bid[:, :, :], bmax[:, :].unsqueeze(2)
                                           .to_broadcast([P, NT, 3]), ALU.is_equal))
                    step(dve.tensor_tensor(win[:, :, 1], win[:, :, 1], win[:, :, 0], ALU.is_gt))
                    step(dve.tensor_tensor(win[:, :, 2], win[:, :, 2], win[:, :, 0], ALU.is_gt))
                    step(dve.tensor_tensor(win[:, :, 2], win[:, :, 2], win[:, :, 1], ALU.is_gt))
                    step(dve.tensor_tensor(wc[:, :, :], win[:, :, :], sg[:, :, 0:3], ALU.mult))
                    step(dve.tensor_reduce(bmax[:, :], wc[:, :, :], AX, ALU.add))
                    step(dve.tensor_scalar(wcs[:, :], bmax[:, :], 1e-6, None, ALU.add))
                    step(dve.reciprocal(wcs[:, :], wcs[:, :]))
                    step(dve.tensor_tensor(wcs[:, :], wcs[:, :], bmax[:, :], ALU.mult))
                    step(dve.tensor_tensor(coef[:, :, :], win[:, :, :], wcs[:, :].unsqueeze(2)
                                           .to_broadcast([P, NT, 3]), ALU.mult))
                    pace("n_trans")
                    def add_expert(uses, e):
                        for t in range(NT):
                            b = bank_of[uses[t // 2]]
                            if t % 2 == 0:
                                take(dve, j, uses[t // 2])
                            ins = dve.scalar_tensor_tensor(out=hA[:, t, :], in0=b.t[:, t % 2 * C:(t % 2 + 1) * C],
                                                           scalar=coef[:, t, e:e + 1], in1=hA[:, t, :],
                                                           op0=ALU.mult, op1=ALU.add)
                            if t % 2:
                                ins.then_inc(b.free, 1)
                        for use in uses:
                            used(dve, j, use)

                    add_expert(["tr0", "tr1"], 2)
                    pace("tr_out")
                    for e in range(2):
                        add_expert([f"e{e}_0", f"e{e}_1"], e)
                        pace("o_out" if e == 0 else "p_out")
                    step(dve.tensor_tensor(hA[:, :, :], hA[:, :, :], per_tile(m_d("gB1")), ALU.mult))
                    pace("scaled")
                    dve.tensor_tensor(xd[:, :, :], xd[:, :, :], hA[:, :, :], ALU.add).then_inc(d_x5.sem, 1)
                    pace("q_out")
                    own.end()

                Pace(PACE["dve"], front, unit, tail, 0).upto(len(S_STEPS))
                first_ffn(0, Pace(PACE["dve"], front, unit, tail, 1))
                with dve.Fori(2, NCH) as i:
                    pace = Pace(PACE["dve"], front, unit, tail, i)
                    attention_on(i - 2, pace)
                    first_ffn(i - 1, pace)
                pace = Pace(PACE["dve"], None, None, None, NCH)
                attention_on(NCH - 2, pace)
                first_ffn(NCH - 1, pace)
                attention_on(NCH - 1, Pace(PACE["dve"], None, None, None, NCH + 1))

            @block.tensor
            def _(pe):
                def turn(dst, src):
                    return pe.transpose(dst, src, ident[:, :])

                def split3(dst, lh, ll, rh, rl):
                    prods = [(a, b) for k in range(len(lh)) for a, b in ((lh[k], rh[k]), (lh[k], rl[k]), (ll[k], rh[k]))]
                    for n, (a, b) in enumerate(prods):
                        last = pe.matmul(dst, a, b, start=n == 0, stop=n == len(prods) - 1)
                    return last

                def front(i, step, k):
                    if step == "turn":
                        pe.wait_ge(s_n.sem, s_n.at(i, 1))
                        for c in range(KC):
                            b = fill(pe, i, f"xn{c}")
                            for t in range(NT):
                                last = turn(b.t[:, t * P:(t + 1) * P], n0[:, t, c * P:(c + 1) * P])
                            last.then_inc(b.full, 1)
                    if step == "z":
                        pe.wait_ge(s_xnl.sem, s_xnl.at(i, KC))
                        b = fill(pe, i, f"z{k}")
                        split3(b.t[:, :], [w_in["h"][:, c, k * P:(k + 1) * P] for c in range(KC)],
                               [w_in["l"][:, c, k * P:(k + 1) * P] for c in range(KC)],
                               [xnh[:, c, :] for c in range(KC)], [xnl[:, c, :] for c in range(KC)])\
                            .then_inc(b.full, 1)
                    if step == "gate":
                        b = fill(pe, i, f"gt{k}")
                        tok = slice(k * P, (k + 1) * P)
                        if k == 2:
                            bct = fill(pe, i, "ct")
                            used(pe, i, "bc")
                        split3(b.t[:, :], [xnh[:, c, tok] for c in range(KC)], [xnl[:, c, tok] for c in range(KC)],
                               [w_in["h"][:, c, DI:2 * DI] for c in range(KC)],
                               [w_in["l"][:, c, DI:2 * DI] for c in range(KC)]).then_inc(b.full, 1)
                        if k == 2:
                            for t in range(NT):
                                last = pe.transpose(bct.t[:, t * 2 * DS:(t + 1) * 2 * DS],
                                                    bcs[:, t * P:(t + 1) * P], ident[0:2 * DS, 0:2 * DS])
                            last.then_inc(bct.full, 1)
                    if step == "bc":
                        used(pe, i, "z3")
                        b = fill(pe, i, "bc")
                        for c in range(DB):
                            last = pe.matmul(b.t[0:2 * DS, :], w_bc[:, c, :], z[:, c, :], start=c == 0, stop=c == DB - 1)
                        last.then_inc(b.full, 1)
                    if step == "dt":
                        pe.wait_ge(s_zl.sem, s_zl.at(i, DB))
                        b = fill(pe, i, f"dt{k}")
                        split3(b.t[:, :], [w_dt["h"][:, c, k * P:(k + 1) * P] for c in range(DB)],
                               [w_dt["l"][:, c, k * P:(k + 1) * P] for c in range(DB)],
                               [zh[:, c, :] for c in range(DB)], [zl[:, c, :] for c in range(DB)])\
                            .then_inc(b.full, 1)

                def unit(i, u):
                    s, t = u // DB - 1, u % DB
                    if s < 0:
                        return
                    use = f"hT{s * NT + t}"
                    b = fill(pe, i, use)
                    if t == 0:
                        for n in (s * DB + DB - 2, s * DB + DB - 1):
                            used(pe, i, f"dA{n}")
                    for d in range(DB):
                        last = turn(b.t[:, d * P:(d + 1) * P], hs[:, s % 2, d, t * P:(t + 1) * P])
                    last.then_inc(b.full, 1)

                def tail(i, step, k):
                    if step == "y":
                        pe.wait_ge(s_yg.sem, s_yg.at(i, 1))
                        b = fill(pe, i, f"y{k}")
                        for t in range(NT):
                            last = turn(b.t[:, t * P:(t + 1) * P], acc[:, t, k * P:(k + 1) * P])
                        last.then_inc(b.full, 1)
                    if step == "out":
                        used(pe, i, "y3")
                        by_token(i, [f"wo{k}"], z, w_out, DB, [k])

                def by_token(j, uses, act, wt, kb, pairs=(0, 1), pace=None):
                    for use, p in zip(uses, pairs):
                        b = fill(pe, j, use)
                        for t in (2 * p, 2 * p + 1):
                            for k in range(kb):
                                last = pe.matmul(b.t[:, t % 2 * C:(t % 2 + 1) * C], act[:, k, t * P:(t + 1) * P],
                                                 wt[:, k, :], start=k == 0, stop=k == kb - 1)
                        last.then_inc(b.full, 1)
                        if pace:
                            pace(use)

                def turns(j, uses, src, pace):
                    for k in range(KC):
                        b = fill(pe, j, uses[k])
                        for t in range(NT):
                            last = turn(b.t[:, t * P:(t + 1) * P], src[:, t, k * P:(k + 1) * P])
                        last.then_inc(b.full, 1)
                        pace(uses[k])

                def parts(j, k):
                    pe.wait_ge(d_fl.sem, d_fl.at(j, KC * (k + 1)))

                def from_f(j, use, wh, wl, lo, hi):
                    b = fill(pe, j, use)
                    return b, split3(b.t[:, :], [wh[:, k, lo:hi] for k in range(KC)], [wl[:, k, lo:hi] for k in range(KC)],
                                     [fh[:, k, :] for k in range(KC)], [fl[:, k, :] for k in range(KC)])

                def logits_ready(j, use, use_t):
                    fill(pe, j, use_t)
                    used(pe, j, use)

                def logits_by_token(use_t):
                    b = bank_of[use_t]
                    for t in range(NT):
                        last = pe.transpose(b.t[:, t * 8:(t + 1) * 8], rows8[:, t * P:(t + 1) * P], ident[0:8, 0:8])
                    last.then_inc(b.full, 1)

                def hidden(j, name, slots, outs, pace):
                    def up(k):
                        if k % HB == 0:
                            slot_ready(pe, j, slots[k // HB])
                        wt = ws_in[SLOTS.index(slots[k // HB]) % 2]
                        c = k % HB
                        b, last = from_f(j, f"{name}{k}", wt[:, 0], wt[:, 1], c * P, (c + 1) * P)
                        last.then_inc(b.full, 1)
                        pace(f"{name}{k}_up")

                    def down(k):
                        if name == "c":
                            used(pe, j, f"{name}{k}")
                        else:
                            pe.wait_ge(d_sq.sem, d_sq.at(j, NHB * "op".index(name) + k + 1))
                        wt = ws_out[SLOTS.index(slots[k // HB]) % 2]
                        for t in range(NT):
                            b = bank_of[outs[t // 2]]
                            if k == 0 and t % 2 == 0:
                                fill(pe, j, outs[t // 2])
                            last = pe.matmul(b.t[:, t % 2 * C:(t % 2 + 1) * C], hid[:, k % HB, t * P:(t + 1) * P],
                                             wt[:, k % HB, :], start=k == 0 and t % 2 == 0,
                                             stop=k == NHB - 1, skip_group_check=True)
                            if k == NHB - 1 and t % 2:
                                last.then_inc(b.full, 1)
                        if k < NHB - 1:
                            last.then_inc(d_hfree.sem, 1)
                        pace(f"{name}{k}")

                    up(0)
                    if name == "c":
                        logits_by_token("routerT")
                    for k in range(NHB):
                        if k < NHB - 1:
                            up(k + 1)
                        down(k)

                def first_ffn(j, pace):
                    pace("a_norm")
                    pe.wait_ge(d_h.sem, d_h.at(j, 1))
                    turns(j, ["h1T0", "h1T1"], hA, pace)
                    parts(j, 0)
                    b, last = from_f(j, "router", w_rt["h"], w_rt["l"], 0, P)
                    last.then_inc(b.full, 1)
                    logits_ready(j, "router", "routerT")
                    pace("b_router")
                    hidden(j, "c", ["ffn_0", "ffn_1"], ["ffn0", "ffn1"], pace)

                def attention_on(j, pace):
                    pace("e_norm")
                    pe.wait_ge(d_h.sem, d_h.at(j, 2))
                    turns(j, ["h2T0", "h2T1"], hA, pace)
                    used(pe, j, "h2T1")
                    for t in range(NT):
                        b = fill(pe, j, f"kq{t}")
                        for k in range(KC):
                            last = pe.matmul(b.t[:, 0:NQ], ff[:, k, t * P:(t + 1) * P], w_kq[:, k, :],
                                             start=k == 0, stop=k == KC - 1)
                        last.then_inc(b.full, 1)
                        pace(f"kq{t}")
                    pace("f_kv")
                    used(pe, j, "kq2")
                    used(pe, j, "kq3")
                    turns(j, ["kvT0", "kvT1"], nn, pace)
                    pe.wait_ge(d_bx.sem, d_bx.at(j, 2))
                    turns(j, ["btT0", "btT1"], bx, pace)
                    turns(j, ["qsT0", "qsT1"], qx, pace)
                    pace("g_scan")
                    used(pe, j, "qsT1")
                    by_token(j, ["ao0", "ao1"], cb, w_ao, KC, pace=pace)
                    pace("i_norm2")
                    pe.wait_ge(d_n.sem, d_n.at(j, 1))
                    turns(j, ["xlT0", "xlT1"], nn, pace)
                    parts(j, 1)
                    slot_ready(pe, j, "rv")
                    rv, sw = ws_in[SLOTS.index("rv") % 2], ws_in[SLOTS.index("sw") % 2]
                    for k in range(KC):
                        b, last = from_f(j, f"r{k}", rv[:, 0], rv[:, 1], k * P, (k + 1) * P)
                        last.then_inc(b.full, 1)
                        pace(f"r{k}")
                        b, last = from_f(j, f"v{k}", rv[:, 0], rv[:, 1], C + k * P, C + (k + 1) * P)
                        last.then_inc(b.full, 1)
                        pace(f"v{k}")
                    slot_ready(pe, j, "sw")
                    for k in range(KC):
                        b, last = from_f(j, f"s{k}", sw[:, 0], sw[:, 1], k * P, (k + 1) * P)
                        last.then_inc(b.full, 1)
                        pace(f"s{k}")
                    used(pe, j, "v0")
                    used(pe, j, "v1")
                    by_token(j, ["att0", "att1"], cb, w_fo, KC, pace=pace)
                    used(pe, j, "s1")
                    for m in range(KC):
                        b = fill(pe, j, f"sW{m}")
                        for k in range(KC):
                            last = pe.matmul(b.t[:, :], w_2[:, k, m * P:(m + 1) * P], ca[:, k, :],
                                             start=k == 0, stop=k == KC - 1)
                        last.then_inc(b.full, 1)
                        pace(f"sW{m}")
                    pace("m_norm")
                    pe.wait_ge(d_n.sem, d_n.at(j, 2))
                    turns(j, ["hhT0", "hhT1"], nn, pace)
                    parts(j, 2)
                    b, last = from_f(j, "bids", w_bd["h"], w_bd["l"], 0, P)
                    last.then_inc(b.full, 1)
                    pace("bids")
                    logits_ready(j, "bids", "bidsT")
                    for k in range(KC):
                        b, last = from_f(j, f"tw{k}", sw[:, 0], sw[:, 1], C + k * P, C + (k + 1) * P)
                        last.then_inc(b.full, 1)
                        if k == 0:
                            logits_by_token("bidsT")
                        pace(f"tw{k}")
                    used(pe, j, "tw1")
                    by_token(j, ["tr0", "tr1"], cb, w_3, KC, pace=pace)
                    hidden(j, "o", ["e0_0", "e0_1"], ["e0_0", "e0_1"], pace)
                    pace("o_out")
                    hidden(j, "p", ["e1_0", "e1_1"], ["e1_0", "e1_1"], pace)
                    pace("q_out")

                Pace(PACE["pe"], front, unit, tail, 0).upto(len(S_STEPS))
                first_ffn(0, Pace(PACE["pe"], front, unit, tail, 1))
                with pe.Fori(2, NCH) as i:
                    pace = Pace(PACE["pe"], front, unit, tail, i)
                    attention_on(i - 2, pace)
                    first_ffn(i - 1, pace)
                pace = Pace(PACE["pe"], None, None, None, NCH)
                attention_on(NCH - 2, pace)
                first_ffn(NCH - 1, pace)
                attention_on(NCH - 1, Pace(PACE["pe"], None, None, None, NCH + 1))


OWN = {"dve_s": 31, "dve_f": 17, "dve_d": 59, "pool_s": 1, "act_s": 4}


def kernel(**inputs):
    import numpy as _np
    import concourse.bacc as _bacc
    from concourse import mybir as _mybir
    from concourse.bass_utils import run_bass_kernel_spmd as _run

    nc = _bacc.Bacc("TRN2", target_bir_lowering=False, num_devices=1)
    unused = {"L1_ffn_v_first"}
    arrays, args = {}, {}
    for name in inputs:
        if name in unused:
            continue
        a = _np.ascontiguousarray(inputs[name])
        arrays[f"in_{name}"] = a
        args[name] = nc.dram_tensor(f"in_{name}", a.shape, _mybir.dt.from_np(a.dtype), kind="ExternalInput").ap()
    out = nc.dram_tensor("out_0", (B, T, C), F32, kind="ExternalOutput").ap()
    build(nc, args, out)
    r = _run(nc, [arrays], core_ids=[0])
    return r.results[0]["out_0"]
```
